# Optimizing a Trainium2 kernel written in Bass

```python
import numpy as np
import jax
import jax.numpy as jnp

def _softmax(x, axis=-1):
    return jax.nn.softmax(x, axis=axis)

def _gelu(x):
    return jax.nn.gelu(x, approximate=True)

def _silu(x):
    return jax.nn.silu(x)

def _sigmoid(x):
    return jax.nn.sigmoid(x)

def _layernorm(x, axis=-1, eps=1e-05):
    m = jnp.mean(x, axis=axis, keepdims=True)
    v = jnp.var(x, axis=axis, keepdims=True)
    return (x - m) / jnp.sqrt(v + eps)

def _scatter_add(tgt, idx, src, axis=0):
    return tgt.at[idx].add(src)

def _segment_sum(src, seg, n):
    return jax.ops.segment_sum(src, seg, n)
kernel_name = 'mk_flamingo_gated_d2_seqx_r4_a0935f'

def setup_inputs(seed: int=0):
    np.random.seed(seed)
    _w = jnp.asarray

    def _rec_inputs():
        import jax
        import jax.numpy as jnp
        _rk = jax.random.key(seed)
        x = -0.0002928 + 1 * jax.random.normal(jax.random.fold_in(_rk, 1), (16, 256, 256), jnp.float32)
        _lenS = 256 - jax.random.randint(jax.random.fold_in(_rk, 7), (16,), 0, max(1, 256 // 4) + 1, jnp.int32)
        _lenS2 = 256 - jax.random.randint(jax.random.fold_in(_rk, 8), (16,), 0, max(1, 256 // 4) + 1, jnp.int32)
        _ctx_1024P = jax.random.normal(jax.random.fold_in(_rk, 11), (16, 16, 256), jnp.float32)
        _ctx_1024c = jax.random.dirichlet(jax.random.fold_in(_rk, 511), 0.3 * jnp.ones((16,), jnp.float32), (16, 256))
        _ctx_1024t = jnp.einsum('bsk,bkd->bsd', _ctx_1024c, _ctx_1024P)
        _ctx_1024t = _ctx_1024t * jax.lax.rsqrt(jnp.mean(jnp.square(_ctx_1024t)) + 1e-12) * 0.953939
        ctx_1024 = -1.39393e-06 + 0.999914 * (_ctx_1024t + 0.3 * jax.random.normal(jax.random.fold_in(_rk, 611), (16, 256, 256), jnp.float32))
        _validS = jnp.arange(256)[None, :] < _lenS[:, None]
        _validS2 = jnp.arange(256)[None, :] < _lenS2[:, None]
        _causal = jnp.tril(jnp.ones((256, 256), dtype=bool))
        mask_BxS2_bf1 = jnp.ones((16, 256), dtype=bool)
        _g = jax.random.normal(jax.random.fold_in(_rk, 9001), (2, 2), jnp.float32)
        _g = jnp.sign(_g) * jnp.maximum(jnp.abs(_g), 1.0) + (_g == 0) * 1.0
        g_xattn = _g[0]
        g_ffn = _g[1]
        return (x, ctx_1024, mask_BxS2_bf1, g_xattn, g_ffn)
    x, ctx_1024, mask_BxS2_bf1, g_xattn, g_ffn = _rec_inputs()

    def _L0_xattn_setup():
        import jax, jax.numpy as jnp
        import numpy as np
        N_HEADS = 16
        HEAD_DIM = 64
        EMB = 256
        B, S = (2, 512)
        key = jax.random.key(seed)
        ks = jax.random.split(key, 8)
        inner = N_HEADS * HEAD_DIM
        return {'query': jax.random.normal(ks[0], (B, S, EMB), dtype=jnp.float32), 'key': jax.random.normal(ks[1], (B, S, EMB), dtype=jnp.float32), 'value': jax.random.normal(ks[2], (B, S, EMB), dtype=jnp.float32), 'positional_mask': jnp.ones((B, S), dtype=bool), 'future_mask': 1, 'Wq': jax.random.normal(ks[3], (inner, EMB), dtype=jnp.float32) * 0.02, 'Wk': jax.random.normal(ks[4], (inner, EMB), dtype=jnp.float32) * 0.02, 'Wv': jax.random.normal(ks[5], (inner, EMB), dtype=jnp.float32) * 0.02, 'Wo': jax.random.normal(ks[6], (EMB, inner), dtype=jnp.float32) * 0.02, 'bo': jax.random.normal(ks[7], (EMB,), dtype=jnp.float32) * 0.02}
    _L0_xattn_all = _L0_xattn_setup()
    _L0_xattn_in = {k: v for k, v in _L0_xattn_all.items() if k in ('Wq', 'Wk', 'Wv', 'Wo', 'bo')}
    del _L0_xattn_all

    def _L0_ffn_setup():
        import jax, jax.numpy as jnp
        import numpy as np
        D = 256
        H = 16
        HD = D // H
        L = 64
        E = 8
        B, T = (4, 512)
        EPS = 1e-06

        def _glorot(k, shape):
            fan_in, fan_out = (shape[-2], shape[-1])
            lim = np.sqrt(6.0 / (fan_in + fan_out)).astype(np.float32)
            return jax.random.uniform(k, shape, jnp.float32, -lim, lim)

        def _rmsnorm(x, gamma):
            return gamma * x * jax.lax.rsqrt(jnp.mean(x * x, axis=-1, keepdims=True) + EPS)
        key = jax.random.key(seed)
        ks = jax.random.split(key, 8)
        return {'x': jax.random.normal(ks[0], (B, T, D), jnp.float32), 'gamma1': jnp.ones((D,), jnp.float32), 'Wq': _glorot(ks[1], (D, D)), 'bq': jnp.zeros((D,), jnp.float32), 'Wdown': _glorot(ks[2], (D, L)), 'bdown': jnp.zeros((L,), jnp.float32), 'Wup': _glorot(ks[3], (L, 2 * D)), 'bup': jnp.zeros((2 * D,), jnp.float32), 'Wo': _glorot(ks[4], (D, D)), 'bo': jnp.zeros((D,), jnp.float32), 'gamma2': jnp.ones((D,), jnp.float32), 'Wg': _glorot(ks[5], (D, E)), 'bg': jnp.zeros((E,), jnp.float32), 'We': _glorot(ks[6], (E, D, D))}
    _L0_ffn_all = _L0_ffn_setup()
    _L0_ffn_in = {k: v for k, v in _L0_ffn_all.items() if k in ('gamma1', 'Wq', 'bq', 'Wdown', 'bdown', 'Wup', 'bup', 'Wo', 'bo', 'gamma2', 'Wg', 'bg', 'We')}
    del _L0_ffn_all

    def _L1_xattn_setup():
        import jax, jax.numpy as jnp
        import numpy as np
        D_MODEL = 256
        NUM_HEADS = 16
        HEAD_DIM = D_MODEL // NUM_HEADS
        key = jax.random.key(seed)
        ks = jax.random.split(key, 11)
        B, S, D = (2, 512, D_MODEL)
        s = 1.0 / np.sqrt(D)
        inp = {'query': jax.random.normal(ks[0], (B, S, D), jnp.float32), 'key': jax.random.normal(ks[1], (B, S, D), jnp.float32), 'value': jax.random.normal(ks[2], (B, S, D), jnp.float32), 'Wq': jax.random.normal(ks[3], (D, D), jnp.float32) * s, 'bq': jnp.zeros((D,), jnp.float32), 'Wk': jax.random.normal(ks[4], (D, D), jnp.float32) * s, 'bk': jnp.zeros((D,), jnp.float32), 'Wv': jax.random.normal(ks[5], (D, D), jnp.float32) * s, 'bv': jnp.zeros((D,), jnp.float32), 'Wo': jax.random.normal(ks[6], (D, D), jnp.float32) * s, 'bo': jnp.zeros((D,), jnp.float32)}
        return inp
    _L1_xattn_all = _L1_xattn_setup()
    _L1_xattn_in = {k: v for k, v in _L1_xattn_all.items() if k in ('Wq', 'bq', 'Wk', 'bk', 'Wv', 'bv', 'Wo', 'bo')}
    del _L1_xattn_all

    def _L1_ffn_setup():
        import jax, jax.numpy as jnp
        import numpy as np
        D_MODEL = 256
        HIDDEN = 1024
        N_ROUTING = 2
        key = jax.random.key(seed)
        ks = jax.random.split(key, 10)
        s = 0.02
        x = jax.random.normal(ks[0], (4, 1024, D_MODEL), dtype=jnp.float32)
        gate_w = jax.random.normal(ks[1], (N_ROUTING, D_MODEL), dtype=jnp.float32) * s
        w1 = jax.random.normal(ks[2], (N_ROUTING, D_MODEL, HIDDEN), dtype=jnp.float32) * s
        b1 = jax.random.normal(ks[3], (N_ROUTING, HIDDEN), dtype=jnp.float32) * s
        w2 = jax.random.normal(ks[4], (N_ROUTING, HIDDEN, D_MODEL), dtype=jnp.float32) * s
        b2 = jax.random.normal(ks[5], (N_ROUTING, D_MODEL), dtype=jnp.float32) * s
        sw1 = jax.random.normal(ks[6], (D_MODEL, HIDDEN), dtype=jnp.float32) * s
        sb1 = jax.random.normal(ks[7], (HIDDEN,), dtype=jnp.float32) * s
        sw2 = jax.random.normal(ks[8], (HIDDEN, D_MODEL), dtype=jnp.float32) * s
        sb2 = jax.random.normal(ks[9], (D_MODEL,), dtype=jnp.float32) * s
        return {'x': x, 'gate_w': gate_w, 'w1': w1, 'b1': b1, 'w2': w2, 'b2': b2, 'sw1': sw1, 'sb1': sb1, 'sw2': sw2, 'sb2': sb2}
    _L1_ffn_all = _L1_ffn_setup()
    _L1_ffn_in = {k: v for k, v in _L1_ffn_all.items() if k in ('gate_w', 'w1', 'b1', 'w2', 'b2', 'sw1', 'sb1', 'sw2', 'sb2')}
    del _L1_ffn_all
    return {'x': x, 'ctx_1024': ctx_1024, 'mask_BxS2_bf1': mask_BxS2_bf1, 'g_xattn': g_xattn, 'g_ffn': g_ffn, 'L0_xattn_Wq': _L0_xattn_in['Wq'], 'L0_xattn_Wk': _L0_xattn_in['Wk'], 'L0_xattn_Wv': _L0_xattn_in['Wv'], 'L0_xattn_Wo': _L0_xattn_in['Wo'], 'L0_xattn_bo': _L0_xattn_in['bo'], 'L0_ffn_gamma1': _L0_ffn_in['gamma1'], 'L0_ffn_Wq': _L0_ffn_in['Wq'], 'L0_ffn_bq': _L0_ffn_in['bq'], 'L0_ffn_Wdown': _L0_ffn_in['Wdown'], 'L0_ffn_bdown': _L0_ffn_in['bdown'], 'L0_ffn_Wup': _L0_ffn_in['Wup'], 'L0_ffn_bup': _L0_ffn_in['bup'], 'L0_ffn_Wo': _L0_ffn_in['Wo'], 'L0_ffn_bo': _L0_ffn_in['bo'], 'L0_ffn_gamma2': _L0_ffn_in['gamma2'], 'L0_ffn_Wg': _L0_ffn_in['Wg'], 'L0_ffn_bg': _L0_ffn_in['bg'], 'L0_ffn_We': _L0_ffn_in['We'], 'L1_xattn_Wq': _L1_xattn_in['Wq'], 'L1_xattn_bq': _L1_xattn_in['bq'], 'L1_xattn_Wk': _L1_xattn_in['Wk'], 'L1_xattn_bk': _L1_xattn_in['bk'], 'L1_xattn_Wv': _L1_xattn_in['Wv'], 'L1_xattn_bv': _L1_xattn_in['bv'], 'L1_xattn_Wo': _L1_xattn_in['Wo'], 'L1_xattn_bo': _L1_xattn_in['bo'], 'L1_ffn_gate_w': _L1_ffn_in['gate_w'], 'L1_ffn_w1': _L1_ffn_in['w1'], 'L1_ffn_b1': _L1_ffn_in['b1'], 'L1_ffn_w2': _L1_ffn_in['w2'], 'L1_ffn_b2': _L1_ffn_in['b2'], 'L1_ffn_sw1': _L1_ffn_in['sw1'], 'L1_ffn_sb1': _L1_ffn_in['sb1'], 'L1_ffn_sw2': _L1_ffn_in['sw2'], 'L1_ffn_sb2': _L1_ffn_in['sb2']}

def reference(x, ctx_1024, mask_BxS2_bf1, g_xattn, g_ffn, L0_xattn_Wq, L0_xattn_Wk, L0_xattn_Wv, L0_xattn_Wo, L0_xattn_bo, L0_ffn_gamma1, L0_ffn_Wq, L0_ffn_bq, L0_ffn_Wdown, L0_ffn_bdown, L0_ffn_Wup, L0_ffn_bup, L0_ffn_Wo, L0_ffn_bo, L0_ffn_gamma2, L0_ffn_Wg, L0_ffn_bg, L0_ffn_We, L1_xattn_Wq, L1_xattn_bq, L1_xattn_Wk, L1_xattn_bk, L1_xattn_Wv, L1_xattn_bv, L1_xattn_Wo, L1_xattn_bo, L1_ffn_gate_w, L1_ffn_w1, L1_ffn_b1, L1_ffn_w2, L1_ffn_b2, L1_ffn_sw1, L1_ffn_sb1, L1_ffn_sw2, L1_ffn_sb2):
    import jax
    import jax.numpy as jnp

    def _L0_xattn_ref(query, key, value, positional_mask, future_mask, Wq, Wk, Wv, Wo, bo):
        import jax, jax.numpy as jnp
        import numpy as np
        N_HEADS = 16
        HEAD_DIM = 64
        EMB = 256
        B, S = (2, 512)
        batch, seq = query.shape[:2]
        q = (query @ Wq.T).reshape(batch, seq, N_HEADS, HEAD_DIM)
        k = (key @ Wk.T).reshape(batch, seq, N_HEADS, HEAD_DIM)
        v = (value @ Wv.T).reshape(batch, seq, N_HEADS, HEAD_DIM)
        scale = 1.0 / np.sqrt(HEAD_DIM).astype(np.float32)
        weights = jnp.einsum('bqhd,bkhd->bhqk', q, k) * scale
        neg_inf = jnp.float32(-jnp.inf)
        reweight = jnp.where(positional_mask, jnp.float32(0.0), neg_inf)
        weights = weights + reweight[:, None, None, :]
        if future_mask:
            causal = jnp.triu(jnp.full((seq, seq), neg_inf, dtype=weights.dtype), k=1)
            weights = weights + causal
        weights = jax.nn.softmax(weights, axis=-1)
        out = jnp.einsum('bhqk,bkhd->bqhd', weights, v).reshape(batch, seq, -1)
        return out @ Wo.T + bo

    def _L0_ffn_ref(x, gamma1, Wq, bq, Wdown, bdown, Wup, bup, Wo, bo, gamma2, Wg, bg, We):
        import jax, jax.numpy as jnp
        import numpy as np
        D = 256
        H = 16
        HD = D // H
        L = 64
        E = 8
        B, T = (4, 512)
        EPS = 1e-06

        def _glorot(k, shape):
            fan_in, fan_out = (shape[-2], shape[-1])
            lim = np.sqrt(6.0 / (fan_in + fan_out)).astype(np.float32)
            return jax.random.uniform(k, shape, jnp.float32, -lim, lim)

        def _rmsnorm(x, gamma):
            return gamma * x * jax.lax.rsqrt(jnp.mean(x * x, axis=-1, keepdims=True) + EPS)
        b, t = (x.shape[0], x.shape[1])
        h = _rmsnorm(x, gamma1)
        q = (h @ Wq + bq).reshape(b, t, H, HD)
        kv = ((h @ Wdown + bdown) @ Wup + bup).reshape(b, t, H, 2 * HD)
        k, v = jnp.split(kv, 2, axis=-1)
        att = jnp.einsum('bthd,btgd->bthg', q, k) / np.sqrt(HD).astype(np.float32)
        att = jax.nn.softmax(att, axis=-1)
        out = jnp.einsum('bthg,btgd->bthd', att, v).reshape(b, t, D)
        x = x + (out @ Wo + bo)
        h2 = _rmsnorm(x, gamma2)
        gate = jax.nn.softmax(h2 @ Wg + bg, axis=-1)
        combined = jnp.einsum('btd,edf,bte->btf', h2, We, gate)
        return x + combined

    def _L1_xattn_ref(query, key, value, Wq, bq, Wk, bk, Wv, bv, Wo, bo):
        import jax, jax.numpy as jnp
        import numpy as np
        D_MODEL = 256
        NUM_HEADS = 16
        HEAD_DIM = D_MODEL // NUM_HEADS
        B, S, D = query.shape
        H, Hd = (NUM_HEADS, HEAD_DIM)
        Q = (query @ Wq.T + bq).reshape(B, S, H, Hd).transpose(0, 2, 1, 3)
        K = (key @ Wk.T + bk).reshape(B, S, H, Hd).transpose(0, 2, 1, 3)
        V = (value @ Wv.T + bv).reshape(B, S, H, Hd).transpose(0, 2, 1, 3)
        scale = 1.0 / jnp.sqrt(jnp.asarray(Hd, Q.dtype))
        scores = jnp.einsum('bhqd,bhkd->bhqk', Q, K) * scale
        attn = jax.nn.softmax(scores, axis=-1)
        out = jnp.einsum('bhqk,bhkd->bhqd', attn, V)
        out = out.transpose(0, 2, 1, 3).reshape(B, S, D)
        return out @ Wo.T + bo

    def _L1_ffn_ref(x, gate_w, w1, b1, w2, b2, sw1, sb1, sw2, sb2):
        import jax, jax.numpy as jnp
        import numpy as np
        D_MODEL = 256
        HIDDEN = 1024
        N_ROUTING = 2
        B, S, D = x.shape
        xf = x.reshape(-1, D)
        gate_scores = xf @ gate_w.T
        gate_probs = jax.nn.softmax(gate_scores, axis=-1)
        top1 = jnp.argmax(gate_probs, axis=-1)
        one_hot = jax.nn.one_hot(top1, N_ROUTING, dtype=xf.dtype)
        masked = xf[None, :, :] * one_hot.T[:, :, None]
        h = jax.nn.relu(jnp.einsum('end,edh->enh', masked, w1) + b1[:, None, :])
        expert_out = jnp.einsum('enh,ehd->end', h, w2) + b2[:, None, :]
        routing_output = expert_out.sum(axis=0)
        shared = jax.nn.relu(xf @ sw1 + sb1) @ sw2 + sb2
        return (routing_output + shared).reshape(B, S, D)
    x = x + jnp.tanh(g_xattn[0]) * _L0_xattn_ref(_layernorm(x, axis=-1), ctx_1024, ctx_1024, mask_BxS2_bf1, 1, L0_xattn_Wq, L0_xattn_Wk, L0_xattn_Wv, L0_xattn_Wo, L0_xattn_bo)
    x = x + jnp.tanh(g_ffn[0]) * _L0_ffn_ref(_layernorm(x, axis=-1), L0_ffn_gamma1, L0_ffn_Wq, L0_ffn_bq, L0_ffn_Wdown, L0_ffn_bdown, L0_ffn_Wup, L0_ffn_bup, L0_ffn_Wo, L0_ffn_bo, L0_ffn_gamma2, L0_ffn_Wg, L0_ffn_bg, L0_ffn_We)
    x = x + jnp.tanh(g_xattn[1]) * _L1_xattn_ref(_layernorm(x, axis=-1), ctx_1024, ctx_1024, L1_xattn_Wq, L1_xattn_bq, L1_xattn_Wk, L1_xattn_bk, L1_xattn_Wv, L1_xattn_bv, L1_xattn_Wo, L1_xattn_bo)
    x = x + jnp.tanh(g_ffn[1]) * _L1_ffn_ref(_layernorm(x, axis=-1), L1_ffn_gate_w, L1_ffn_w1, L1_ffn_b1, L1_ffn_w2, L1_ffn_b2, L1_ffn_sw1, L1_ffn_sb1, L1_ffn_sw2, L1_ffn_sb2)
    return x

_drawn_inputs = setup_inputs


def setup_inputs(seed=0):
    import zlib

    import numpy as np

    out = dict(_drawn_inputs(seed))
    spreads = {'g_ffn': (-1.0, 0.6),
     'L0_ffn_gamma1': (1.0, 0.2),
     'L0_ffn_bq': (0.0, 0.338),
     'L0_ffn_bdown': (0.0, 0.335),
     'L0_ffn_bup': (0.0, 0.1),
     'L0_ffn_bo': (0.0, 0.1),
     'L0_ffn_gamma2': (1.0, 0.2),
     'L0_ffn_bg': (0.0, 0.1),
     'L1_xattn_bq': (0.0, 0.1),
     'L1_xattn_bk': (0.0, 0.8),
     'L1_xattn_bv': (0.0, 0.1),
     'L1_xattn_bo': (0.0, 0.1)}
    factors = {'L0_xattn_Wq': 8.0,
     'L0_xattn_Wk': 8.0,
     'L0_xattn_bo': 2.848,
     'L1_ffn_b1': 4.734,
     'L1_ffn_sb1': 6.204}
    for name, (base, spread) in spreads.items():
        noise = np.random.default_rng([zlib.crc32(name.encode()), seed]).standard_normal(out[name].shape)
        drawn = base * np.exp(spread * noise) if base else spread * noise
        out[name] = jnp.asarray(drawn.astype(out[name].dtype))
    for name, factor in factors.items():
        out[name] = (out[name] * factor).astype(out[name].dtype)
    return out
```

```python
from contextlib import ExitStack

import concourse.bass as bass
from concourse import mybir
from concourse.alu_op_type import AluOpType as ALU

F32 = mybir.dt.float32
F32R = mybir.dt.float32r
U8 = mybir.dt.uint8
ACT = mybir.ActivationFunctionType
AX = mybir.AxisListType

B, S, D = 16, 256, 256
P = 128
NT = S // P
ND = D // P
H = 16
HD0 = 64
INNER = H * HD0
NC0 = INNER // P
HPC = P // HD0
HD = D // H
LAT = 64
E = 8
HID = 1024
NHC = HID // P
SLOT = 32
NC1 = H * SLOT // P
HPC1 = P // SLOT
LN_EPS = 1e-5
RMS_EPS = 1e-6
NEG = 1e30
CAUSAL = S + P


class Banks:

    def __init__(self, nc, ctx, name, uses):
        assert len(uses) % 2 == 0
        self.uses = uses
        self.bank = [ctx.enter_context(nc.psum_tensor(f"{name}{n}", [P, 512], F32)) for n in range(2)]
        self.full = [ctx.enter_context(nc.semaphore(f"{name}{n}_full")) for n in range(2)]
        self.free = [ctx.enter_context(nc.semaphore(f"{name}{n}_free")) for n in range(2)]

    def at(self, use, batch):
        k = self.uses.index(use)
        turn = batch * (len(self.uses) // 2) + k // 2 + 1
        return self.bank[k % 2], self.full[k % 2], self.free[k % 2], turn

    def emptied(self, engine, use, batch):
        _, _, free, turn = self.at(use, batch)
        engine.wait_ge(free, turn + 1)

    def open(self, engine):
        for f in self.free:
            engine.sem_inc(f, 1)


def first(batch):
    return isinstance(batch, int) and batch == 0


def wait_apart(engine, passed, sem, value):
    engine.wait_ge(sem, value)
    engine.sem_inc(passed, 1)


def product3(nc, out, terms):
    last = None
    for n, (wh, wl, xh, xl) in enumerate(terms):
        last = nc.tensor.matmul(out, wh, xh, start=n == 0, stop=False)
        last = nc.tensor.matmul(out, wh, xl, start=False, stop=False)
        last = nc.tensor.matmul(out, wl, xh, start=False, stop=n == len(terms) - 1)
    return last


def layer0(nc, ins, x2):
    with ExitStack() as ctx:
        def sb(name, shape, dtype=F32):
            return ctx.enter_context(nc.sbuf_tensor("l0_" + name, shape, dtype))

        def sem(name):
            return ctx.enter_context(nc.semaphore("l0_" + name))

        def pair(name, shape):
            return sb(name + "_hi", shape, F32R), sb(name + "_lo", shape, F32R)

        wq, wk, wv = pair("wq", [P, ND, INNER]), pair("wk", [P, ND, INNER]), pair("wv", [P, ND, INNER])
        fq, fdown, fup, fo = pair("fq", [P, ND, D]), pair("fdown", [P, ND, LAT]), pair("fup", [LAT, 2 * D]), pair("fo", [P, ND, D])
        wg, we = pair("wg", [P, ND, E]), pair("we", [P, ND, E * D])
        wo = sb("wo", [P, NC0, D])
        prod = sb("prod", [P, 2, H * D // 2])
        stage = prod
        bo, bq, bup, bfo, bg = sb("bo", [P, D]), sb("bq", [P, D]), sb("bup", [P, 2 * D]), sb("bfo", [P, D]), sb("bg", [P, E])
        bdown, gamma1, gamma2 = sb("bdown", [LAT, 1]), sb("gamma1", [P, ND]), sb("gamma2", [P, ND])
        gates, tg = sb("gates", [P, 4]), sb("tg", [P, 4])
        maskbits = sb("maskbits", [P, S], U8)
        ident, cmask, neghalf = sb("ident", [P, P]), sb("cmask", [P, CAUSAL]), sb("neghalf", [P, NT])

        xin, ctxin = sb("xin", [P, NT, D]), sb("ctxin", [P, ND, S])
        xn = sb("xn", [P, NT, D])
        statA, mvA, varA, rstdA = sb("statA", [P, NT, 6]), sb("mvA", [P, NT, 2]), sb("varA", [P, NT]), sb("rstdA", [P, NT])
        xT, cT = pair("xT", [P, ND, S]), pair("cT", [P, ND, S])
        qT, kT, v = sb("qT", [P, NC0, S]), sb("kT", [P, NC0, S]), sb("v", [P, NT, INNER])
        pos, mbias = sb("pos", [P, S]), sb("mbias", [P, CAUSAL])
        probs, probsT = sb("probs", [P, 4, CAUSAL]), sb("probsT", [P, 2, CAUSAL])
        negmax, rsum, rinv = sb("negmax", [P, H, NT]), sb("rsum", [P, H, NT]), sb("rinv", [P, H, NT])
        oT, x1, ytmp = sb("oT", [P, NC0, S]), sb("x1", [P, NT, D]), sb("ytmp", [P, NT, D])

        x1res, n, h = sb("x1res", [P, NT, D]), sb("n", [P, NT, D]), sb("h", [P, NT, D])
        statB, mvB, varB, rstdB = sb("statB", [P, NT, 6]), sb("mvB", [P, NT, 2]), sb("varB", [P, NT]), sb("rstdB", [P, NT])
        ms1, r1, ms2, r2 = sb("ms1", [P, NT]), sb("r1", [P, NT]), sb("ms2", [P, NT]), sb("r2", [P, NT])
        hT, dT = pair("hT", [P, ND, S]), pair("dT", [LAT, S])
        q, kv = sb("q", [P, NT, D]), sb("kv", [P, NT, 2 * D])
        att, amax, asum = sb("att", [P, NT, D]), sb("amax", [P, NT * H]), sb("asum", [P, NT * H])
        glog, gmax, gsum, gate = sb("glog", [P, NT, E]), sb("gmax", [P, NT]), sb("gsum", [P, NT]), sb("gate", [P, NT, E])
        y = q
        o, foT = h, hT
        x2out = ytmp

        attn = Banks(nc, ctx, "l0_attn", ["xT"] + [f"k{j}" for j in range(4)] + [f"v{j}" for j in range(4)]
                     + [f"q{j}" for j in range(4)] + [f"T{j}" for j in range(H)] + ["out"])
        score = Banks(nc, ctx, "l0_score", [f"s{j}" for j in range(H)])
        heads = Banks(nc, ctx, "l0_heads", [f"o{j}" for j in range(4)])
        ffn = Banks(nc, ctx, "l0_ffn", ["hT", "q", "down", "up0", "up1", "oT", "out", "h2T", "gate0", "gate1"]
                    + [f"we{j}" for j in range(E)])

        raw_in, split_hi, split_lo = [sem("raw_in0"), sem("raw_in1")], sem("split_hi"), sem("split_lo")
        mask_in, scored = sem("mask_in"), sem("scored")
        pool_passed, dve_passed, sp_passed = sem("pool_passed"), sem("dve_passed"), sem("sp_passed")
        params_in, consts, tanh_done = sem("params_in"), sem("consts"), sem("tanh_done")
        x_in, ctx_in, xres_in, x2_stored = sem("x_in"), sem("ctx_in"), sem("xres_in"), sem("x2_stored")
        varA_ready, rstdA_ready, xn_ready, ctx_ready = sem("varA_ready"), sem("rstdA_ready"), sem("xn_ready"), sem("ctx_ready")
        mask_ready, exp_done, rinv_ready, norm_done = sem("mask_ready"), sem("exp_done"), sem("rinv_ready"), sem("norm_done")
        xT_hi, pv_done, x1_ready, x1_copied = sem("xT_hi"), sem("pv_done"), sem("x1_ready"), sem("x1_copied")
        varB_ready, rstdB_ready, ms1_ready, r1_ready = sem("varB_ready"), sem("rstdB_ready"), sem("ms1_ready"), sem("r1_ready")
        h_ready, hT_hi, dT_hi = sem("h_ready"), sem("hT_hi"), sem("dT_hi")
        prod_ready, sub_ready, aexp_done, o_ready = sem("prod_ready"), sem("sub_ready"), sem("aexp_done"), sem("o_ready")
        foT_hi, ms2_ready, r2_ready, h2_ready = sem("foT_hi"), sem("ms2_ready"), sem("r2_ready"), sem("h2_ready")
        h2T_hi, glog_ready, gexp_done, x2_ready = sem("h2T_hi"), sem("glog_ready"), sem("gexp_done"), sem("x2_ready")

        def piece(src, dst, rows=P):
            return src, dst[0], dst[1], rows
        splits = [piece(ins["wk"], (wk[0][:].rearrange("p c n -> p (c n)"), wk[1][:].rearrange("p c n -> p (c n)"))),
                  piece(ins["wv"], (wv[0][:].rearrange("p c n -> p (c n)"), wv[1][:].rearrange("p c n -> p (c n)"))),
                  piece(ins["wq"], (wq[0][:].rearrange("p c n -> p (c n)"), wq[1][:].rearrange("p c n -> p (c n)"))),
                  piece(ins["fq"], (fq[0][:].rearrange("p c n -> p (c n)"), fq[1][:].rearrange("p c n -> p (c n)"))),
                  piece(ins["fdown"], (fdown[0][:].rearrange("p c n -> p (c n)"), fdown[1][:].rearrange("p c n -> p (c n)"))),
                  piece(ins["fup"], (fup[0][:], fup[1][:]), LAT),
                  piece(ins["fo"], (fo[0][:].rearrange("p c n -> p (c n)"), fo[1][:].rearrange("p c n -> p (c n)"))),
                  piece(ins["wg"], (wg[0][:].rearrange("p c n -> p (c n)"), wg[1][:].rearrange("p c n -> p (c n)"))),
                  piece(ins["we"][:, 0, :], (we[0][:, 0, :], we[1][:, 0, :])),
                  piece(ins["we"][:, 1, :], (we[0][:, 1, :], we[1][:, 1, :]))]
        NS = len(splits)
        params = [(wo[:].rearrange("p c n -> p (c n)"), ins["wo"]), (bo[:], ins["bo"].to_broadcast([P, D])),
                  (bq[:], ins["bq"].to_broadcast([P, D])), (bup[:], ins["bup"].to_broadcast([P, 2 * D])),
                  (bfo[:], ins["bfo"].to_broadcast([P, D])), (bg[:], ins["bg"].to_broadcast([P, E])),
                  (bdown[:], ins["bdown"]), (gamma1[:], ins["gamma1"]), (gamma2[:], ins["gamma2"]),
                  (gates[:], ins["gates"].to_broadcast([P, 4]))]

        with nc.Block() as block:

            @block.sync
            def _(sp):
                def load(b):
                    if not first(b):
                        sp.wait_ge(xn_ready, b)
                    sp.dma_start(xin[:], ins["x"][bass.ds(b, 1)][0]).then_inc(x_in, 16)
                    if not first(b):
                        sp.wait_ge(ctx_ready, b)
                    sp.dma_start(ctxin[:], ins["ctx"][bass.ds(b, 1)][0]).then_inc(ctx_in, 16)

                    if not first(b):
                        wait_apart(sp, sp_passed, mask_ready, b)
                    sp.dma_start(maskbits[:], ins["mask"][bass.ds(b, 1)].to_broadcast([P, S])).then_inc(mask_in, 16)

                def load_residual(b):
                    if not first(b):
                        sp.wait_ge(x1_copied, b)
                        sp.wait_ge(h_ready, b)
                    sp.dma_start(x1[:], ins["x"][bass.ds(b, 1)][0]).then_inc(xres_in, 16)

                def store(b):
                    sp.wait_ge(x2_ready, b + 1)
                    sp.dma_start(x2[bass.ds(b, 1)][0], x2out[:]).then_inc(x2_stored, 16)

                load(0)
                load_residual(0)
                for k, (src, _hi, _lo, rows) in enumerate(splits):
                    if k >= 2:
                        sp.wait_ge(split_lo, k - 1)
                    sp.dma_start(stage[0:rows, k % 2, 0:src.shape[1]], src).then_inc(raw_in[k % 2], 16)
                    if k == 1:
                        for dst, src in params:
                            sp.dma_start(dst, src).then_inc(params_in, 16)
                load(1)
                load_residual(1)
                with sp.Fori(2, B) as b:
                    load(b)
                    store(b - 2)
                    load_residual(b)
                store(B - 2)
                store(B - 1)
                sp.wait_ge(x2_stored, 16 * B)

            @block.gpsimd
            def _(pool):
                nc.gpsimd.memset(ident[:], 0.0)
                nc.gpsimd.memset(cmask[:], 0.0)
                nc.gpsimd.memset(neghalf[:], -0.5)
                pool.drain()
                nc.gpsimd.affine_select(out=ident[:], in_=ident[:], compare_op=ALU.not_equal, fill=1.0, base=0,
                                        pattern=[[-1, P]], channel_multiplier=1)
                for c in (P, S):
                    last = nc.gpsimd.affine_select(out=cmask[:, c:c + P], in_=cmask[:, c:c + P], compare_op=ALU.is_ge,
                                                   fill=-NEG, base=0, pattern=[[-1, P]], channel_multiplier=1)
                last.then_inc(consts, 1)

                def power(ready, done, src, dst, b):
                    pool.wait_ge(ready, b + 1)
                    nc.gpsimd.tensor_tensor(dst[:], src[:], neghalf[:], ALU.pow).then_inc(done, 1)

                def split_context(a):
                    if not first(a):
                        _, full, _, turn = attn.at("v3", a - 1)
                        pool.wait_ge(full, turn)
                    wait_apart(pool, pool_passed, ctx_in, 16 * (a + 1))
                    nc.gpsimd.tensor_copy(cT[0][:], ctxin[:])
                    pool.drain()
                    nc.gpsimd.tensor_sub(cT[1][:], ctxin[:], cT[0][:].bitcast(F32)).then_inc(ctx_ready, 1)

                def mask(a):
                    if not first(a):
                        score.emptied(pool, f"s{H - 2}", a - 1)
                        score.emptied(pool, f"s{H - 1}", a - 1)
                    wait_apart(pool, pool_passed, mask_in, 16 * (a + 1))
                    nc.gpsimd.tensor_scalar(pos[:], maskbits[:], -1.0, NEG, ALU.add, ALU.mult)
                    pool.drain()
                    nc.gpsimd.tensor_tensor(mbias[:, 0:S], cmask[:, 0:S], pos[:], ALU.add)
                    nc.gpsimd.tensor_tensor(mbias[:, S:CAUSAL], cmask[:, S:CAUSAL], pos[:, 0:P], ALU.add).then_inc(mask_ready, 1)

                def normalise(a, j):
                    wait_apart(pool, pool_passed, rinv_ready, H * a + j + 1)
                    nc.gpsimd.tensor_scalar(probs[:, j % 4, 0:S], probs[:, j % 4, 0:S], rinv[:, j, 1:2], 1.0, ALU.mult, ALU.mult)
                    nc.gpsimd.tensor_scalar(probs[:, j % 4, S:CAUSAL], probs[:, j % 4, S:CAUSAL], rinv[:, j, 0:1], 1.0,
                                            ALU.mult, ALU.mult).then_inc(norm_done, 1)

                def query_key(b, t, u):
                    half, piece = H // 2, NT * t + u
                    if piece < 2:
                        ffn.emptied(pool, "q", b)
                        ffn.emptied(pool, f"up{t}", b)
                    else:
                        ffn.emptied(pool, f"up{t}", b)
                        pool.wait_ge(scored, 4 * b + piece - 1)
                    k4 = kv[:, t].rearrange("p (g two d) -> p g two d", two=2, d=HD)[:, :, 0, :]
                    q4 = q[:, t].rearrange("p (h d) -> p h d", d=HD)
                    nc.gpsimd.tensor_tensor(
                        prod[:, u].rearrange("p (h g d) -> p h g d", h=half, g=H),
                        q4[:, u * half:(u + 1) * half].unsqueeze(2).to_broadcast([P, half, H, HD]),
                        k4.unsqueeze(1).to_broadcast([P, half, H, HD]), ALU.mult).then_inc(prod_ready, 1)

                def copy_residual(b):
                    if not first(b):
                        pool.wait_ge(x2_ready, b)
                    wait_apart(pool, pool_passed, x1_ready, b + 1)
                    nc.gpsimd.tensor_copy(x1res[:], x1[:]).then_inc(x1_copied, 1)

                def body(a, b, nxt):
                    if b is not None:
                        power(varB_ready, rstdB_ready, varB, rstdB, b)
                        power(ms1_ready, r1_ready, ms1, r1, b)
                        copy_residual(b)
                    if a is not None:
                        mask(a)
                    if b is not None:
                        for t in range(NT):
                            for u in range(2):
                                query_key(b, t, u)
                    for j in range(H):
                        if a is not None:
                            normalise(a, j)
                        if nxt is not None and j == 6:
                            split_context(nxt)
                        if nxt is not None and j == 10:
                            power(varA_ready, rstdA_ready, varA, rstdA, nxt)
                        if b is not None and j == 12:
                            power(ms2_ready, r2_ready, ms2, r2, b)

                split_context(0)
                power(varA_ready, rstdA_ready, varA, rstdA, 0)
                body(0, None, 1)
                body(1, 0, 2)
                with pool.Fori(2, B - 1) as a:
                    body(a, a - 1, a + 1)
                body(B - 1, B - 2, None)
                body(None, B - 1, None)

            @block.scalar
            def _(act):
                nc.scalar.preload_act_table(ACT.Exp)
                for k, (src, hi, _lo, rows) in enumerate(splits):
                    act.wait_ge(raw_in[k % 2], 16 * (k // 2 + 1))
                    nc.scalar.copy(hi, stage[0:rows, k % 2, 0:src.shape[1]]).then_inc(split_hi, 1)
                act.wait_ge(params_in, 16 * len(params))
                nc.scalar.activation(tg[:], gates[:], ACT.Tanh).then_inc(tanh_done, 1)

                def high(banks, use, batch, dst, ready, scales=None):
                    ps, full, free, turn = banks.at(use, batch)
                    act.wait_ge(full, turn)
                    if scales is None:
                        nc.scalar.copy(dst[:].rearrange("p c n -> p (c n)"), ps[:]).then_inc(ready, 1)
                    else:
                        for c in range(ND):
                            last = nc.scalar.activation(dst[:, c, :], ps[:, c * S:(c + 1) * S], ACT.Copy, scale=scales[:, c:c + 1])
                        last.then_inc(ready, 1)

                def body(a, b, nxt):
                    if b is not None:
                        high(ffn, "hT", b, hT[0], hT_hi, gamma1)
                    if a is not None:
                        high(attn, "xT", a, xT[0], xT_hi)
                    if b is not None:
                        ps, full, free, turn = ffn.at("down", b)
                        act.wait_ge(full, turn)
                        nc.scalar.activation(dT[0][:], ps[0:LAT, 0:S], ACT.Identity, bias=bdown[:]).then_inc(dT_hi, 1)
                    if a is not None:
                        for name, dst in (("k", kT), ("v", v), ("q", qT)):
                            for j in range(4):
                                ps, full, free, turn = attn.at(f"{name}{j}", a)
                                act.wait_ge(full, turn)
                                out = (v[:, j // 2, (j % 2) * 512:(j % 2 + 1) * 512] if name == "v"
                                       else dst[:, 2 * j:2 * j + 2, :].rearrange("p c n -> p (c n)"))
                                nc.scalar.copy(out, ps[:]).then_inc(free, 1)
                    for s in range(H + 3):
                        if b is not None and s == 3:
                            act.wait_ge(sub_ready, b + 1)
                            nc.scalar.activation(att[:], att[:], ACT.Exp, scale=HD ** -0.5).then_inc(aexp_done, 1)
                        if b is not None and s == 10:
                            high(ffn, "oT", b, foT[0], foT_hi)
                        if b is not None and s == 15:
                            high(ffn, "h2T", b, hT[0], h2T_hi, gamma2)
                        if b is not None and s == 18:
                            act.wait_ge(glog_ready, b + 1)
                            for t in range(NT):
                                last = nc.scalar.activation(gate[:, t], glog[:, t], ACT.Exp, bias=gmax[:, t:t + 1], accum_out=gsum[:, t:t + 1])
                            last.then_inc(gexp_done, 1)
                        if a is not None and s < H:
                            score.emptied(act, f"s{s}", a)
                            nc.scalar.activation(probs[:, s % 4, 0:S], probs[:, s % 4, 0:S], ACT.Exp, bias=negmax[:, s, 1:2],
                                                 scale=-1.0, accum_out=rsum[:, s, 1:2])
                            nc.scalar.activation(probs[:, s % 4, S:CAUSAL], probs[:, s % 4, S:CAUSAL], ACT.Exp, bias=negmax[:, s, 0:1],
                                                 scale=-1.0, accum_out=rsum[:, s, 0:1]).then_inc(exp_done, 1)
                        if a is not None and 2 <= s < H + 2:
                            j = s - 2
                            ps, full, free, turn = attn.at(f"T{j}", a)
                            act.wait_ge(full, turn)
                            if j >= 2:
                                act.wait_ge(pv_done, H * a + j - 1)
                            nc.scalar.copy(probsT[:, j % 2, :], ps[:, 0:CAUSAL]).then_inc(free, 1)
                        if a is not None and s >= 3 and (s - 3) % 4 == 3:
                            j = (s - 3) // 4
                            ps, _, free, _ = heads.at(f"o{j}", a)
                            act.wait_ge(pv_done, H * a + 4 * j + 4)
                            nc.scalar.copy(oT[:, 2 * j:2 * j + 2, :].rearrange("p c n -> p (c n)"), ps[:]).then_inc(free, 1)

                body(0, None, 1)
                body(1, 0, 2)
                with act.Fori(2, B - 1) as a:
                    body(a, a - 1, a + 1)
                body(B - 1, B - 2, None)
                body(None, B - 1, None)

            @block.vector
            def _(dve):
                for banks in (attn, score, heads, ffn):
                    banks.open(dve)
                V = nc.vector

                def variance(src, stat, mv, var, ready):
                    for t in range(NT):
                        V.bn_stats(stat[:, t], src[:, t])
                    dve.drain()
                    for t in range(NT):
                        V.bn_aggr(mv[:, t], stat[:, t])
                    dve.drain()
                    V.tensor_scalar(var[:], mv[:, :, 1], LN_EPS, None, ALU.add).then_inc(ready, 1)

                def pre_variance(a):
                    dve.wait_ge(x_in, 16 * (a + 1))
                    variance(xin, statA, mvA, varA, varA_ready)

                def pre_normalise(a):
                    dve.wait_ge(rstdA_ready, a + 1)
                    for t in range(NT):
                        last = V.tensor_scalar(xn[:, t], xin[:, t], mvA[:, t, 0:1], rstdA[:, t:t + 1], ALU.subtract, ALU.mult)
                    last.then_inc(xn_ready, 1)

                def low(banks, use, batch, dst, hi_ready, scales=None):
                    ps, _, free, _ = banks.at(use, batch)
                    dve.wait_ge(hi_ready, batch + 1)
                    if scales is None:
                        last = V.tensor_sub(dst[1][:].rearrange("p c n -> p (c n)"), ps[:],
                                            dst[0][:].rearrange("p c n -> p (c n)").bitcast(F32))
                    else:
                        for c in range(ND):
                            last = V.scalar_tensor_tensor(out=dst[1][:, c, :], in0=ps[:, c * S:(c + 1) * S], scalar=scales[:, c:c + 1],
                                                          in1=dst[0][:, c, :].bitcast(F32), op0=ALU.mult, op1=ALU.subtract)
                    last.then_inc(free, 1)

                def ffn_norm(b):
                    dve.drain()
                    variance(x1, statB, mvB, varB, varB_ready)
                    dve.wait_ge(rstdB_ready, b + 1)
                    V.tensor_tensor(ms1[:], mvB[:, :, 1], rstdB[:], ALU.mult)
                    for t in range(NT):
                        V.tensor_scalar(n[:, t], x1[:, t], mvB[:, t, 0:1], rstdB[:, t:t + 1], ALU.subtract, ALU.mult)
                    dve.drain()
                    V.tensor_tensor(ms1[:], ms1[:], rstdB[:], ALU.mult)
                    dve.drain()
                    V.tensor_scalar(ms1[:], ms1[:], RMS_EPS, None, ALU.add).then_inc(ms1_ready, 1)
                    dve.wait_ge(r1_ready, b + 1)
                    for t in range(NT):
                        last = V.tensor_scalar(h[:, t], n[:, t], r1[:, t:t + 1], None, ALU.mult)
                    last.then_inc(h_ready, 1)

                def ffn_project(b):
                    ps, full, free, turn = ffn.at("q", b)
                    dve.wait_ge(full, turn)
                    V.tensor_tensor(q[:], ps[:].rearrange("p (t n) -> p t n", t=NT), bq[:].unsqueeze(1).to_broadcast([P, NT, D]),
                                    ALU.add).then_inc(free, 1)
                    ps, full, free, turn = ffn.at("down", b)
                    dve.wait_ge(dT_hi, b + 1)
                    V.scalar_tensor_tensor(out=dT[1][:], in0=ps[0:LAT, 0:S], scalar=bdown[:], in1=dT[0][:].bitcast(F32),
                                           op0=ALU.add, op1=ALU.subtract).then_inc(free, 1)

                def ffn_kv(b, t):
                    ps, full, free, turn = ffn.at(f"up{t}", b)
                    dve.wait_ge(full, turn)
                    V.tensor_tensor(kv[:, t], ps[:], bup[:], ALU.add).then_inc(free, 1)

                def ffn_scores(b, t):
                    for u in range(2):
                        dve.wait_ge(prod_ready, 4 * b + 2 * t + u + 1)
                        V.tensor_reduce(att[:, t, u * P:(u + 1) * P], prod[:, u].rearrange("p (x d) -> p x d", d=HD),
                                        axis=AX.X, op=ALU.add).then_inc(scored, 1)

                att3 = att[:].rearrange("p t (h g) -> p (t h) g", g=H)

                def ffn_softmax_max(b):
                    dve.drain()
                    V.tensor_reduce(amax[:], att3, axis=AX.X, op=ALU.max)
                    dve.drain()
                    V.tensor_tensor(att3, att3, amax[:].unsqueeze(2).to_broadcast([P, NT * H, H]), ALU.subtract).then_inc(sub_ready, 1)

                def ffn_softmax_divide(b):
                    dve.wait_ge(aexp_done, b + 1)
                    V.tensor_reduce(asum[:], att3, axis=AX.X, op=ALU.add)
                    dve.drain()
                    V.reciprocal(asum[:], asum[:])
                    dve.drain()
                    V.tensor_tensor(att3, att3, asum[:].unsqueeze(2).to_broadcast([P, NT * H, H]), ALU.mult)
                    dve.drain()

                half = H // 2

                def ffn_weigh(t, u):
                    v4 = kv[:, t].rearrange("p (g two d) -> p two d g", two=2, d=HD)[:, 1]
                    a4 = att[:, t].rearrange("p (h g) -> p h g", g=H)[:, u * half:(u + 1) * half]
                    V.tensor_tensor(prod[:, u].rearrange("p (h d g) -> p h d g", h=half, d=HD),
                                    a4.unsqueeze(2).to_broadcast([P, half, HD, H]), v4.unsqueeze(1).to_broadcast([P, half, HD, H]), ALU.mult)

                def ffn_gather(t, u):
                    return V.tensor_reduce(o[:, t, u * P:(u + 1) * P], prod[:, u].rearrange("p (x g) -> p x g", g=H),
                                    axis=AX.X, op=ALU.add)

                def ffn_residual(b):
                    if not first(b):
                        dve.wait_ge(x2_stored, 16 * b)
                    ps, full, free, turn = ffn.at("out", b)
                    dve.wait_ge(full, turn)
                    V.tensor_tensor(y[:], ps[:].rearrange("p (t n) -> p t n", t=NT), bfo[:].unsqueeze(1).to_broadcast([P, NT, D]),
                                    ALU.add).then_inc(free, 1)
                    dve.drain()
                    V.tensor_tensor(y[:], y[:], n[:], ALU.add)
                    dve.drain()
                    for t in range(NT):
                        V.tensor_tensor_reduce(out=ytmp[:, t], in0=y[:, t], in1=y[:, t], scale=1.0 / D, scalar=0.0,
                                               op0=ALU.mult, op1=ALU.add, accum_out=ms2[:, t:t + 1])
                    dve.drain()
                    V.tensor_scalar(ms2[:], ms2[:], RMS_EPS, None, ALU.add).then_inc(ms2_ready, 1)

                def ffn_norm2(b):
                    dve.wait_ge(r2_ready, b + 1)
                    for t in range(NT):
                        last = V.tensor_scalar(h[:, t], y[:, t], r2[:, t:t + 1], None, ALU.mult)
                    last.then_inc(h2_ready, 1)

                def ffn_gate_logits(b):
                    for t in range(NT):
                        ps, full, free, turn = ffn.at(f"gate{t}", b)
                        dve.wait_ge(full, turn)
                        V.tensor_tensor(glog[:, t], ps[:, 0:E], bg[:], ALU.add).then_inc(free, 1)
                    dve.drain()
                    V.tensor_reduce(gmax[:], glog[:], axis=AX.X, op=ALU.max, negate=True).then_inc(glog_ready, 1)

                def ffn_gate(b):
                    dve.wait_ge(gexp_done, b + 1)
                    V.reciprocal(gsum[:], gsum[:])
                    dve.drain()
                    V.tensor_tensor(gate[:], gate[:], gsum[:].unsqueeze(2).to_broadcast([P, NT, E]), ALU.mult)
                    dve.drain()

                def ffn_experts(b, t, u):
                    ps, full, free, turn = ffn.at(f"we{t * 4 + u}", b)
                    dve.wait_ge(full, turn)
                    for w in range(2):
                        e = 2 * u + w
                        last = V.scalar_tensor_tensor(out=y[:, t], in0=ps[:, w * D:(w + 1) * D], scalar=gate[:, t, e:e + 1], in1=y[:, t],
                                                      op0=ALU.mult, op1=ALU.add)
                        if w == 0:
                            dve.drain()
                    last.then_inc(free, 1)
                    dve.drain()

                def ffn_final(b):
                    dve.wait_ge(x1_copied, b + 1)
                    if not first(b):
                        dve.wait_ge(x2_stored, 16 * b)
                    V.scalar_tensor_tensor(out=x2out[:], in0=y[:], scalar=tg[:, 1:2], in1=x1res[:], op0=ALU.mult, op1=ALU.add).then_inc(x2_ready, 1)

                def attn_max(a, j):
                    ps, full, free, turn = score.at(f"s{j}", a)
                    wait_apart(dve, dve_passed, full, turn)
                    for t, lo, hi in ((1, 0, S), (0, S, CAUSAL)):
                        last = V.tensor_tensor_reduce(out=probs[:, j % 4, lo:hi], in0=ps[:, lo:hi], in1=mbias[:, lo:hi], scale=-HD0 ** -0.5,
                                                      scalar=3e38, op0=ALU.add, op1=ALU.min, accum_out=negmax[:, j, t:t + 1])
                    last.then_inc(free, 1)

                def attn_sum(a, j):
                    dve.wait_ge(exp_done, H * a + j + 1)
                    V.reciprocal(rinv[:, j], rsum[:, j]).then_inc(rinv_ready, 1)

                def attn_final(a):
                    ps, full, free, turn = attn.at("out", a)
                    dve.wait_ge(full, turn)
                    V.tensor_tensor(ytmp[:], ps[:].rearrange("p (t n) -> p t n", t=NT), bo[:].unsqueeze(1).to_broadcast([P, NT, D]),
                                    ALU.add).then_inc(free, 1)
                    dve.drain()
                    dve.wait_ge(xres_in, 16 * (a + 1))
                    V.scalar_tensor_tensor(out=x1[:], in0=ytmp[:], scalar=tg[:, 0:1], in1=x1[:], op0=ALU.mult,
                                           op1=ALU.add).then_inc(x1_ready, 1)

                def ffn_step(b, s):
                    if s == 0 or s == 1:
                        ffn_scores(b, s)
                    elif s == 2:
                        ffn_softmax_max(b)
                    elif s == 4:
                        ffn_softmax_divide(b)
                        ffn_weigh(0, 0)
                    elif s == 5:
                        ffn_weigh(0, 1)
                        dve.drain()
                    elif s == 6:
                        ffn_gather(0, 0)
                        ffn_gather(0, 1)
                        dve.drain()
                    elif s == 7:
                        ffn_weigh(1, 0)
                    elif s == 8:
                        ffn_weigh(1, 1)
                        dve.drain()
                    elif s == 9:
                        ffn_gather(1, 0)
                        ffn_gather(1, 1).then_inc(o_ready, 1)
                    elif s == 11:
                        low(ffn, "oT", b, foT, foT_hi)
                    elif s == 13:
                        ffn_residual(b)
                    elif s == 14:
                        ffn_norm2(b)
                    elif s == 15:
                        low(ffn, "h2T", b, hT, h2T_hi, gamma2)

                def body(a, b, nxt):
                    if b is not None:
                        ffn_norm(b)
                        low(ffn, "hT", b, hT, hT_hi, gamma1)
                    if a is not None:
                        low(attn, "xT", a, xT, xT_hi)
                        dve.wait_ge(mask_ready, a + 1)
                    if b is not None:
                        ffn_project(b)
                        ffn_kv(b, 0)
                        ffn_kv(b, 1)
                    for s in range(H):
                        if b is not None:
                            ffn_step(b, s)
                        if a is not None:
                            attn_max(a, s)
                            if s >= 1:
                                attn_sum(a, s - 1)
                        if nxt is not None and s == 9:
                            pre_variance(nxt)
                        if nxt is not None and s == 13:
                            pre_normalise(nxt)
                    if a is not None:
                        attn_sum(a, H - 1)
                    if b is not None:
                        ffn_gate_logits(b)
                        ffn_gate(b)
                        for u in range(4):
                            ffn_experts(b, 0, u)
                    if a is not None:
                        attn_final(a)
                    if b is not None:
                        for u in range(4):
                            ffn_experts(b, 1, u)
                        ffn_final(b)

                for k, (src, hi, lo, rows) in enumerate(splits):
                    dve.wait_ge(split_hi, k + 1)
                    V.tensor_sub(lo, stage[0:rows, k % 2, 0:src.shape[1]], hi.bitcast(F32)).then_inc(split_lo, 1)
                dve.wait_ge(params_in, 16 * len(params))
                dve.wait_ge(tanh_done, 1)
                pre_variance(0)
                pre_normalise(0)
                body(0, None, 1)
                body(1, 0, 2)
                with dve.Fori(2, B - 1) as a:
                    body(a, a - 1, a + 1)
                body(B - 1, B - 2, None)
                body(None, B - 1, None)

            @block.tensor
            def _(pe):
                T = nc.tensor

                def transpose4(banks, use, batch, src):
                    ps, full, free, turn = banks.at(use, batch)
                    pe.wait_ge(free, turn)
                    for c in range(ND):
                        for t in range(NT):
                            last = T.transpose(ps[:, c * S + t * P:c * S + (t + 1) * P], src[:, t, c * P:(c + 1) * P], ident[:])
                    last.then_inc(full, 1)

                def features(use, a, w, x):
                    j = int(use[1:])
                    ps, full, free, turn = attn.at(use, a)
                    pe.wait_ge(free, turn)
                    for u in range(2):
                        m = slice((2 * j + u) * P, (2 * j + u + 1) * P)
                        last = product3(nc, ps[:, u * S:(u + 1) * S],
                                        [(w[0][:, c, m], w[1][:, c, m], x[0][:, c, :], x[1][:, c, :]) for c in range(ND)])
                    last.then_inc(full, 1)

                def values(j, a):
                    t, m = j // 2, slice((j % 2) * 512, (j % 2 + 1) * 512)
                    ps, full, free, turn = attn.at(f"v{j}", a)
                    pe.wait_ge(free, turn)
                    product3(nc, ps[:], [(cT[0][:, c, t * P:(t + 1) * P], cT[1][:, c, t * P:(t + 1) * P], wv[0][:, c, m], wv[1][:, c, m])
                                         for c in range(ND)]).then_inc(full, 1)

                def tokens(use, b, x, w, cols):
                    ps, full, free, turn = ffn.at(use, b)
                    pe.wait_ge(free, turn)
                    for t in range(NT):
                        last = product3(nc, ps[:, t * cols:(t + 1) * cols],
                                        [(x[0][:, c, t * P:(t + 1) * P], x[1][:, c, t * P:(t + 1) * P], w[0][:, c, :], w[1][:, c, :])
                                         for c in range(ND)])
                    last.then_inc(full, 1)

                def ffn_down(b):
                    ps, full, free, turn = ffn.at("down", b)
                    pe.wait_ge(free, turn)
                    product3(nc, ps[0:LAT, 0:S], [(fdown[0][:, c, :], fdown[1][:, c, :], hT[0][:, c, :], hT[1][:, c, :])
                                                  for c in range(ND)]).then_inc(full, 1)

                def ffn_up(b):
                    ffn.emptied(pe, "down", b)
                    for t in range(NT):
                        ps, full, free, turn = ffn.at(f"up{t}", b)
                        pe.wait_ge(free, turn)
                        product3(nc, ps[:], [(dT[0][:, t * P:(t + 1) * P], dT[1][:, t * P:(t + 1) * P], fup[0][:], fup[1][:])]).then_inc(full, 1)

                def ffn_experts(b, j):
                    t, u = j // 4, j % 4
                    ps, full, free, turn = ffn.at(f"we{j}", b)
                    pe.wait_ge(free, turn)
                    product3(nc, ps[:], [(hT[0][:, c, t * P:(t + 1) * P], hT[1][:, c, t * P:(t + 1) * P],
                                          we[0][:, c, u * 512:(u + 1) * 512], we[1][:, c, u * 512:(u + 1) * 512])
                                         for c in range(ND)]).then_inc(full, 1)

                def head_scores(a, j):
                    c, r = j // HPC, slice((j % HPC) * HD0, (j % HPC + 1) * HD0)
                    ps, full, free, turn = score.at(f"s{j}", a)
                    pe.wait_ge(free, turn)
                    T.matmul(ps[:, 0:S], qT[r, c, P:S], kT[r, c, :], start=True, stop=True)
                    T.matmul(ps[:, S:CAUSAL], qT[r, c, 0:P], kT[r, c, 0:P], start=True, stop=True).then_inc(full, 1)

                def head_transpose(a, j):
                    ps, full, free, turn = attn.at(f"T{j}", a)
                    pe.wait_ge(free, turn)
                    pe.wait_ge(norm_done, H * a + j + 1)
                    T.transpose(ps[:, 0:P], probs[:, j % 4, S:CAUSAL], ident[:])
                    T.transpose(ps[:, P:S], probs[:, j % 4, 0:P], ident[:])
                    T.transpose(ps[:, S:CAUSAL], probs[:, j % 4, P:S], ident[:]).then_inc(full, 1)

                def head_values(a, j):
                    g, u, r = j // 4, (j // HPC) % 2, slice((j % HPC) * HD0, (j % HPC + 1) * HD0)
                    ps, full, free, turn = heads.at(f"o{g}", a)
                    if j % 4 == 0:
                        pe.wait_ge(free, turn)
                    attn.emptied(pe, f"T{j}", a)
                    m = slice(j * HD0, (j + 1) * HD0)
                    T.matmul(ps[r, u * S:(u + 1) * S], v[:, 0, m], probsT[:, j % 2, 0:S], start=True, stop=False)
                    last = T.matmul(ps[r, u * S + P:(u + 1) * S], v[:, 1, m], probsT[:, j % 2, S:CAUSAL], start=False, stop=True)
                    last.then_inc(pv_done, 1)

                def attn_out(a):
                    ps, full, free, turn = attn.at("out", a)
                    pe.wait_ge(free, turn)
                    for t in range(NT):
                        for c in range(NC0):
                            last = T.matmul(ps[:, t * D:(t + 1) * D], oT[:, c, t * P:(t + 1) * P], wo[:, c, :], start=c == 0, stop=c == NC0 - 1)
                    last.then_inc(full, 1)

                def body(a, b, nxt):
                    if b is not None:
                        pe.wait_ge(h_ready, b + 1)
                        transpose4(ffn, "hT", b, h)
                    if a is not None:
                        pe.wait_ge(xn_ready, a + 1)
                        transpose4(attn, "xT", a, xn)
                    if b is not None:
                        ffn.emptied(pe, "hT", b)
                        tokens("q", b, hT, fq, D)
                        ffn_down(b)
                    if a is not None:
                        pe.wait_ge(ctx_ready, a + 1)
                        for j in range(4):
                            features(f"k{j}", a, wk, cT)
                    if b is not None:
                        ffn_up(b)
                    if a is not None:
                        for j in range(4):
                            values(j, a)
                        attn.emptied(pe, "xT", a)
                        for j in range(4):
                            features(f"q{j}", a, wq, xT)
                        for j in (2, 3):
                            attn.emptied(pe, f"q{j}", a)
                    for s in range(H + 3):
                        if a is not None:
                            if s < H:
                                head_scores(a, s)
                            if 2 <= s < H + 2:
                                head_transpose(a, s - 2)
                            if s >= 3:
                                head_values(a, s - 3)
                        if b is not None:
                            if s == 9:
                                pe.wait_ge(o_ready, b + 1)
                                transpose4(ffn, "oT", b, o)
                            elif s == 12:
                                ffn.emptied(pe, "oT", b)
                                tokens("out", b, foT, fo, D)
                            elif s == 14:
                                pe.wait_ge(h2_ready, b + 1)
                                transpose4(ffn, "h2T", b, h)
                            elif s == 16:
                                ffn.emptied(pe, "h2T", b)
                                for t in range(NT):
                                    ps, full, free, turn = ffn.at(f"gate{t}", b)
                                    pe.wait_ge(free, turn)
                                    product3(nc, ps[:, 0:E], [(hT[0][:, c, t * P:(t + 1) * P], hT[1][:, c, t * P:(t + 1) * P],
                                                               wg[0][:, c, :], wg[1][:, c, :]) for c in range(ND)]).then_inc(full, 1)
                    if b is not None:
                        for j in range(4):
                            ffn_experts(b, j)
                    if a is not None:
                        heads.emptied(pe, "o2", a)
                        heads.emptied(pe, "o3", a)
                        attn_out(a)
                    if b is not None:
                        for j in range(4, E):
                            ffn_experts(b, j)

                pe.wait_ge(consts, 1)
                pe.wait_ge(params_in, 16 * len(params))
                pe.wait_ge(split_lo, NS)
                body(0, None, 1)
                body(1, 0, 2)
                with pe.Fori(2, B - 1) as a:
                    body(a, a - 1, a + 1)
                body(B - 1, B - 2, None)
                body(None, B - 1, None)


def layer1(nc, ins, x2, out):
    with ExitStack() as ctx:
        def sb(name, shape, dtype=F32):
            return ctx.enter_context(nc.sbuf_tensor("l1_" + name, shape, dtype))

        def sem(name):
            return ctx.enter_context(nc.semaphore("l1_" + name))

        def pair(name, shape):
            return sb(name + "_hi", shape, F32R), sb(name + "_lo", shape, F32R)

        wq, wk, wv = pair("wq", [P, ND, NC1 * P]), pair("wk", [P, ND, NC1 * P]), pair("wv", [P, ND, D])
        w1 = pair("w1", [P, ND, 3 * HID])
        wo, w2 = sb("wo", [P, NC1, D]), sb("w2", [P, 3 * NHC, D])
        bq, bk, b1 = sb("bq", [P, NC1]), sb("bk", [P, NC1]), sb("b1", [P, 3 * NHC])
        bv, bo, b2, b2sum = sb("bv", [P, D]), sb("bo", [P, D]), sb("b2", [P, 3, D]), sb("b2sum", [P, D])
        gw, gates, tg = sb("gw", [P, 2, D]), sb("gates", [P, 4]), sb("tg", [P, 4])
        ident, neghalf = sb("ident", [P, P]), sb("neghalf", [P, NT])
        again = sb("again", [P, 1])

        xin, ctxin, xn = sb("xin", [P, NT, D]), sb("ctxin", [P, ND, S]), sb("xn", [P, NT, D])
        statC, mvC, varC, rstdC = sb("statC", [P, NT, 6]), sb("mvC", [P, NT, 2]), sb("varC", [P, NT]), sb("rstdC", [P, NT])
        xT, cT, k = pair("xT", [P, ND, S]), pair("cT", [P, ND, S]), pair("k", [P, NC1, S])
        qfull, qhi, q = sb("qfull", [P, NC1, S]), sb("qhi", [P, NC1, S], F32R), sb("q", [P, NC1, S], F32R)
        v = sb("v", [P, NT, H, SLOT])
        probs, probsT = sb("probs", [P, 4, NT * S]), sb("probsT", [P, 2, NT * S])
        negmax, rsum, rinv = sb("negmax", [P, H, NT]), sb("rsum", [P, H, NT]), sb("rinv", [P, H, NT])
        oT, x3, ytmp = sb("oT", [P, NC1, S]), sb("x3", [P, NT, D]), sb("ytmp", [P, NT, D])

        x3res, xf, x0 = sb("x3res", [P, NT, D]), sb("xf", [P, NT, D]), sb("x0", [P, NT, D])
        statF, mvF, varF, rstdF = sb("statF", [P, NT, 6]), sb("mvF", [P, NT, 2]), sb("varF", [P, NT]), sb("rstdF", [P, NT])
        gscore, first_wins = sb("gscore", [P, NT, 2]), sb("first_wins", [P, NT])
        xfT, x0T, x1T = pair("xfT", [P, ND, S]), pair("x0T", [P, ND, S]), pair("x1T", [P, ND, S])
        hid = sb("hid", [P, 3 * NHC, S])
        stage = hid[:].rearrange("p (a c) n -> p a (c n)", a=2)
        x4 = sb("x4", [P, NT, D])

        attn = Banks(nc, ctx, "l1_attn", ["xT", "k0", "k1", "v0", "v1", "q0", "q1"] + [f"T{j}" for j in range(H)] + ["out"])
        score = Banks(nc, ctx, "l1_score", [f"s{j}" for j in range(H)])
        heads = Banks(nc, ctx, "l1_heads", ["o0", "o1"])
        ffn = Banks(nc, ctx, "l1_ffn", ["xfT", "x0T"] + [f"h{j}" for j in range(12)] + ["y0", "y1"])

        raw_in, split_hi, split_lo = [sem("raw_in0"), sem("raw_in1")], sem("split_hi"), sem("split_lo")
        pool_passed, dve_passed, sp_passed = sem("pool_passed"), sem("dve_passed"), sem("sp_passed")
        params_in, consts, tanh_done, bias_ready = sem("params_in"), sem("consts"), sem("tanh_done"), sem("bias_ready")
        x_in, ctx_in, xres_in, x4_stored = sem("x_in"), sem("ctx_in"), sem("xres_in"), sem("x4_stored")
        varC_ready, rstdC_ready, xn_ready, ctx_ready = sem("varC_ready"), sem("rstdC_ready"), sem("xn_ready"), sem("ctx_ready")
        xT_hi, k_hi, q_hi, max_ready = sem("xT_hi"), sem("k_hi"), sem("q_hi"), sem("max_ready")
        exp_done, rinv_ready, norm_done, pv_done = sem("exp_done"), sem("rinv_ready"), sem("norm_done"), sem("pv_done")
        x3_ready, x3_copied, varF_ready, rstdF_ready = sem("x3_ready"), sem("x3_copied"), sem("varF_ready"), sem("rstdF_ready")
        xf_ready, xfT_hi, x0T_hi, x1T_ready, x4_ready = sem("xf_ready"), sem("xfT_hi"), sem("x0T_hi"), sem("x1T_ready"), sem("x4_ready")

        def flat(t):
            return t[:].rearrange("p c n -> p (c n)")
        splits = [(ins["wk1"], flat(wk[0]), flat(wk[1])), (ins["wv1"], flat(wv[0]), flat(wv[1])), (ins["wq1"], flat(wq[0]), flat(wq[1])),
                  (ins["w1"][:, 0, :], w1[0][:, 0, :], w1[1][:, 0, :]), (ins["w1"][:, 1, :], w1[0][:, 1, :], w1[1][:, 1, :])]
        NS = len(splits)
        params = [(flat(wo), ins["wo1"]), (bq[:], ins["bq1"]), (bk[:], ins["bk1"]), (b1[:], ins["b1"]),
                  (bv[:], ins["bv1"].to_broadcast([P, D])), (bo[:], ins["bo1"].to_broadcast([P, D])),
                  (flat(b2), ins["b2"].to_broadcast([P, 3 * D])), (flat(gw), ins["gw"].to_broadcast([P, 2 * D])),
                  (gates[:], ins["gates"].to_broadcast([P, 4])), (again[:], ins["again"]), (flat(w2), ins["w2"])]

        with nc.Block() as block:

            @block.sync
            def _(sp):
                def load(b):
                    if not first(b):
                        sp.wait_ge(xn_ready, b)
                    sp.dma_start(xin[:], x2[bass.ds(b, 1)][0]).then_inc(x_in, 16)
                    if not first(b):
                        sp.wait_ge(ctx_ready, b)
                    sp.dma_start(ctxin[:], ins["ctx"][bass.ds(b, 1)][0]).then_inc(ctx_in, 16)

                def load_residual(b):
                    if not first(b):
                        sp.wait_ge(x3_copied, b)
                        sp.wait_ge(xf_ready, b)
                    sp.dma_start(x3[:], x2[bass.ds(b, 1)][0]).then_inc(xres_in, 16)

                def store(b):
                    sp.wait_ge(x4_ready, b + 1)
                    sp.dma_start(out[bass.ds(b, 1)][0], x4[:]).then_inc(x4_stored, 16)

                load(0)
                load_residual(0)
                for n, (src, _hi, _lo) in enumerate(splits):
                    if n >= 2:
                        sp.wait_ge(split_lo, n - 1)
                    sp.dma_start(stage[:, n % 2, 0:src.shape[1]], src).then_inc(raw_in[n % 2], 16)
                    if n == 1:
                        for dst, src in params:
                            sp.dma_start(dst, src).then_inc(params_in, 16)
                load(1)
                load_residual(1)
                with sp.Fori(2, B) as b:
                    load(b)
                    store(b - 2)
                    load_residual(b)
                store(B - 2)
                store(B - 1)
                sp.wait_ge(x4_stored, 16 * B)

            @block.gpsimd
            def _(pool):
                nc.gpsimd.memset(ident[:], 0.0)
                nc.gpsimd.memset(neghalf[:], -0.5)
                nc.gpsimd.memset(v[:], 0.0)
                pool.drain()
                nc.gpsimd.affine_select(out=ident[:], in_=ident[:], compare_op=ALU.not_equal, fill=1.0, base=0,
                                        pattern=[[-1, P]], channel_multiplier=1).then_inc(consts, 1)

                def power(ready, done, src, dst, b):
                    pool.wait_ge(ready, b + 1)
                    nc.gpsimd.tensor_tensor(dst[:], src[:], neghalf[:], ALU.pow).then_inc(done, 1)

                def split_context(a):
                    if not first(a):
                        _, full, _, turn = attn.at("v1", a - 1)
                        pool.wait_ge(full, turn)
                    wait_apart(pool, pool_passed, ctx_in, 16 * (a + 1))
                    nc.gpsimd.tensor_copy(cT[0][:], ctxin[:])
                    pool.drain()
                    nc.gpsimd.tensor_sub(cT[1][:], ctxin[:], cT[0][:].bitcast(F32)).then_inc(ctx_ready, 1)

                def normalise(a, j):
                    wait_apart(pool, pool_passed, rinv_ready, H * a + j + 1)
                    for t in range(NT):
                        last = nc.gpsimd.tensor_scalar(probs[:, j % 4, t * S:(t + 1) * S], probs[:, j % 4, t * S:(t + 1) * S],
                                                       rinv[:, j, t:t + 1], 1.0, ALU.mult, ALU.mult)
                    last.then_inc(norm_done, 1)

                def copy_residual(b):
                    if not first(b):
                        pool.wait_ge(x4_ready, b)
                    wait_apart(pool, pool_passed, x3_ready, b + 1)
                    nc.gpsimd.tensor_copy(x3res[:], x3[:]).then_inc(x3_copied, 1)

                def other_tokens(b):
                    ffn.emptied(pool, "xfT", b)
                    ffn.emptied(pool, "x0T", b)
                    for part in range(2):
                        last = nc.gpsimd.tensor_sub(x1T[part][:], xfT[part][:].bitcast(F32), x0T[part][:].bitcast(F32))
                    last.then_inc(x1T_ready, 1)

                def body(a, b, nxt):
                    if b is not None:
                        power(varF_ready, rstdF_ready, varF, rstdF, b)
                        copy_residual(b)
                        other_tokens(b)
                    for j in range(H):
                        if a is not None:
                            normalise(a, j)
                        if nxt is not None and j == 6:
                            split_context(nxt)
                        if nxt is not None and j == 10:
                            power(varC_ready, rstdC_ready, varC, rstdC, nxt)

                split_context(0)
                power(varC_ready, rstdC_ready, varC, rstdC, 0)
                body(0, None, 1)
                body(1, 0, 2)
                with pool.Fori(2, B - 1) as a:
                    body(a, a - 1, a + 1)
                body(B - 1, B - 2, None)
                body(None, B - 1, None)

            @block.scalar
            def _(act):
                nc.scalar.preload_act_table(ACT.Exp)
                for n, (src, hi, _lo) in enumerate(splits):
                    act.wait_ge(raw_in[n % 2], 16 * (n // 2 + 1))
                    nc.scalar.copy(hi, stage[:, n % 2, 0:src.shape[1]]).then_inc(split_hi, 1)
                act.wait_ge(params_in, 16 * len(params))
                nc.scalar.activation(tg[:], gates[:], ACT.Tanh).then_inc(tanh_done, 1)
                act.wait_ge(bias_ready, 1)

                def high(banks, use, batch, dst, ready):
                    ps, full, _, turn = banks.at(use, batch)
                    act.wait_ge(full, turn)
                    nc.scalar.copy(flat(dst), ps[:]).then_inc(ready, 1)

                def keys_queries(a):
                    for name in ("k", "q"):
                        for j in range(2):
                            ps, full, _, turn = attn.at(f"{name}{j}", a)
                            act.wait_ge(full, turn)
                            for u in range(2):
                                c, src = 2 * j + u, ps[:, u * S:(u + 1) * S]
                                if name == "k":
                                    last = nc.scalar.activation(k[0][:, c, :], src, ACT.Identity, bias=bk[:, c:c + 1])
                                else:
                                    nc.scalar.activation(qfull[:, c, :], src, ACT.Identity, bias=bq[:, c:c + 1], scale=HD ** -0.5)
                                    last = nc.scalar.activation(qhi[:, c, :], src, ACT.Identity, bias=bq[:, c:c + 1], scale=HD ** -0.5)
                            last.then_inc(k_hi if name == "k" else q_hi, 1)

                def hidden(b, j):
                    ps, full, free, turn = ffn.at(f"h{j}", b)
                    act.wait_ge(full, turn)
                    for u in range(2):
                        c = 2 * j + u
                        last = nc.scalar.activation(hid[:, c, :], ps[:, u * S:(u + 1) * S], ACT.Relu, bias=b1[:, c:c + 1])
                    last.then_inc(free, 1)

                def body(a, b, nxt):
                    if b is not None:
                        high(ffn, "xfT", b, xfT[0], xfT_hi)
                        high(ffn, "x0T", b, x0T[0], x0T_hi)
                    if a is not None:
                        high(attn, "xT", a, xT[0], xT_hi)
                        keys_queries(a)
                    for s in range(H + 3):
                        if b is not None and 1 <= s <= 12:
                            hidden(b, s - 1)
                        if a is not None and s < H:
                            ps, _, free, _ = score.at(f"s{s}", a)
                            act.wait_ge(max_ready, H * a + s + 1)
                            for t in range(NT):
                                last = nc.scalar.activation(probs[:, s % 4, t * S:(t + 1) * S], ps[:, t * S:(t + 1) * S], ACT.Exp,
                                                            bias=negmax[:, s, t:t + 1], accum_out=rsum[:, s, t:t + 1])
                            last.then_inc(free, 1)
                        if a is not None and s in (10, 18):
                            g = (s - 10) // 8
                            ps, _, free, _ = heads.at(f"o{g}", a)
                            act.wait_ge(pv_done, H * a + 8 * g + 8)
                            nc.scalar.copy(oT[:, 2 * g:2 * g + 2, :].rearrange("p c n -> p (c n)"), ps[:]).then_inc(free, 1)

                body(0, None, 1)
                body(1, 0, 2)
                with act.Fori(2, B - 1) as a:
                    body(a, a - 1, a + 1)
                body(B - 1, B - 2, None)
                body(None, B - 1, None)

            @block.vector
            def _(dve):
                for banks in (attn, score, heads, ffn):
                    banks.open(dve)
                V = nc.vector

                def variance(src, stat, mv, var, ready):
                    for t in range(NT):
                        V.bn_stats(stat[:, t], src[:, t])
                    dve.drain()
                    for t in range(NT):
                        V.bn_aggr(mv[:, t], stat[:, t])
                    dve.drain()
                    V.tensor_scalar(var[:], mv[:, :, 1], LN_EPS, None, ALU.add).then_inc(ready, 1)

                def pre_variance(a):
                    dve.wait_ge(x_in, 16 * (a + 1))
                    variance(xin, statC, mvC, varC, varC_ready)

                def pre_normalise(a):
                    dve.wait_ge(rstdC_ready, a + 1)
                    for t in range(NT):
                        last = V.tensor_scalar(xn[:, t], xin[:, t], mvC[:, t, 0:1], rstdC[:, t:t + 1], ALU.subtract, ALU.mult)
                    last.then_inc(xn_ready, 1)

                def low(banks, use, batch, dst, hi_ready):
                    ps, _, free, _ = banks.at(use, batch)
                    dve.wait_ge(hi_ready, batch + 1)
                    V.tensor_sub(flat(dst[1]), ps[:], flat(dst[0]).bitcast(F32)).then_inc(free, 1)

                def ffn_norm(b):
                    dve.drain()
                    variance(x3, statF, mvF, varF, varF_ready)
                    dve.wait_ge(rstdF_ready, b + 1)
                    for t in range(NT):
                        V.tensor_scalar(xf[:, t], x3[:, t], mvF[:, t, 0:1], rstdF[:, t:t + 1], ALU.subtract, ALU.mult)
                    dve.drain()
                    for t in range(NT):
                        for e in range(2):
                            V.tensor_tensor_reduce(out=(ytmp, x0)[t][:, e], in0=xf[:, t], in1=gw[:, e], scale=1.0, scalar=0.0,
                                                   op0=ALU.mult, op1=ALU.add, accum_out=gscore[:, t, e:e + 1])
                    dve.drain()
                    V.tensor_tensor(first_wins[:], gscore[:, :, 0], gscore[:, :, 1], ALU.is_ge)
                    dve.drain()
                    for t in range(NT):
                        last = V.tensor_scalar(x0[:, t], xf[:, t], first_wins[:, t:t + 1], None, ALU.mult)
                    last.then_inc(xf_ready, 1)

                def keys(a, j):
                    ps, _, free, _ = attn.at(f"k{j}", a)
                    dve.wait_ge(k_hi, 2 * a + j + 1)
                    for u in range(2):
                        c = 2 * j + u
                        last = V.scalar_tensor_tensor(out=k[1][:, c, :], in0=ps[:, u * S:(u + 1) * S], scalar=bk[:, c:c + 1],
                                                      in1=k[0][:, c, :].bitcast(F32), op0=ALU.add, op1=ALU.subtract)
                    last.then_inc(free, 1)

                def values(a, t):
                    ps, full, free, turn = attn.at(f"v{t}", a)
                    dve.wait_ge(full, turn)
                    V.tensor_tensor(v[:, t, :, 0:HD], ps[:, 0:D].rearrange("p (h d) -> p h d", d=HD),
                                    bv[:].rearrange("p (h d) -> p h d", d=HD), ALU.add).then_inc(free, 1)

                def queries(a, j):
                    _, _, free, _ = attn.at(f"q{j}", a)
                    dve.wait_ge(q_hi, 2 * a + j + 1)
                    V.scalar_tensor_tensor(out=q[:, 2 * j:2 * j + 2, :], in0=qhi[:, 2 * j:2 * j + 2, :].bitcast(F32), scalar=again[:],
                                           in1=qfull[:, 2 * j:2 * j + 2, :], op0=ALU.mult, op1=ALU.add).then_inc(free, 1)

                def attn_max(a, j):
                    ps, full, _, turn = score.at(f"s{j}", a)
                    dve.wait_ge(full, turn)
                    V.tensor_reduce(negmax[:, j], ps[:].rearrange("p (t k) -> p t k", t=NT), axis=AX.X, op=ALU.max,
                                    negate=True).then_inc(max_ready, 1)

                def attn_sum(a, j):
                    score.emptied(dve, f"s{j}", a)
                    V.reciprocal(rinv[:, j], rsum[:, j]).then_inc(rinv_ready, 1)

                def attn_copy(a, j):
                    ps, full, free, turn = attn.at(f"T{j}", a)
                    dve.wait_ge(full, turn)
                    if j >= 2:
                        dve.wait_ge(pv_done, H * a + j - 1)
                    V.tensor_copy(probsT[:, j % 2, :], ps[:]).then_inc(free, 1)

                def attn_final(a):
                    ps, full, free, turn = attn.at("out", a)
                    dve.wait_ge(full, turn)
                    V.tensor_tensor(ytmp[:], ps[:].rearrange("p (t n) -> p t n", t=NT), bo[:].unsqueeze(1).to_broadcast([P, NT, D]),
                                    ALU.add).then_inc(free, 1)
                    dve.drain()
                    dve.wait_ge(xres_in, 16 * (a + 1))
                    V.scalar_tensor_tensor(out=x3[:], in0=ytmp[:], scalar=tg[:, 2:3], in1=x3[:], op0=ALU.mult,
                                           op1=ALU.add).then_inc(x3_ready, 1)

                def ffn_final(b):
                    if not first(b):
                        dve.wait_ge(x4_stored, 16 * b)
                    for t in range(NT):
                        ps, full, free, turn = ffn.at(f"y{t}", b)
                        dve.wait_ge(full, turn)
                        V.tensor_tensor(x4[:, t], ps[:, 0:D], b2sum[:], ALU.add).then_inc(free, 1)
                    dve.drain()
                    dve.wait_ge(x3_copied, b + 1)
                    V.scalar_tensor_tensor(out=x4[:], in0=x4[:], scalar=tg[:, 3:4], in1=x3res[:], op0=ALU.mult,
                                           op1=ALU.add).then_inc(x4_ready, 1)

                def body(a, b, nxt):
                    if b is not None:
                        ffn_norm(b)
                        low(ffn, "xfT", b, xfT, xfT_hi)
                        low(ffn, "x0T", b, x0T, x0T_hi)
                    if a is not None:
                        low(attn, "xT", a, xT, xT_hi)
                        keys(a, 0)
                        keys(a, 1)
                        values(a, 0)
                        values(a, 1)
                        queries(a, 0)
                        queries(a, 1)
                    for s in range(H + 2):
                        if a is not None:
                            if s < H:
                                attn_max(a, s)
                            if 1 <= s < H + 1:
                                attn_sum(a, s - 1)
                            if s >= 2:
                                attn_copy(a, s - 2)
                        if nxt is not None and s == 9:
                            pre_variance(nxt)
                        if nxt is not None and s == 13:
                            pre_normalise(nxt)
                    if a is not None:
                        attn_final(a)
                    if b is not None:
                        ffn_final(b)

                for n, (src, hi, lo) in enumerate(splits):
                    dve.wait_ge(split_hi, n + 1)
                    V.tensor_sub(lo, stage[:, n % 2, 0:src.shape[1]], hi.bitcast(F32)).then_inc(split_lo, 1)
                dve.wait_ge(params_in, 16 * len(params))
                V.tensor_scalar(bq[:], bq[:], HD ** -0.5, None, ALU.mult).then_inc(bias_ready, 1)
                V.tensor_tensor(b2sum[:], b2[:, 1], b2[:, 2], ALU.add)
                dve.drain()
                V.tensor_tensor(b2sum[:], b2sum[:], b2[:, 0], ALU.add)
                dve.wait_ge(tanh_done, 1)
                dve.wait_ge(consts, 1)
                pre_variance(0)
                pre_normalise(0)
                body(0, None, 1)
                body(1, 0, 2)
                with dve.Fori(2, B - 1) as a:
                    body(a, a - 1, a + 1)
                body(B - 1, B - 2, None)
                body(None, B - 1, None)

            @block.tensor
            def _(pe):
                T = nc.tensor

                def transpose4(banks, use, batch, src):
                    ps, full, free, turn = banks.at(use, batch)
                    pe.wait_ge(free, turn)
                    for c in range(ND):
                        for t in range(NT):
                            last = T.transpose(ps[:, c * S + t * P:c * S + (t + 1) * P], src[:, t, c * P:(c + 1) * P], ident[:])
                    last.then_inc(full, 1)

                def features(banks, use, batch, w, x, chunk):
                    ps, full, free, turn = banks.at(use, batch)
                    pe.wait_ge(free, turn)
                    for u in range(2):
                        m = slice((chunk + u) * P, (chunk + u + 1) * P)
                        last = product3(nc, ps[:, u * S:(u + 1) * S],
                                        [(w[0][:, c, m], w[1][:, c, m], x[0][:, c, :], x[1][:, c, :]) for c in range(ND)])
                    last.then_inc(full, 1)

                def values(a, t):
                    ps, full, free, turn = attn.at(f"v{t}", a)
                    pe.wait_ge(free, turn)
                    m = slice(t * P, (t + 1) * P)
                    product3(nc, ps[:, 0:D], [(cT[0][:, c, m], cT[1][:, c, m], wv[0][:, c, :], wv[1][:, c, :])
                                              for c in range(ND)]).then_inc(full, 1)

                def head_scores(a, j):
                    c, r = j // HPC1, slice((j % HPC1) * SLOT, (j % HPC1 + 1) * SLOT)
                    ps, full, free, turn = score.at(f"s{j}", a)
                    pe.wait_ge(free, turn)
                    for t in range(NT):
                        for part in range(2):
                            last = T.matmul(ps[:, t * S:(t + 1) * S], q[r, c, t * P:(t + 1) * P], k[part][r, c, :], start=part == 0, stop=part == 1)
                    last.then_inc(full, 1)

                def head_transpose(a, j):
                    ps, full, free, turn = attn.at(f"T{j}", a)
                    pe.wait_ge(free, turn)
                    pe.wait_ge(norm_done, H * a + j + 1)
                    for kt in range(NT):
                        for t in range(NT):
                            last = T.transpose(ps[:, kt * S + t * P:kt * S + (t + 1) * P], probs[:, j % 4, t * S + kt * P:t * S + (kt + 1) * P], ident[:])
                    last.then_inc(full, 1)

                def head_values(a, j):
                    g, u, r = j // 8, (j // HPC1) % 2, slice((j % HPC1) * SLOT, (j % HPC1 + 1) * SLOT)
                    ps, _, free, turn = heads.at(f"o{g}", a)
                    if j % 8 == 0:
                        pe.wait_ge(free, turn)
                    attn.emptied(pe, f"T{j}", a)
                    for kt in range(NT):
                        last = T.matmul(ps[r, u * S:(u + 1) * S], v[:, kt, j, :], probsT[:, j % 2, kt * S:(kt + 1) * S], start=kt == 0, stop=kt == NT - 1)
                    last.then_inc(pv_done, 1)

                def attn_out(a):
                    ps, full, free, turn = attn.at("out", a)
                    heads.emptied(pe, "o0", a)
                    heads.emptied(pe, "o1", a)
                    pe.wait_ge(free, turn)
                    for t in range(NT):
                        for c in range(NC1):
                            last = T.matmul(ps[:, t * D:(t + 1) * D], oT[:, c, t * P:(t + 1) * P], wo[:, c, :], start=c == 0, stop=c == NC1 - 1)
                    last.then_inc(full, 1)

                def ffn_down(b, t, piece):
                    ps, full, free, turn = ffn.at(f"y{t}", b)
                    if piece == 0:
                        pe.wait_ge(free, turn)
                        ffn.emptied(pe, "h10", b)
                        ffn.emptied(pe, "h11", b)
                    n = 3 * NHC // 4
                    for c in range(piece * n, (piece + 1) * n):
                        last = T.matmul(ps[:, 0:D], hid[:, c, t * P:(t + 1) * P], w2[:, c, :], start=c == 0, stop=c == 3 * NHC - 1)
                    if piece == 3:
                        last.then_inc(full, 1)

                def body(a, b, nxt):
                    if b is not None:
                        pe.wait_ge(xf_ready, b + 1)
                        transpose4(ffn, "xfT", b, xf)
                        transpose4(ffn, "x0T", b, x0)
                    if a is not None:
                        pe.wait_ge(xn_ready, a + 1)
                        transpose4(attn, "xT", a, xn)
                        pe.wait_ge(ctx_ready, a + 1)
                        features(attn, "k0", a, wk, cT, 0)
                        features(attn, "k1", a, wk, cT, 2)
                        values(a, 0)
                        values(a, 1)
                        attn.emptied(pe, "xT", a)
                        features(attn, "q0", a, wq, xT, 0)
                        features(attn, "q1", a, wq, xT, 2)
                        attn.emptied(pe, "q0", a)
                        attn.emptied(pe, "q1", a)
                    for s in range(H + 3):
                        if a is not None:
                            if s < H:
                                head_scores(a, s)
                            if 2 <= s < H + 2:
                                head_transpose(a, s - 2)
                            if s >= 3:
                                head_values(a, s - 3)
                        if b is not None:
                            if s == 0:
                                ffn.emptied(pe, "xfT", b)
                                ffn.emptied(pe, "x0T", b)
                            if s == 8:
                                pe.wait_ge(x1T_ready, b + 1)
                            if s < 12:
                                features(ffn, f"h{s}", b, w1, (xfT, x0T, x1T)[s // 4], 2 * s)
                            if 14 <= s < 18:
                                ffn_down(b, 0, s - 14)
                    if a is not None:
                        attn_out(a)
                    if b is not None:
                        for piece in range(4):
                            ffn_down(b, 1, piece)

                pe.wait_ge(consts, 1)
                pe.wait_ge(params_in, 16 * len(params))
                pe.wait_ge(split_lo, NS)
                body(0, None, 1)
                body(1, 0, 2)
                with pe.Fori(2, B - 1) as a:
                    body(a, a - 1, a + 1)
                body(B - 1, B - 2, None)
                body(None, B - 1, None)



def chunked(w):
    c = w.shape[0] // P
    return w.reshape(c, P, w.shape[1]).transpose(1, 0, 2).reshape(P, c * w.shape[1])


def layouts(i):
    import numpy as np
    gates = np.stack([i["g_xattn"][0], i["g_ffn"][0], i["g_xattn"][1], i["g_ffn"][1]])[None]
    tiles = lambda x: x.reshape(B, NT, P, D).transpose(0, 2, 1, 3)
    w1 = np.concatenate([i["L1_ffn_sw1"][None], i["L1_ffn_w1"]])
    w2 = np.concatenate([i["L1_ffn_sw2"][None], i["L1_ffn_w2"]])
    b1 = np.concatenate([i["L1_ffn_sb1"][None], i["L1_ffn_b1"]])
    b2 = np.concatenate([i["L1_ffn_sb2"][None], i["L1_ffn_b2"]])
    again = np.zeros((P, 1), np.float32)
    again.reshape(HPC1, 2, HD)[:, 1] = -1.0

    def twice(w):
        w = w.reshape(*w.shape[:-1], H, 1, HD)
        return np.concatenate([w, w], axis=-2).reshape(*w.shape[:-3], NC1 * P)
    spread = np.zeros((H, SLOT, D), np.float32)
    spread[:, 0:HD] = i["L1_xattn_Wo"].T.reshape(H, HD, D)
    return {
        "wq1": chunked(twice(i["L1_xattn_Wq"].T)), "wk1": chunked(twice(i["L1_xattn_Wk"].T)), "wv1": chunked(i["L1_xattn_Wv"].T),
        "bq1": twice(i["L1_xattn_bq"]).reshape(NC1, P).T, "bk1": twice(i["L1_xattn_bk"]).reshape(NC1, P).T,
        "wo1": chunked(spread.reshape(H * SLOT, D)), "bv1": i["L1_xattn_bv"][None], "bo1": i["L1_xattn_bo"][None],
        "w1": w1.transpose(1, 0, 2).reshape(ND, P, 3 * HID).transpose(1, 0, 2), "b1": b1.reshape(3 * NHC, P).T,
        "w2": chunked(w2.reshape(3 * HID, D)), "b2": b2.reshape(1, 3 * D), "gw": i["L1_ffn_gate_w"].reshape(1, 2 * D),
        "again": again,
        "x": tiles(i["x"]),
        "ctx": i["ctx_1024"].transpose(0, 2, 1).reshape(B, ND, P, S).transpose(0, 2, 1, 3),
        "mask": i["mask_BxS2_bf1"],
        "gates": gates,
        "wq": chunked(i["L0_xattn_Wq"].T), "wk": chunked(i["L0_xattn_Wk"].T), "wv": chunked(i["L0_xattn_Wv"].T),
        "wo": chunked(i["L0_xattn_Wo"].T), "bo": i["L0_xattn_bo"][None],
        "fq": chunked(i["L0_ffn_Wq"]), "fdown": chunked(i["L0_ffn_Wdown"]), "fup": i["L0_ffn_Wup"], "fo": chunked(i["L0_ffn_Wo"]),
        "wg": chunked(i["L0_ffn_Wg"]),
        "we": i["L0_ffn_We"].transpose(1, 0, 2).reshape(ND, P, E * D).transpose(1, 0, 2),
        "bq": i["L0_ffn_bq"][None], "bup": i["L0_ffn_bup"][None], "bfo": i["L0_ffn_bo"][None], "bg": i["L0_ffn_bg"][None],
        "bdown": i["L0_ffn_bdown"][:, None],
        "gamma1": i["L0_ffn_gamma1"].reshape(ND, P).T, "gamma2": i["L0_ffn_gamma2"].reshape(ND, P).T,
    }


def kernel(**inputs):
    import numpy as np
    import concourse.bacc as bacc
    from concourse.bass_utils import run_bass_kernel_spmd

    nc = bacc.Bacc("TRN2", target_bir_lowering=False, num_devices=1)
    arrays = {f"in_{k}": np.ascontiguousarray(v) for k, v in layouts({k: np.asarray(v) for k, v in inputs.items()}).items()}
    ins = {k[3:]: nc.dram_tensor(k, v.shape, mybir.dt.from_np(v.dtype), kind="ExternalInput").ap() for k, v in arrays.items()}
    out = nc.dram_tensor("out", (B, P, NT, D), F32, kind="ExternalOutput").ap()
    x2 = nc.dram_tensor("x2", (B, P, NT, D), F32, kind="Internal").ap()
    layer0(nc, ins, x2)
    layer1(nc, ins, x2, out)
    got = run_bass_kernel_spmd(nc, [arrays], core_ids=[0]).results[0]["out"]
    return got.reshape(B, P, NT, D).transpose(0, 2, 1, 3).reshape(B, S, D)
```

```python
from contextlib import ExitStack

import concourse.bass as bass
from concourse import mybir
from concourse.alu_op_type import AluOpType as ALU

F32 = mybir.dt.float32
F32R = mybir.dt.float32r
U8 = mybir.dt.uint8
ACT = mybir.ActivationFunctionType
AX = mybir.AxisListType

B, S, D = 16, 256, 256
P = 128
NT = S // P
ND = D // P
H = 16
HD0 = 64
INNER = H * HD0
NC0 = INNER // P
HPC = P // HD0
HD = D // H
LAT = 64
E = 8
HID = 1024
NHC = HID // P
SLOT = 32
NC1 = H * SLOT // P
HPC1 = P // SLOT
LN_EPS = 1e-5
RMS_EPS = 1e-6
NEG = 1e30
CAUSAL = S + P
LAG_T, LAG_V = 3, 4
STEPS = H + LAG_V


class Banks:

    def __init__(self, nc, ctx, name, uses, count=2, ahead=()):
        assert len(uses) % count == 0
        self.uses, self.count, self.ahead = uses, count, list(ahead)
        self.bank = [ctx.enter_context(nc.psum_tensor(f"{name}{n}", [P, 512], F32)) for n in range(count)]
        self.full = [ctx.enter_context(nc.semaphore(f"{name}{n}_full")) for n in range(count)]
        self.free = [ctx.enter_context(nc.semaphore(f"{name}{n}_free")) for n in range(count)]

    def at(self, use, batch):
        uses = self.uses
        if use in self.ahead and first(batch):
            k = self.ahead.index(use)
        elif use in self.ahead:
            batch, k = batch - 1, len(self.ahead) + uses.index(use)
        else:
            if isinstance(batch, int) and batch == B - 1:
                uses = [u for u in uses if u not in self.ahead]
            k = len(self.ahead) + uses.index(use)
        turn = batch * (len(self.uses) // self.count) + k // self.count + 1
        n = k % self.count
        return self.bank[n], self.full[n], self.free[n], turn

    def emptied(self, engine, use, batch):
        _, _, free, turn = self.at(use, batch)
        engine.wait_ge(free, turn + 1)

    def open(self, engine):
        for f in self.free:
            engine.sem_inc(f, 1)


def first(batch):
    return isinstance(batch, int) and batch == 0


def wait_apart(engine, passed, sem, value):
    engine.wait_ge(sem, value)
    engine.sem_inc(passed, 1)


def product3(nc, out, terms):
    last = None
    for n, (wh, wl, xh, xl) in enumerate(terms):
        last = nc.tensor.matmul(out, wh, xh, start=n == 0, stop=False)
        last = nc.tensor.matmul(out, wh, xl, start=False, stop=False)
        last = nc.tensor.matmul(out, wl, xh, start=False, stop=n == len(terms) - 1)
    return last


def layer0(nc, ins, x2):
    with ExitStack() as ctx:
        def sb(name, shape, dtype=F32):
            return ctx.enter_context(nc.sbuf_tensor("l0_" + name, shape, dtype))

        def sem(name):
            return ctx.enter_context(nc.semaphore("l0_" + name))

        def pair(name, shape):
            return sb(name + "_hi", shape, F32R), sb(name + "_lo", shape, F32R)

        wq, wk, wv = pair("wq", [P, ND, INNER]), pair("wk", [P, ND, INNER]), pair("wv", [P, ND, INNER])
        fq, fdown, fup, fo = pair("fq", [P, ND, D]), pair("fdown", [P, ND, LAT]), pair("fup", [LAT, 2 * D]), pair("fo", [P, ND, D])
        wg, we = pair("wg", [P, ND, E]), pair("we", [P, ND, E * D])
        wo = sb("wo", [P, NC0, D])
        prod = sb("prod", [P, 2, H * D // 2])
        stage = prod
        bo, bq, bup, bfo, bg = sb("bo", [P, D]), sb("bq", [P, D]), sb("bup", [P, 2 * D]), sb("bfo", [P, D]), sb("bg", [P, E])
        bdown, gamma1, gamma2 = sb("bdown", [LAT, 1]), sb("gamma1", [P, ND]), sb("gamma2", [P, ND])
        gates, tg = sb("gates", [P, 4]), sb("tg", [P, 4])
        maskbits = sb("maskbits", [P, S], U8)
        ident, cmask, neghalf = sb("ident", [P, P]), sb("cmask", [P, CAUSAL]), sb("neghalf", [P, NT])

        xin, ctxin = sb("xin", [P, NT, D]), sb("ctxin", [P, ND, S])
        xn = sb("xn", [P, NT, D])
        statA, mvA, varA, rstdA = sb("statA", [P, NT, 6]), sb("mvA", [P, NT, 2]), sb("varA", [P, NT]), sb("rstdA", [P, NT])
        xT, cT = pair("xT", [P, ND, S]), pair("cT", [P, ND, S])
        qT, kT, v = sb("qT", [P, NC0, S]), sb("kT", [P, NC0, S]), sb("v", [P, NT, INNER])
        pos, mbias = sb("pos", [P, S]), sb("mbias", [P, CAUSAL])
        probs, probsT = sb("probs", [P, 4, CAUSAL]), sb("probsT", [P, 2, CAUSAL])
        negmax, rsum, rinv = sb("negmax", [P, H, NT]), sb("rsum", [P, H, NT]), sb("rinv", [P, H, NT])
        x1, ytmp = sb("x1", [P, NT, D]), sb("ytmp", [P, NT, D])
        oT = qT

        x1res, n, h = sb("x1res", [P, NT, D]), sb("n", [P, NT, D]), sb("h", [P, NT, D])
        statB, mvB, varB, rstdB = sb("statB", [P, NT, 6]), sb("mvB", [P, NT, 2]), sb("varB", [P, NT]), sb("rstdB", [P, NT])
        ms1, r1, ms2, r2 = sb("ms1", [P, NT]), sb("r1", [P, NT]), sb("ms2", [P, NT]), sb("r2", [P, NT])
        hT, dT = pair("hT", [P, ND, S]), pair("dT", [LAT, S])
        q, kv = sb("q", [P, NT, D]), sb("kv", [P, NT, 2 * D])
        att, amax, asum = sb("att", [P, NT, D]), sb("amax", [P, NT * H]), sb("asum", [P, NT * H])
        glog, gmax, gsum, gate = sb("glog", [P, NT, E]), sb("gmax", [P, NT]), sb("gsum", [P, NT]), sb("gate", [P, NT, E])
        y, acc, h2T = sb("y", [P, NT, D]), sb("acc", [P, NT, D]), pair("h2T", [P, ND, S])
        o, foT = h, hT

        own_at = {0: "k3", 1: "v1", 2: "v3", 3: "q2", 5: "q3"}
        ahead_at = {9: "k0", 10: "xT", 11: "k1", 13: "v0", 15: "k2", 17: "v2"}
        attn_uses = ["q0", "q1"]
        for s in range(STEPS):
            attn_uses += [f"T{s - LAG_T}"] * (LAG_T <= s < H + LAG_T)
            attn_uses += [use for at, use in (own_at | ahead_at).items() if at == s]
        attn = Banks(nc, ctx, "l0_attn", attn_uses + ["out"], ahead=["xT", "k0", "k1", "k2", "v0", "v2"])
        mix_at = {2: "hT", 3: "q", 4: "down", 5: "up0", 6: "up1"}
        expert_at = {7: 0, 8: 1, 10: 2, 12: 3, 14: 4, 16: 5, 17: 6, 18: 7}
        score_at = {7: 0, 9: 1, 11: 2, 12: 3}
        score = Banks(nc, ctx, "l0_score", [f"s{j}" for j in range(H)])
        heads = Banks(nc, ctx, "l0_heads", [f"o{j}" for j in range(4)])
        mix = Banks(nc, ctx, "l0_mix", ["hT", "q", "down", "up0", "up1"], 1)
        moe = Banks(nc, ctx, "l0_moe", ["oT", "out", "h2T", "gate0", "gate1"] + [f"we{j}" for j in range(E)], 1)

        raw_in, split_hi, split_lo = [sem("raw_in0"), sem("raw_in1")], sem("split_hi"), sem("split_lo")
        mask_in, scored = sem("mask_in"), sem("scored")
        pool_passed, dve_passed, sp_passed = sem("pool_passed"), sem("dve_passed"), sem("sp_passed")
        params_in, consts, tanh_done = sem("params_in"), sem("consts"), sem("tanh_done")
        x_in, ctx_in, xres_in, x2_stored = sem("x_in"), sem("ctx_in"), sem("xres_in"), sem("x2_stored")
        varA_ready, rstdA_ready, xn_ready, ctx_ready = sem("varA_ready"), sem("rstdA_ready"), sem("xn_ready"), sem("ctx_ready")
        mask_ready, exp_done, rinv_ready, norm_done = sem("mask_ready"), sem("exp_done"), sem("rinv_ready"), sem("norm_done")
        xT_hi, pv_done, x1_ready, x1_copied = sem("xT_hi"), sem("pv_done"), sem("x1_ready"), sem("x1_copied")
        varB_ready, rstdB_ready, ms1_ready, r1_ready = sem("varB_ready"), sem("rstdB_ready"), sem("ms1_ready"), sem("r1_ready")
        h_ready, hT_hi, dT_hi = sem("h_ready"), sem("hT_hi"), sem("dT_hi")
        prod_ready, sub_ready, aexp_done, o_ready = sem("prod_ready"), sem("sub_ready"), sem("aexp_done"), sem("o_ready")
        foT_hi, ms2_ready, r2_ready, h2_ready = sem("foT_hi"), sem("ms2_ready"), sem("r2_ready"), sem("h2_ready")
        att_ready, gathered = sem("att_ready"), sem("gathered")
        h2T_hi, glog_ready, gexp_done, x2_ready = sem("h2T_hi"), sem("glog_ready"), sem("gexp_done"), sem("x2_ready")

        def piece(src, dst, rows=P):
            return src, dst[0], dst[1], rows
        splits = [piece(ins["wk"], (wk[0][:].rearrange("p c n -> p (c n)"), wk[1][:].rearrange("p c n -> p (c n)"))),
                  piece(ins["wv"], (wv[0][:].rearrange("p c n -> p (c n)"), wv[1][:].rearrange("p c n -> p (c n)"))),
                  piece(ins["wq"], (wq[0][:].rearrange("p c n -> p (c n)"), wq[1][:].rearrange("p c n -> p (c n)"))),
                  piece(ins["fq"], (fq[0][:].rearrange("p c n -> p (c n)"), fq[1][:].rearrange("p c n -> p (c n)"))),
                  piece(ins["fdown"], (fdown[0][:].rearrange("p c n -> p (c n)"), fdown[1][:].rearrange("p c n -> p (c n)"))),
                  piece(ins["fup"], (fup[0][:], fup[1][:]), LAT),
                  piece(ins["fo"], (fo[0][:].rearrange("p c n -> p (c n)"), fo[1][:].rearrange("p c n -> p (c n)"))),
                  piece(ins["wg"], (wg[0][:].rearrange("p c n -> p (c n)"), wg[1][:].rearrange("p c n -> p (c n)"))),
                  piece(ins["we"][:, 0, :], (we[0][:, 0, :], we[1][:, 0, :])),
                  piece(ins["we"][:, 1, :], (we[0][:, 1, :], we[1][:, 1, :]))]
        NS = len(splits)
        params = [(wo[:].rearrange("p c n -> p (c n)"), ins["wo"]), (bo[:], ins["bo"].to_broadcast([P, D])),
                  (bq[:], ins["bq"].to_broadcast([P, D])), (bup[:], ins["bup"].to_broadcast([P, 2 * D])),
                  (bfo[:], ins["bfo"].to_broadcast([P, D])), (bg[:], ins["bg"].to_broadcast([P, E])),
                  (bdown[:], ins["bdown"]), (gamma1[:], ins["gamma1"]), (gamma2[:], ins["gamma2"]),
                  (gates[:], ins["gates"].to_broadcast([P, 4]))]

        with nc.Block() as block:

            @block.sync
            def _(sp):
                def load(b):
                    if not first(b):
                        sp.wait_ge(xn_ready, b)
                    sp.dma_start(xin[:], ins["x"][bass.ds(b, 1)][0]).then_inc(x_in, 16)
                    if not first(b):
                        sp.wait_ge(ctx_ready, b)
                    sp.dma_start(ctxin[:], ins["ctx"][bass.ds(b, 1)][0]).then_inc(ctx_in, 16)

                    if not first(b):
                        wait_apart(sp, sp_passed, mask_ready, b)
                    sp.dma_start(maskbits[:], ins["mask"][bass.ds(b, 1)].to_broadcast([P, S])).then_inc(mask_in, 16)

                def load_residual(b):
                    if not first(b):
                        sp.wait_ge(x1_copied, b)
                        sp.wait_ge(h_ready, b)
                    sp.dma_start(x1[:], ins["x"][bass.ds(b, 1)][0]).then_inc(xres_in, 16)

                def store(b):
                    sp.wait_ge(x2_ready, b + 1)
                    sp.dma_start(x2[bass.ds(b, 1)][0], acc[:]).then_inc(x2_stored, 16)

                load(0)
                load_residual(0)
                for k, (src, _hi, _lo, rows) in enumerate(splits):
                    if k >= 2:
                        sp.wait_ge(split_lo, k - 1)
                    sp.dma_start(stage[0:rows, k % 2, 0:src.shape[1]], src).then_inc(raw_in[k % 2], 16)
                    if k == 1:
                        for dst, src in params:
                            sp.dma_start(dst, src).then_inc(params_in, 16)
                load(1)
                load(2)
                load_residual(1)
                with sp.Fori(3, B) as b:
                    load(b)
                    load_residual(b - 1)
                    store(b - 3)
                load_residual(B - 1)
                for b in (B - 3, B - 2, B - 1):
                    store(b)
                sp.wait_ge(x2_stored, 16 * B)

            @block.gpsimd
            def _(pool):
                nc.gpsimd.memset(ident[:], 0.0)
                nc.gpsimd.memset(cmask[:], 0.0)
                nc.gpsimd.memset(neghalf[:], -0.5)
                pool.drain()
                nc.gpsimd.affine_select(out=ident[:], in_=ident[:], compare_op=ALU.not_equal, fill=1.0, base=0,
                                        pattern=[[-1, P]], channel_multiplier=1)
                for c in (P, S):
                    last = nc.gpsimd.affine_select(out=cmask[:, c:c + P], in_=cmask[:, c:c + P], compare_op=ALU.is_ge,
                                                   fill=-NEG, base=0, pattern=[[-1, P]], channel_multiplier=1)
                last.then_inc(consts, 1)

                def power(ready, done, src, dst, b):
                    pool.wait_ge(ready, b + 1)
                    nc.gpsimd.tensor_tensor(dst[:], src[:], neghalf[:], ALU.pow).then_inc(done, 1)

                def split_context(a):
                    if not first(a):
                        _, full, _, turn = attn.at("v3", a - 1)
                        pool.wait_ge(full, turn)
                    wait_apart(pool, pool_passed, ctx_in, 16 * (a + 1))
                    nc.gpsimd.tensor_copy(cT[0][:], ctxin[:])
                    pool.drain()
                    nc.gpsimd.tensor_sub(cT[1][:], ctxin[:], cT[0][:].bitcast(F32)).then_inc(ctx_ready, 1)

                def mask(a):
                    if not first(a):
                        score.emptied(pool, f"s{H - 2}", a - 1)
                        score.emptied(pool, f"s{H - 1}", a - 1)
                    wait_apart(pool, pool_passed, mask_in, 16 * (a + 1))
                    nc.gpsimd.tensor_scalar(pos[:], maskbits[:], -1.0, NEG, ALU.add, ALU.mult)
                    pool.drain()
                    nc.gpsimd.tensor_tensor(mbias[:, 0:S], cmask[:, 0:S], pos[:], ALU.add)
                    nc.gpsimd.tensor_tensor(mbias[:, S:CAUSAL], cmask[:, S:CAUSAL], pos[:, 0:P], ALU.add).then_inc(mask_ready, 1)

                def query_key(b, t, u):
                    half, piece = H // 2, NT * t + u
                    if piece < 2:
                        mix.emptied(pool, "q", b)
                        mix.emptied(pool, f"up{t}", b)
                    else:
                        mix.emptied(pool, f"up{t}", b)
                        pool.wait_ge(scored, 4 * b + piece - 1)
                    k4 = kv[:, t].rearrange("p (g two d) -> p g two d", two=2, d=HD)[:, :, 0, :]
                    q4 = q[:, t].rearrange("p (h d) -> p h d", d=HD)
                    nc.gpsimd.tensor_tensor(
                        prod[:, u].rearrange("p (h g d) -> p h g d", h=half, g=H),
                        q4[:, u * half:(u + 1) * half].unsqueeze(2).to_broadcast([P, half, H, HD]),
                        k4.unsqueeze(1).to_broadcast([P, half, H, HD]), ALU.mult).then_inc(prod_ready, 1)

                def weigh(b, u):
                    half = H // 2
                    if u == 0:
                        pool.wait_ge(att_ready, b + 1)
                    else:
                        pool.wait_ge(gathered, 2 * b + 1)
                    v4 = kv[:, 0].rearrange("p (g two d) -> p two d g", two=2, d=HD)[:, 1]
                    a4 = att[:, 0].rearrange("p (h g) -> p h g", g=H)[:, u * half:(u + 1) * half]
                    nc.gpsimd.tensor_tensor(prod[:, 1].rearrange("p (h d g) -> p h d g", h=half, d=HD),
                                            a4.unsqueeze(2).to_broadcast([P, half, HD, H]), v4.unsqueeze(1).to_broadcast([P, half, HD, H]),
                                            ALU.mult).then_inc(prod_ready, 1)

                def body(a, b, c, nxt):
                    if a is not None:
                        mask(a)
                    if b is not None:
                        power(varB_ready, rstdB_ready, varB, rstdB, b)
                    if b is not None:
                        power(ms1_ready, r1_ready, ms1, r1, b)
                    if c is not None:
                        power(ms2_ready, r2_ready, ms2, r2, c)
                    if nxt is not None:
                        split_context(nxt)
                        power(varA_ready, rstdA_ready, varA, rstdA, nxt)
                    if b is not None:
                        query_key(b, 0, 0)
                        query_key(b, 0, 1)
                        query_key(b, 1, 0)
                        query_key(b, 1, 1)
                        weigh(b, 0)
                        weigh(b, 1)

                split_context(0)
                power(varA_ready, rstdA_ready, varA, rstdA, 0)
                body(0, None, None, 1)
                body(1, 0, None, 2)
                body(2, 1, 0, 3)
                with pool.Fori(3, B - 1) as a:
                    body(a, a - 1, a - 2, a + 1)
                body(B - 1, B - 2, B - 3, None)
                body(None, B - 1, B - 2, None)
                body(None, None, B - 1, None)

            @block.scalar
            def _(act):
                nc.scalar.preload_act_table(ACT.Exp)
                for k, (src, hi, _lo, rows) in enumerate(splits):
                    act.wait_ge(raw_in[k % 2], 16 * (k // 2 + 1))
                    nc.scalar.copy(hi, stage[0:rows, k % 2, 0:src.shape[1]]).then_inc(split_hi, 1)
                act.wait_ge(params_in, 16 * len(params))
                nc.scalar.activation(tg[:], gates[:], ACT.Tanh).then_inc(tanh_done, 1)

                def high(banks, use, batch, dst, ready, scales=None):
                    ps, full, free, turn = banks.at(use, batch)
                    act.wait_ge(full, turn)
                    if scales is None:
                        nc.scalar.copy(dst[:].rearrange("p c n -> p (c n)"), ps[:]).then_inc(ready, 1)
                    else:
                        for c in range(ND):
                            last = nc.scalar.activation(dst[:, c, :], ps[:, c * S:(c + 1) * S], ACT.Copy, scale=scales[:, c:c + 1])
                        last.then_inc(ready, 1)

                def copy_out(use, a, dst):
                    ps, full, free, turn = attn.at(use, a)
                    act.wait_ge(full, turn)
                    nc.scalar.copy(dst, ps[:]).then_inc(free, 1)

                def pair_of(t, j):
                    return t[:, 2 * j:2 * j + 2, :].rearrange("p c n -> p (c n)")

                def attn_exp(a, s):
                    score.emptied(act, f"s{s}", a)
                    nc.scalar.activation(probs[:, s % 4, 0:S], probs[:, s % 4, 0:S], ACT.Exp, bias=negmax[:, s, 1:2],
                                         scale=-1.0, accum_out=rsum[:, s, 1:2])
                    nc.scalar.activation(probs[:, s % 4, S:CAUSAL], probs[:, s % 4, S:CAUSAL], ACT.Exp, bias=negmax[:, s, 0:1],
                                         scale=-1.0, accum_out=rsum[:, s, 0:1]).then_inc(exp_done, 1)

                def attn_normalise(a, j):
                    act.wait_ge(rinv_ready, H * a + j + 1)
                    nc.scalar.activation(probs[:, j % 4, 0:S], probs[:, j % 4, 0:S], ACT.Copy, scale=rinv[:, j, 1:2])
                    nc.scalar.activation(probs[:, j % 4, S:CAUSAL], probs[:, j % 4, S:CAUSAL], ACT.Copy,
                                         scale=rinv[:, j, 0:1]).then_inc(norm_done, 1)

                def attn_copy(a, j):
                    ps, full, free, turn = attn.at(f"T{j}", a)
                    act.wait_ge(full, turn)
                    if j >= 2:
                        act.wait_ge(pv_done, H * a + j - 1)
                    nc.scalar.copy(probsT[:, j % 2, :], ps[:, 0:CAUSAL]).then_inc(free, 1)

                def project(use, a):
                    j = int(use[1:]) if use != "xT" else None
                    if use == "xT":
                        high(attn, "xT", a, xT[0], xT_hi)
                    elif use[0] == "q":
                        copy_out(use, a, pair_of(qT, j))
                    elif use[0] == "k":
                        copy_out(use, a, pair_of(kT, j))
                    else:
                        copy_out(use, a, v[:, j // 2, (j % 2) * 512:(j % 2 + 1) * 512])

                def before_exp(b, c, s):
                    if b is not None and mix_at.get(s) == "hT":
                        high(mix, "hT", b, hT[0], hT_hi, gamma1)
                    if b is not None and mix_at.get(s) == "down":
                        ps, full, _, turn = mix.at("down", b)
                        act.wait_ge(full, turn)
                        nc.scalar.activation(dT[0][:], ps[0:LAT, 0:S], ACT.Identity, bias=bdown[:]).then_inc(dT_hi, 1)
                    if c is not None and s == 4:
                        high(moe, "h2T", c, h2T[0], h2T_hi, gamma2)

                def beside_head(a, b, c, nxt, s):
                    if c is not None and s == 6:
                        act.wait_ge(glog_ready, c + 1)
                        for t in range(NT):
                            last = nc.scalar.activation(gate[:, t], glog[:, t], ACT.Exp, bias=gmax[:, t:t + 1], accum_out=gsum[:, t:t + 1])
                        last.then_inc(gexp_done, 1)
                    if b is not None and s == 12:
                        act.wait_ge(sub_ready, b + 1)
                        nc.scalar.activation(att[:], att[:], ACT.Exp, scale=HD ** -0.5).then_inc(aexp_done, 1)
                    if a is not None and s in own_at:
                        project(own_at[s], a)
                    if nxt is not None and s in ahead_at:
                        project(ahead_at[s], nxt)

                def head_group(a, j):
                    ps, _, free, _ = heads.at(f"o{j}", a)
                    act.wait_ge(pv_done, H * a + 4 * j + 4)
                    nc.scalar.copy(pair_of(oT, j), ps[:]).then_inc(free, 1)

                def body(a, b, c, nxt):
                    if c is not None:
                        high(moe, "oT", c, foT[0], foT_hi)
                    if a is not None:
                        project("q0", a)
                        project("q1", a)
                    for s in range(STEPS):
                        if s >= 1:
                            beside_head(a, b, c, nxt, s - 1)
                        before_exp(b, c, s)
                        if a is not None:
                            if LAG_T <= s < H + LAG_T:
                                attn_copy(a, s - LAG_T)
                            if s < H:
                                attn_exp(a, s)
                            if 1 <= s < H + 1:
                                attn_normalise(a, s - 1)
                            if s - LAG_V in (4, 8, 12):
                                head_group(a, (s - LAG_V) // 4 - 1)
                    if a is not None:
                        head_group(a, 3)
                    beside_head(a, b, c, nxt, STEPS - 1)

                for use in attn.ahead:
                    project(use, 0)
                body(0, None, None, 1)
                body(1, 0, None, 2)
                body(2, 1, 0, 3)
                with act.Fori(3, B - 1) as a:
                    body(a, a - 1, a - 2, a + 1)
                body(B - 1, B - 2, B - 3, None)
                body(None, B - 1, B - 2, None)
                body(None, None, B - 1, None)

            @block.vector
            def _(dve):
                for banks in (attn, score, heads, mix, moe):
                    banks.open(dve)
                V = nc.vector

                def variance(src, stat, mv, var, ready):
                    for t in range(NT):
                        V.bn_stats(stat[:, t], src[:, t])
                    dve.drain()
                    for t in range(NT):
                        V.bn_aggr(mv[:, t], stat[:, t])
                    dve.drain()
                    V.tensor_scalar(var[:], mv[:, :, 1], LN_EPS, None, ALU.add).then_inc(ready, 1)

                def pre_variance(a):
                    dve.wait_ge(x_in, 16 * (a + 1))
                    variance(xin, statA, mvA, varA, varA_ready)

                def pre_normalise(a):
                    dve.wait_ge(rstdA_ready, a + 1)
                    for t in range(NT):
                        last = V.tensor_scalar(xn[:, t], xin[:, t], mvA[:, t, 0:1], rstdA[:, t:t + 1], ALU.subtract, ALU.mult)
                    last.then_inc(xn_ready, 1)

                def low(banks, use, batch, dst, hi_ready, scales=None):
                    ps, _, free, _ = banks.at(use, batch)
                    dve.wait_ge(hi_ready, batch + 1)
                    if scales is None:
                        last = V.tensor_sub(dst[1][:].rearrange("p c n -> p (c n)"), ps[:],
                                            dst[0][:].rearrange("p c n -> p (c n)").bitcast(F32))
                    else:
                        for c in range(ND):
                            last = V.scalar_tensor_tensor(out=dst[1][:, c, :], in0=ps[:, c * S:(c + 1) * S], scalar=scales[:, c:c + 1],
                                                          in1=dst[0][:, c, :].bitcast(F32), op0=ALU.mult, op1=ALU.subtract)
                    last.then_inc(free, 1)

                def mix_normalise(b):
                    dve.wait_ge(rstdB_ready, b + 1)
                    V.tensor_tensor(ms1[:], mvB[:, :, 1], rstdB[:], ALU.mult)
                    for t in range(NT):
                        V.tensor_scalar(n[:, t], x1[:, t], mvB[:, t, 0:1], rstdB[:, t:t + 1], ALU.subtract, ALU.mult)
                    dve.drain()
                    V.tensor_tensor(ms1[:], ms1[:], rstdB[:], ALU.mult)
                    dve.drain()
                    V.tensor_scalar(ms1[:], ms1[:], RMS_EPS, None, ALU.add).then_inc(ms1_ready, 1)

                def mix_rms(b):
                    dve.wait_ge(r1_ready, b + 1)
                    for t in range(NT):
                        last = V.tensor_scalar(h[:, t], n[:, t], r1[:, t:t + 1], None, ALU.mult)
                    last.then_inc(h_ready, 1)

                def mix_queries(b):
                    ps, full, free, turn = mix.at("q", b)
                    dve.wait_ge(full, turn)
                    V.tensor_tensor(q[:], ps[:].rearrange("p (t n) -> p t n", t=NT), bq[:].unsqueeze(1).to_broadcast([P, NT, D]),
                                    ALU.add).then_inc(free, 1)

                def mix_down(b):
                    ps, _, free, _ = mix.at("down", b)
                    dve.wait_ge(dT_hi, b + 1)
                    V.scalar_tensor_tensor(out=dT[1][:], in0=ps[0:LAT, 0:S], scalar=bdown[:], in1=dT[0][:].bitcast(F32),
                                           op0=ALU.add, op1=ALU.subtract).then_inc(free, 1)

                def mix_kv(b, t):
                    ps, full, free, turn = mix.at(f"up{t}", b)
                    dve.wait_ge(full, turn)
                    V.tensor_tensor(kv[:, t], ps[:], bup[:], ALU.add).then_inc(free, 1)

                def mix_scores(b, t, u):
                    dve.wait_ge(prod_ready, 6 * b + 2 * t + u + 1)
                    V.tensor_reduce(att[:, t, u * P:(u + 1) * P], prod[:, u].rearrange("p (x d) -> p x d", d=HD),
                                    axis=AX.X, op=ALU.add).then_inc(scored, 1)

                att3 = att[:].rearrange("p t (h g) -> p (t h) g", g=H)

                def mix_softmax_max(b):
                    dve.drain()
                    V.tensor_reduce(amax[:], att3, axis=AX.X, op=ALU.max)
                    dve.drain()
                    V.tensor_tensor(att3, att3, amax[:].unsqueeze(2).to_broadcast([P, NT * H, H]), ALU.subtract).then_inc(sub_ready, 1)

                def mix_softmax_divide(b):
                    dve.wait_ge(aexp_done, b + 1)
                    V.tensor_reduce(asum[:], att3, axis=AX.X, op=ALU.add)
                    dve.drain()
                    V.reciprocal(asum[:], asum[:])
                    dve.drain()
                    V.tensor_tensor(att3, att3, asum[:].unsqueeze(2).to_broadcast([P, NT * H, H]), ALU.mult).then_inc(att_ready, 1)
                    dve.drain()

                half = H // 2

                def mix_weigh(u):
                    v4 = kv[:, 1].rearrange("p (g two d) -> p two d g", two=2, d=HD)[:, 1]
                    a4 = att[:, 1].rearrange("p (h g) -> p h g", g=H)[:, u * half:(u + 1) * half]
                    V.tensor_tensor(prod[:, 0].rearrange("p (h d g) -> p h d g", h=half, d=HD),
                                    a4.unsqueeze(2).to_broadcast([P, half, HD, H]), v4.unsqueeze(1).to_broadcast([P, half, HD, H]), ALU.mult)

                def mix_gather(t, u, buffer):
                    return V.tensor_reduce(o[:, t, u * P:(u + 1) * P], prod[:, buffer].rearrange("p (x g) -> p x g", g=H),
                                           axis=AX.X, op=ALU.add)

                def moe_residual(c):
                    ps, full, free, turn = moe.at("out", c)
                    dve.wait_ge(full, turn)
                    V.tensor_tensor(y[:], ps[:].rearrange("p (t n) -> p t n", t=NT), bfo[:].unsqueeze(1).to_broadcast([P, NT, D]),
                                    ALU.add).then_inc(free, 1)
                    dve.drain()
                    V.tensor_tensor(y[:], y[:], n[:], ALU.add)
                    dve.drain()

                def moe_squares(c):
                    if not first(c):
                        dve.wait_ge(x2_stored, 16 * c)
                    V.scalar_tensor_tensor(out=acc[:], in0=y[:], scalar=tg[:, 1:2], in1=x1res[:], op0=ALU.mult, op1=ALU.add)
                    for t in range(NT):
                        V.tensor_tensor_reduce(out=ytmp[:, t], in0=y[:, t], in1=y[:, t], scale=1.0 / D, scalar=0.0,
                                               op0=ALU.mult, op1=ALU.add, accum_out=ms2[:, t:t + 1])
                    dve.drain()
                    V.tensor_scalar(ms2[:], ms2[:], RMS_EPS, None, ALU.add).then_inc(ms2_ready, 1)

                def moe_normalise(c):
                    dve.wait_ge(r2_ready, c + 1)
                    for t in range(NT):
                        last = V.tensor_scalar(y[:, t], y[:, t], r2[:, t:t + 1], None, ALU.mult)
                    last.then_inc(h2_ready, 1)

                def moe_gate_logits(c, t):
                    ps, full, free, turn = moe.at(f"gate{t}", c)
                    dve.wait_ge(full, turn)
                    V.tensor_tensor(glog[:, t], ps[:, 0:E], bg[:], ALU.add).then_inc(free, 1)
                    if t == NT - 1:
                        dve.drain()
                        V.tensor_reduce(gmax[:], glog[:], axis=AX.X, op=ALU.max, negate=True).then_inc(glog_ready, 1)

                def moe_gate(c):
                    dve.wait_ge(gexp_done, c + 1)
                    V.reciprocal(gsum[:], gsum[:])
                    dve.drain()
                    V.tensor_scalar(gsum[:], gsum[:], tg[:, 1:2], None, ALU.mult)
                    dve.drain()
                    V.tensor_tensor(gate[:], gate[:], gsum[:].unsqueeze(2).to_broadcast([P, NT, E]), ALU.mult)
                    dve.drain()

                def moe_experts(c, j):
                    t, u = j // 4, j % 4
                    ps, full, free, turn = moe.at(f"we{j}", c)
                    dve.wait_ge(full, turn)
                    for w in range(2):
                        e = 2 * u + w
                        last = V.scalar_tensor_tensor(out=acc[:, t], in0=ps[:, w * D:(w + 1) * D], scalar=gate[:, t, e:e + 1], in1=acc[:, t],
                                                      op0=ALU.mult, op1=ALU.add)
                        if w == 0:
                            dve.drain()
                    last.then_inc(free, 1)
                    if j == E - 1:
                        dve.drain().then_inc(x2_ready, 1)
                    elif j == E // 2 - 1:
                        pass
                    else:
                        dve.drain()

                def attn_max(a, j):
                    ps, full, free, turn = score.at(f"s{j}", a)
                    wait_apart(dve, dve_passed, full, turn)
                    for t, lo, hi in ((1, 0, S), (0, S, CAUSAL)):
                        last = V.tensor_tensor_reduce(out=probs[:, j % 4, lo:hi], in0=ps[:, lo:hi], in1=mbias[:, lo:hi], scale=-HD0 ** -0.5,
                                                      scalar=3e38, op0=ALU.add, op1=ALU.min, accum_out=negmax[:, j, t:t + 1])
                    last.then_inc(free, 1)

                def attn_sum(a, j):
                    dve.wait_ge(exp_done, H * a + j + 1)
                    V.reciprocal(rinv[:, j], rsum[:, j]).then_inc(rinv_ready, 1)

                def attn_final(a):
                    ps, full, free, turn = attn.at("out", a)
                    dve.wait_ge(full, turn)
                    V.tensor_tensor(ytmp[:], ps[:].rearrange("p (t n) -> p t n", t=NT), bo[:].unsqueeze(1).to_broadcast([P, NT, D]),
                                    ALU.add).then_inc(free, 1)
                    dve.drain()
                    dve.wait_ge(xres_in, 16 * (a + 1))
                    V.scalar_tensor_tensor(out=x1[:], in0=ytmp[:], scalar=tg[:, 0:1], in1=x1[:], op0=ALU.mult,
                                           op1=ALU.add).then_inc(x1_ready, 1)

                def beside_head(b, c, nxt, s):
                    if s == 0 and b is not None:
                        mix_rms(b)
                    if s == 1:
                        if c is not None:
                            moe_squares(c)
                        if b is not None:
                            V.tensor_copy(x1res[:], x1[:]).then_inc(x1_copied, 1)
                    if b is not None and s in mix_at:
                        use = mix_at[s]
                        if use == "hT":
                            low(mix, "hT", b, hT, hT_hi, gamma1)
                        elif use == "q":
                            mix_queries(b)
                        elif use == "down":
                            mix_down(b)
                        else:
                            mix_kv(b, int(use[2:]))
                    if c is not None:
                        if s == 2:
                            moe_normalise(c)
                        elif s == 4:
                            low(moe, "h2T", c, h2T, h2T_hi, gamma2)
                        elif s in (5, 6):
                            moe_gate_logits(c, s - 5)
                        elif s in expert_at:
                            if expert_at[s] == 0:
                                moe_gate(c)
                            moe_experts(c, expert_at[s])
                    if nxt is not None:
                        if s == 3:
                            pre_variance(nxt)
                        elif s == 7:
                            pre_normalise(nxt)
                        elif ahead_at.get(s) == "xT":
                            low(attn, "xT", nxt, xT, xT_hi)
                    if b is not None:
                        if s in score_at:
                            mix_scores(b, score_at[s] // 2, score_at[s] % 2)
                            if score_at[s] == 3:
                                mix_softmax_max(b)
                        elif s == 13:
                            mix_softmax_divide(b)
                            mix_weigh(0)
                        elif s == 14:
                            dve.drain()
                            mix_gather(1, 0, 0)
                        elif s == 15:
                            mix_gather_ready(b, 0)
                            mix_gather(0, 0, 1).then_inc(gathered, 1)
                        elif s == 16:
                            dve.drain()
                            mix_weigh(1)
                        elif s == 17:
                            dve.drain()
                            mix_gather(1, 1, 0)
                        elif s == 19:
                            mix_gather_ready(b, 1)
                            mix_gather(0, 1, 1).then_inc(gathered, 1)

                def mix_gather_ready(b, u):
                    dve.wait_ge(prod_ready, 6 * b + 4 + u + 1)

                def body(a, b, c, nxt):
                    if c is not None:
                        low(moe, "oT", c, foT, foT_hi)
                    if b is not None:
                        dve.drain()
                        variance(x1, statB, mvB, varB, varB_ready)
                    if c is not None:
                        moe_residual(c)
                    if b is not None:
                        mix_normalise(b)
                    if a is not None:
                        dve.wait_ge(mask_ready, a + 1)
                    for s in range(STEPS):
                        if a is not None:
                            if s < H:
                                attn_max(a, s)
                            if 1 <= s < H + 1:
                                attn_sum(a, s - 1)
                        beside_head(b, c, nxt, s)
                    if a is not None:
                        attn_final(a)

                for k, (src, hi, lo, rows) in enumerate(splits):
                    dve.wait_ge(split_hi, k + 1)
                    V.tensor_sub(lo, stage[0:rows, k % 2, 0:src.shape[1]], hi.bitcast(F32)).then_inc(split_lo, 1)
                dve.wait_ge(params_in, 16 * len(params))
                dve.wait_ge(tanh_done, 1)
                pre_variance(0)
                pre_normalise(0)
                low(attn, "xT", 0, xT, xT_hi)
                body(0, None, None, 1)
                body(1, 0, None, 2)
                body(2, 1, 0, 3)
                with dve.Fori(3, B - 1) as a:
                    body(a, a - 1, a - 2, a + 1)
                body(B - 1, B - 2, B - 3, None)
                body(None, B - 1, B - 2, None)
                body(None, None, B - 1, None)

            @block.tensor
            def _(pe):
                T = nc.tensor

                def transpose4(banks, use, batch, src):
                    ps, full, free, turn = banks.at(use, batch)
                    pe.wait_ge(free, turn)
                    for c in range(ND):
                        for t in range(NT):
                            last = T.transpose(ps[:, c * S + t * P:c * S + (t + 1) * P], src[:, t, c * P:(c + 1) * P], ident[:])
                    last.then_inc(full, 1)

                def features(use, a, w, x):
                    j = int(use[1:])
                    ps, full, free, turn = attn.at(use, a)
                    pe.wait_ge(free, turn)
                    for u in range(2):
                        m = slice((2 * j + u) * P, (2 * j + u + 1) * P)
                        last = product3(nc, ps[:, u * S:(u + 1) * S],
                                        [(w[0][:, c, m], w[1][:, c, m], x[0][:, c, :], x[1][:, c, :]) for c in range(ND)])
                    last.then_inc(full, 1)

                def values(j, a):
                    t, m = j // 2, slice((j % 2) * 512, (j % 2 + 1) * 512)
                    ps, full, free, turn = attn.at(f"v{j}", a)
                    pe.wait_ge(free, turn)
                    product3(nc, ps[:], [(cT[0][:, c, t * P:(t + 1) * P], cT[1][:, c, t * P:(t + 1) * P], wv[0][:, c, m], wv[1][:, c, m])
                                         for c in range(ND)]).then_inc(full, 1)

                def tokens(banks, use, b, x, w, cols):
                    ps, full, free, turn = banks.at(use, b)
                    pe.wait_ge(free, turn)
                    for t in range(NT):
                        last = product3(nc, ps[:, t * cols:(t + 1) * cols],
                                        [(x[0][:, c, t * P:(t + 1) * P], x[1][:, c, t * P:(t + 1) * P], w[0][:, c, :], w[1][:, c, :])
                                         for c in range(ND)])
                    last.then_inc(full, 1)

                def mix_down(b):
                    ps, full, free, turn = mix.at("down", b)
                    pe.wait_ge(free, turn)
                    product3(nc, ps[0:LAT, 0:S], [(fdown[0][:, c, :], fdown[1][:, c, :], hT[0][:, c, :], hT[1][:, c, :])
                                                  for c in range(ND)]).then_inc(full, 1)

                def mix_up(b, t):
                    if t == 0:
                        mix.emptied(pe, "down", b)
                    ps, full, free, turn = mix.at(f"up{t}", b)
                    pe.wait_ge(free, turn)
                    product3(nc, ps[:], [(dT[0][:, t * P:(t + 1) * P], dT[1][:, t * P:(t + 1) * P], fup[0][:], fup[1][:])]).then_inc(full, 1)

                def moe_gate(c, t):
                    if t == 0:
                        moe.emptied(pe, "h2T", c)
                    ps, full, free, turn = moe.at(f"gate{t}", c)
                    pe.wait_ge(free, turn)
                    product3(nc, ps[:, 0:E], [(h2T[0][:, k, t * P:(t + 1) * P], h2T[1][:, k, t * P:(t + 1) * P],
                                               wg[0][:, k, :], wg[1][:, k, :]) for k in range(ND)]).then_inc(full, 1)

                def moe_experts(c, j):
                    t, u = j // 4, j % 4
                    ps, full, free, turn = moe.at(f"we{j}", c)
                    pe.wait_ge(free, turn)
                    product3(nc, ps[:], [(h2T[0][:, k, t * P:(t + 1) * P], h2T[1][:, k, t * P:(t + 1) * P],
                                          we[0][:, k, u * 512:(u + 1) * 512], we[1][:, k, u * 512:(u + 1) * 512])
                                         for k in range(ND)]).then_inc(full, 1)

                def head_scores(a, j):
                    c, r = j // HPC, slice((j % HPC) * HD0, (j % HPC + 1) * HD0)
                    ps, full, free, turn = score.at(f"s{j}", a)
                    pe.wait_ge(free, turn)
                    T.matmul(ps[:, 0:S], qT[r, c, P:S], kT[r, c, :], start=True, stop=True)
                    T.matmul(ps[:, S:CAUSAL], qT[r, c, 0:P], kT[r, c, 0:P], start=True, stop=True).then_inc(full, 1)

                def head_transpose(a, j):
                    ps, full, free, turn = attn.at(f"T{j}", a)
                    pe.wait_ge(free, turn)
                    pe.wait_ge(norm_done, H * a + j + 1)
                    T.transpose(ps[:, 0:P], probs[:, j % 4, S:CAUSAL], ident[:])
                    T.transpose(ps[:, P:S], probs[:, j % 4, 0:P], ident[:])
                    T.transpose(ps[:, S:CAUSAL], probs[:, j % 4, P:S], ident[:]).then_inc(full, 1)

                def head_values(a, j):
                    g, u, r = j // 4, (j // HPC) % 2, slice((j % HPC) * HD0, (j % HPC + 1) * HD0)
                    ps, full, free, turn = heads.at(f"o{g}", a)
                    if j % 4 == 0:
                        pe.wait_ge(free, turn)
                    attn.emptied(pe, f"T{j}", a)
                    m = slice(j * HD0, (j + 1) * HD0)
                    T.matmul(ps[r, u * S:(u + 1) * S], v[:, 0, m], probsT[:, j % 2, 0:S], start=True, stop=False)
                    last = T.matmul(ps[r, u * S + P:(u + 1) * S], v[:, 1, m], probsT[:, j % 2, S:CAUSAL], start=False, stop=True)
                    last.then_inc(pv_done, 1)

                def attn_out(a):
                    ps, full, free, turn = attn.at("out", a)
                    pe.wait_ge(free, turn)
                    for t in range(NT):
                        for c in range(NC0):
                            last = T.matmul(ps[:, t * D:(t + 1) * D], oT[:, c, t * P:(t + 1) * P], wo[:, c, :], start=c == 0, stop=c == NC0 - 1)
                    last.then_inc(full, 1)

                def project(use, a):
                    if use == "xT":
                        pe.wait_ge(xn_ready, a + 1)
                        transpose4(attn, "xT", a, xn)
                    elif use[0] == "q":
                        features(use, a, wq, xT)
                    elif use[0] == "k":
                        if use == "k0":
                            pe.wait_ge(ctx_ready, a + 1)
                        features(use, a, wk, cT)
                    else:
                        values(int(use[1:]), a)

                def beside_head(b, c, s):
                    if b is not None and s in mix_at:
                        use = mix_at[s]
                        if use == "hT":
                            pe.wait_ge(h_ready, b + 1)
                            transpose4(mix, "hT", b, h)
                        elif use == "q":
                            mix.emptied(pe, "hT", b)
                            tokens(mix, "q", b, hT, fq, D)
                        elif use == "down":
                            mix_down(b)
                        else:
                            mix_up(b, int(use[2:]))
                    if c is not None:
                        if s == 4:
                            pe.wait_ge(h2_ready, c + 1)
                            transpose4(moe, "h2T", c, y)
                        elif s in (5, 6):
                            moe_gate(c, s - 5)
                        elif s in expert_at:
                            moe_experts(c, expert_at[s])

                def body(a, b, c, nxt):
                    if c is not None:
                        pe.wait_ge(gathered, 2 * (c + 1))
                        transpose4(moe, "oT", c, o)
                    if a is not None:
                        attn.emptied(pe, "xT", a)
                        project("q0", a)
                        project("q1", a)
                    if c is not None:
                        moe.emptied(pe, "oT", c)
                        tokens(moe, "out", c, foT, fo, D)
                    if a is not None:
                        attn.emptied(pe, "v2", a)
                        attn.emptied(pe, "q0", a)
                    for s in range(STEPS):
                        if a is not None and s < H:
                            if s % 4 == 0 and s > 0:
                                attn.emptied(pe, f"q{s // 4}", a)
                            if s == 12:
                                attn.emptied(pe, "k3", a)
                            head_scores(a, s)
                        beside_head(b, c, s)
                        if a is not None:
                            if LAG_T <= s < H + LAG_T:
                                head_transpose(a, s - LAG_T)
                            if s >= LAG_V:
                                if s - LAG_V == 8:
                                    attn.emptied(pe, "v1", a)
                                    attn.emptied(pe, "v3", a)
                                head_values(a, s - LAG_V)
                            if s in own_at:
                                project(own_at[s], a)
                        if nxt is not None and s in ahead_at:
                            project(ahead_at[s], nxt)
                    if a is not None:
                        heads.emptied(pe, "o2", a)
                        heads.emptied(pe, "o3", a)
                        attn_out(a)

                pe.wait_ge(consts, 1)
                pe.wait_ge(params_in, 16 * len(params))
                pe.wait_ge(split_lo, NS)
                for use in attn.ahead:
                    project(use, 0)
                body(0, None, None, 1)
                body(1, 0, None, 2)
                body(2, 1, 0, 3)
                with pe.Fori(3, B - 1) as a:
                    body(a, a - 1, a - 2, a + 1)
                body(B - 1, B - 2, B - 3, None)
                body(None, B - 1, B - 2, None)
                body(None, None, B - 1, None)


def layer1(nc, ins, x2, out):
    with ExitStack() as ctx:
        def sb(name, shape, dtype=F32):
            return ctx.enter_context(nc.sbuf_tensor("l1_" + name, shape, dtype))

        def sem(name):
            return ctx.enter_context(nc.semaphore("l1_" + name))

        def pair(name, shape):
            return sb(name + "_hi", shape, F32R), sb(name + "_lo", shape, F32R)

        wq, wk, wv = pair("wq", [P, ND, NC1 * P]), pair("wk", [P, ND, NC1 * P]), pair("wv", [P, ND, D])
        w1 = pair("w1", [P, ND, 3 * HID])
        wo, w2 = sb("wo", [P, NC1, D]), sb("w2", [P, 3 * NHC, D])
        bq, bk, b1 = sb("bq", [P, NC1]), sb("bk", [P, NC1]), sb("b1", [P, 3 * NHC])
        bv, bo, b2, b2sum = sb("bv", [P, D]), sb("bo", [P, D]), sb("b2", [P, 3, D]), sb("b2sum", [P, D])
        gw, gates, tg = sb("gw", [P, 2, D]), sb("gates", [P, 4]), sb("tg", [P, 4])
        ident, neghalf = sb("ident", [P, P]), sb("neghalf", [P, NT])
        again = sb("again", [P, 1])

        xin, ctxin, xn = sb("xin", [P, NT, D]), sb("ctxin", [P, ND, S]), sb("xn", [P, NT, D])
        statC, mvC, varC, rstdC = sb("statC", [P, NT, 6]), sb("mvC", [P, NT, 2]), sb("varC", [P, NT]), sb("rstdC", [P, NT])
        xT, cT, k = pair("xT", [P, ND, S]), pair("cT", [P, ND, S]), pair("k", [P, NC1, S])
        qfull, qhi, q = sb("qfull", [P, NC1, S]), sb("qhi", [P, NC1, S], F32R), sb("q", [P, NC1, S], F32R)
        v = sb("v", [P, NT, H, SLOT])
        probs, probsT = sb("probs", [P, 4, NT * S]), sb("probsT", [P, 2, NT * S])
        negmax, rsum, rinv = sb("negmax", [P, H, NT]), sb("rsum", [P, H, NT]), sb("rinv", [P, H, NT])
        oT, x3, ytmp = sb("oT", [P, NC1, S]), sb("x3", [P, NT, D]), sb("ytmp", [P, NT, D])

        x3res, xf, x0 = sb("x3res", [P, NT, D]), sb("xf", [P, NT, D]), sb("x0", [P, NT, D])
        statF, mvF, varF, rstdF = sb("statF", [P, NT, 6]), sb("mvF", [P, NT, 2]), sb("varF", [P, NT]), sb("rstdF", [P, NT])
        gscore, first_wins = sb("gscore", [P, NT, 2]), sb("first_wins", [P, NT])
        xfT, x0T, x1T = pair("xfT", [P, ND, S]), pair("x0T", [P, ND, S]), pair("x1T", [P, ND, S])
        hid = sb("hid", [P, 3 * NHC, S])
        stage = hid[:].rearrange("p (a c) n -> p a (c n)", a=2)
        x4 = sb("x4", [P, NT, D])

        attn = Banks(nc, ctx, "l1_attn", ["xT", "k0", "k1", "v0", "v1", "q0", "q1"] + [f"T{j}" for j in range(H)] + ["out"])
        score = Banks(nc, ctx, "l1_score", [f"s{j}" for j in range(H)])
        heads = Banks(nc, ctx, "l1_heads", ["o0", "o1"])
        ffn = Banks(nc, ctx, "l1_ffn", ["xfT", "x0T"] + [f"h{j}" for j in range(12)] + ["y0", "y1"])

        raw_in, split_hi, split_lo = [sem("raw_in0"), sem("raw_in1")], sem("split_hi"), sem("split_lo")
        pool_passed, dve_passed, sp_passed = sem("pool_passed"), sem("dve_passed"), sem("sp_passed")
        params_in, consts, tanh_done, bias_ready = sem("params_in"), sem("consts"), sem("tanh_done"), sem("bias_ready")
        x_in, ctx_in, xres_in, x4_stored = sem("x_in"), sem("ctx_in"), sem("xres_in"), sem("x4_stored")
        varC_ready, rstdC_ready, xn_ready, ctx_ready = sem("varC_ready"), sem("rstdC_ready"), sem("xn_ready"), sem("ctx_ready")
        xT_hi, k_hi, q_hi, max_ready = sem("xT_hi"), sem("k_hi"), sem("q_hi"), sem("max_ready")
        exp_done, rinv_ready, norm_done, pv_done = sem("exp_done"), sem("rinv_ready"), sem("norm_done"), sem("pv_done")
        x3_ready, x3_copied, varF_ready, rstdF_ready = sem("x3_ready"), sem("x3_copied"), sem("varF_ready"), sem("rstdF_ready")
        xf_ready, xfT_hi, x0T_hi, x1T_ready, x4_ready = sem("xf_ready"), sem("xfT_hi"), sem("x0T_hi"), sem("x1T_ready"), sem("x4_ready")

        def flat(t):
            return t[:].rearrange("p c n -> p (c n)")
        splits = [(ins["wk1"], flat(wk[0]), flat(wk[1])), (ins["wv1"], flat(wv[0]), flat(wv[1])), (ins["wq1"], flat(wq[0]), flat(wq[1])),
                  (ins["w1"][:, 0, :], w1[0][:, 0, :], w1[1][:, 0, :]), (ins["w1"][:, 1, :], w1[0][:, 1, :], w1[1][:, 1, :])]
        NS = len(splits)
        params = [(flat(wo), ins["wo1"]), (bq[:], ins["bq1"]), (bk[:], ins["bk1"]), (b1[:], ins["b1"]),
                  (bv[:], ins["bv1"].to_broadcast([P, D])), (bo[:], ins["bo1"].to_broadcast([P, D])),
                  (flat(b2), ins["b2"].to_broadcast([P, 3 * D])), (flat(gw), ins["gw"].to_broadcast([P, 2 * D])),
                  (gates[:], ins["gates"].to_broadcast([P, 4])), (again[:], ins["again"]), (flat(w2), ins["w2"])]

        with nc.Block() as block:

            @block.sync
            def _(sp):
                def load(b):
                    if not first(b):
                        sp.wait_ge(xn_ready, b)
                    sp.dma_start(xin[:], x2[bass.ds(b, 1)][0]).then_inc(x_in, 16)
                    if not first(b):
                        sp.wait_ge(ctx_ready, b)
                    sp.dma_start(ctxin[:], ins["ctx"][bass.ds(b, 1)][0]).then_inc(ctx_in, 16)

                def load_residual(b):
                    if not first(b):
                        sp.wait_ge(x3_copied, b)
                        sp.wait_ge(xf_ready, b)
                    sp.dma_start(x3[:], x2[bass.ds(b, 1)][0]).then_inc(xres_in, 16)

                def store(b):
                    sp.wait_ge(x4_ready, b + 1)
                    sp.dma_start(out[bass.ds(b, 1)][0], x4[:]).then_inc(x4_stored, 16)

                load(0)
                load_residual(0)
                for n, (src, _hi, _lo) in enumerate(splits):
                    if n >= 2:
                        sp.wait_ge(split_lo, n - 1)
                    sp.dma_start(stage[:, n % 2, 0:src.shape[1]], src).then_inc(raw_in[n % 2], 16)
                    if n == 1:
                        for dst, src in params:
                            sp.dma_start(dst, src).then_inc(params_in, 16)
                load(1)
                load_residual(1)
                with sp.Fori(2, B) as b:
                    load(b)
                    store(b - 2)
                    load_residual(b)
                store(B - 2)
                store(B - 1)
                sp.wait_ge(x4_stored, 16 * B)

            @block.gpsimd
            def _(pool):
                nc.gpsimd.memset(ident[:], 0.0)
                nc.gpsimd.memset(neghalf[:], -0.5)
                nc.gpsimd.memset(v[:], 0.0)
                pool.drain()
                nc.gpsimd.affine_select(out=ident[:], in_=ident[:], compare_op=ALU.not_equal, fill=1.0, base=0,
                                        pattern=[[-1, P]], channel_multiplier=1).then_inc(consts, 1)

                def power(ready, done, src, dst, b):
                    pool.wait_ge(ready, b + 1)
                    nc.gpsimd.tensor_tensor(dst[:], src[:], neghalf[:], ALU.pow).then_inc(done, 1)

                def split_context(a):
                    if not first(a):
                        _, full, _, turn = attn.at("v1", a - 1)
                        pool.wait_ge(full, turn)
                    wait_apart(pool, pool_passed, ctx_in, 16 * (a + 1))
                    nc.gpsimd.tensor_copy(cT[0][:], ctxin[:])
                    pool.drain()
                    nc.gpsimd.tensor_sub(cT[1][:], ctxin[:], cT[0][:].bitcast(F32)).then_inc(ctx_ready, 1)

                def normalise(a, j):
                    wait_apart(pool, pool_passed, rinv_ready, H * a + j + 1)
                    for t in range(NT):
                        last = nc.gpsimd.tensor_scalar(probs[:, j % 4, t * S:(t + 1) * S], probs[:, j % 4, t * S:(t + 1) * S],
                                                       rinv[:, j, t:t + 1], 1.0, ALU.mult, ALU.mult)
                    last.then_inc(norm_done, 1)

                def copy_residual(b):
                    if not first(b):
                        pool.wait_ge(x4_ready, b)
                    wait_apart(pool, pool_passed, x3_ready, b + 1)
                    nc.gpsimd.tensor_copy(x3res[:], x3[:]).then_inc(x3_copied, 1)

                def other_tokens(b):
                    ffn.emptied(pool, "xfT", b)
                    ffn.emptied(pool, "x0T", b)
                    for part in range(2):
                        last = nc.gpsimd.tensor_sub(x1T[part][:], xfT[part][:].bitcast(F32), x0T[part][:].bitcast(F32))
                    last.then_inc(x1T_ready, 1)

                def body(a, b, nxt):
                    if b is not None:
                        power(varF_ready, rstdF_ready, varF, rstdF, b)
                        copy_residual(b)
                        other_tokens(b)
                    for j in range(H):
                        if a is not None:
                            normalise(a, j)
                        if nxt is not None and j == 6:
                            split_context(nxt)
                        if nxt is not None and j == 10:
                            power(varC_ready, rstdC_ready, varC, rstdC, nxt)

                split_context(0)
                power(varC_ready, rstdC_ready, varC, rstdC, 0)
                body(0, None, 1)
                body(1, 0, 2)
                with pool.Fori(2, B - 1) as a:
                    body(a, a - 1, a + 1)
                body(B - 1, B - 2, None)
                body(None, B - 1, None)

            @block.scalar
            def _(act):
                nc.scalar.preload_act_table(ACT.Exp)
                for n, (src, hi, _lo) in enumerate(splits):
                    act.wait_ge(raw_in[n % 2], 16 * (n // 2 + 1))
                    nc.scalar.copy(hi, stage[:, n % 2, 0:src.shape[1]]).then_inc(split_hi, 1)
                act.wait_ge(params_in, 16 * len(params))
                nc.scalar.activation(tg[:], gates[:], ACT.Tanh).then_inc(tanh_done, 1)
                act.wait_ge(bias_ready, 1)

                def high(banks, use, batch, dst, ready):
                    ps, full, _, turn = banks.at(use, batch)
                    act.wait_ge(full, turn)
                    nc.scalar.copy(flat(dst), ps[:]).then_inc(ready, 1)

                def keys_queries(a):
                    for name in ("k", "q"):
                        for j in range(2):
                            ps, full, _, turn = attn.at(f"{name}{j}", a)
                            act.wait_ge(full, turn)
                            for u in range(2):
                                c, src = 2 * j + u, ps[:, u * S:(u + 1) * S]
                                if name == "k":
                                    last = nc.scalar.activation(k[0][:, c, :], src, ACT.Identity, bias=bk[:, c:c + 1])
                                else:
                                    nc.scalar.activation(qfull[:, c, :], src, ACT.Identity, bias=bq[:, c:c + 1], scale=HD ** -0.5)
                                    last = nc.scalar.activation(qhi[:, c, :], src, ACT.Identity, bias=bq[:, c:c + 1], scale=HD ** -0.5)
                            last.then_inc(k_hi if name == "k" else q_hi, 1)

                def hidden(b, j):
                    ps, full, free, turn = ffn.at(f"h{j}", b)
                    act.wait_ge(full, turn)
                    for u in range(2):
                        c = 2 * j + u
                        last = nc.scalar.activation(hid[:, c, :], ps[:, u * S:(u + 1) * S], ACT.Relu, bias=b1[:, c:c + 1])
                    last.then_inc(free, 1)

                def body(a, b, nxt):
                    if b is not None:
                        high(ffn, "xfT", b, xfT[0], xfT_hi)
                        high(ffn, "x0T", b, x0T[0], x0T_hi)
                    if a is not None:
                        high(attn, "xT", a, xT[0], xT_hi)
                        keys_queries(a)
                    for s in range(H + 3):
                        if b is not None and 1 <= s <= 12:
                            hidden(b, s - 1)
                        if a is not None and s < H:
                            ps, _, free, _ = score.at(f"s{s}", a)
                            act.wait_ge(max_ready, H * a + s + 1)
                            for t in range(NT):
                                last = nc.scalar.activation(probs[:, s % 4, t * S:(t + 1) * S], ps[:, t * S:(t + 1) * S], ACT.Exp,
                                                            bias=negmax[:, s, t:t + 1], accum_out=rsum[:, s, t:t + 1])
                            last.then_inc(free, 1)
                        if a is not None and s in (10, 18):
                            g = (s - 10) // 8
                            ps, _, free, _ = heads.at(f"o{g}", a)
                            act.wait_ge(pv_done, H * a + 8 * g + 8)
                            nc.scalar.copy(oT[:, 2 * g:2 * g + 2, :].rearrange("p c n -> p (c n)"), ps[:]).then_inc(free, 1)

                body(0, None, 1)
                body(1, 0, 2)
                with act.Fori(2, B - 1) as a:
                    body(a, a - 1, a + 1)
                body(B - 1, B - 2, None)
                body(None, B - 1, None)

            @block.vector
            def _(dve):
                for banks in (attn, score, heads, ffn):
                    banks.open(dve)
                V = nc.vector

                def variance(src, stat, mv, var, ready):
                    for t in range(NT):
                        V.bn_stats(stat[:, t], src[:, t])
                    dve.drain()
                    for t in range(NT):
                        V.bn_aggr(mv[:, t], stat[:, t])
                    dve.drain()
                    V.tensor_scalar(var[:], mv[:, :, 1], LN_EPS, None, ALU.add).then_inc(ready, 1)

                def pre_variance(a):
                    dve.wait_ge(x_in, 16 * (a + 1))
                    variance(xin, statC, mvC, varC, varC_ready)

                def pre_normalise(a):
                    dve.wait_ge(rstdC_ready, a + 1)
                    for t in range(NT):
                        last = V.tensor_scalar(xn[:, t], xin[:, t], mvC[:, t, 0:1], rstdC[:, t:t + 1], ALU.subtract, ALU.mult)
                    last.then_inc(xn_ready, 1)

                def low(banks, use, batch, dst, hi_ready):
                    ps, _, free, _ = banks.at(use, batch)
                    dve.wait_ge(hi_ready, batch + 1)
                    V.tensor_sub(flat(dst[1]), ps[:], flat(dst[0]).bitcast(F32)).then_inc(free, 1)

                def ffn_norm(b):
                    dve.drain()
                    variance(x3, statF, mvF, varF, varF_ready)
                    dve.wait_ge(rstdF_ready, b + 1)
                    for t in range(NT):
                        V.tensor_scalar(xf[:, t], x3[:, t], mvF[:, t, 0:1], rstdF[:, t:t + 1], ALU.subtract, ALU.mult)
                    dve.drain()
                    for t in range(NT):
                        for e in range(2):
                            V.tensor_tensor_reduce(out=(ytmp, x0)[t][:, e], in0=xf[:, t], in1=gw[:, e], scale=1.0, scalar=0.0,
                                                   op0=ALU.mult, op1=ALU.add, accum_out=gscore[:, t, e:e + 1])
                    dve.drain()
                    V.tensor_tensor(first_wins[:], gscore[:, :, 0], gscore[:, :, 1], ALU.is_ge)
                    dve.drain()
                    for t in range(NT):
                        last = V.tensor_scalar(x0[:, t], xf[:, t], first_wins[:, t:t + 1], None, ALU.mult)
                    last.then_inc(xf_ready, 1)

                def keys(a, j):
                    ps, _, free, _ = attn.at(f"k{j}", a)
                    dve.wait_ge(k_hi, 2 * a + j + 1)
                    for u in range(2):
                        c = 2 * j + u
                        last = V.scalar_tensor_tensor(out=k[1][:, c, :], in0=ps[:, u * S:(u + 1) * S], scalar=bk[:, c:c + 1],
                                                      in1=k[0][:, c, :].bitcast(F32), op0=ALU.add, op1=ALU.subtract)
                    last.then_inc(free, 1)

                def values(a, t):
                    ps, full, free, turn = attn.at(f"v{t}", a)
                    dve.wait_ge(full, turn)
                    V.tensor_tensor(v[:, t, :, 0:HD], ps[:, 0:D].rearrange("p (h d) -> p h d", d=HD),
                                    bv[:].rearrange("p (h d) -> p h d", d=HD), ALU.add).then_inc(free, 1)

                def queries(a, j):
                    _, _, free, _ = attn.at(f"q{j}", a)
                    dve.wait_ge(q_hi, 2 * a + j + 1)
                    V.scalar_tensor_tensor(out=q[:, 2 * j:2 * j + 2, :], in0=qhi[:, 2 * j:2 * j + 2, :].bitcast(F32), scalar=again[:],
                                           in1=qfull[:, 2 * j:2 * j + 2, :], op0=ALU.mult, op1=ALU.add).then_inc(free, 1)

                def attn_max(a, j):
                    ps, full, _, turn = score.at(f"s{j}", a)
                    dve.wait_ge(full, turn)
                    V.tensor_reduce(negmax[:, j], ps[:].rearrange("p (t k) -> p t k", t=NT), axis=AX.X, op=ALU.max,
                                    negate=True).then_inc(max_ready, 1)

                def attn_sum(a, j):
                    score.emptied(dve, f"s{j}", a)
                    V.reciprocal(rinv[:, j], rsum[:, j]).then_inc(rinv_ready, 1)

                def attn_copy(a, j):
                    ps, full, free, turn = attn.at(f"T{j}", a)
                    dve.wait_ge(full, turn)
                    if j >= 2:
                        dve.wait_ge(pv_done, H * a + j - 1)
                    V.tensor_copy(probsT[:, j % 2, :], ps[:]).then_inc(free, 1)

                def attn_final(a):
                    ps, full, free, turn = attn.at("out", a)
                    dve.wait_ge(full, turn)
                    V.tensor_tensor(ytmp[:], ps[:].rearrange("p (t n) -> p t n", t=NT), bo[:].unsqueeze(1).to_broadcast([P, NT, D]),
                                    ALU.add).then_inc(free, 1)
                    dve.drain()
                    dve.wait_ge(xres_in, 16 * (a + 1))
                    V.scalar_tensor_tensor(out=x3[:], in0=ytmp[:], scalar=tg[:, 2:3], in1=x3[:], op0=ALU.mult,
                                           op1=ALU.add).then_inc(x3_ready, 1)

                def ffn_final(b):
                    if not first(b):
                        dve.wait_ge(x4_stored, 16 * b)
                    for t in range(NT):
                        ps, full, free, turn = ffn.at(f"y{t}", b)
                        dve.wait_ge(full, turn)
                        V.tensor_tensor(x4[:, t], ps[:, 0:D], b2sum[:], ALU.add).then_inc(free, 1)
                    dve.drain()
                    dve.wait_ge(x3_copied, b + 1)
                    V.scalar_tensor_tensor(out=x4[:], in0=x4[:], scalar=tg[:, 3:4], in1=x3res[:], op0=ALU.mult,
                                           op1=ALU.add).then_inc(x4_ready, 1)

                def body(a, b, nxt):
                    if b is not None:
                        ffn_norm(b)
                        low(ffn, "xfT", b, xfT, xfT_hi)
                        low(ffn, "x0T", b, x0T, x0T_hi)
                    if a is not None:
                        low(attn, "xT", a, xT, xT_hi)
                        keys(a, 0)
                        keys(a, 1)
                        values(a, 0)
                        values(a, 1)
                        queries(a, 0)
                        queries(a, 1)
                    for s in range(H + 2):
                        if a is not None:
                            if s < H:
                                attn_max(a, s)
                            if 1 <= s < H + 1:
                                attn_sum(a, s - 1)
                            if s >= 2:
                                attn_copy(a, s - 2)
                        if nxt is not None and s == 9:
                            pre_variance(nxt)
                        if nxt is not None and s == 13:
                            pre_normalise(nxt)
                    if a is not None:
                        attn_final(a)
                    if b is not None:
                        ffn_final(b)

                for n, (src, hi, lo) in enumerate(splits):
                    dve.wait_ge(split_hi, n + 1)
                    V.tensor_sub(lo, stage[:, n % 2, 0:src.shape[1]], hi.bitcast(F32)).then_inc(split_lo, 1)
                dve.wait_ge(params_in, 16 * len(params))
                V.tensor_scalar(bq[:], bq[:], HD ** -0.5, None, ALU.mult).then_inc(bias_ready, 1)
                V.tensor_tensor(b2sum[:], b2[:, 1], b2[:, 2], ALU.add)
                dve.drain()
                V.tensor_tensor(b2sum[:], b2sum[:], b2[:, 0], ALU.add)
                dve.wait_ge(tanh_done, 1)
                dve.wait_ge(consts, 1)
                pre_variance(0)
                pre_normalise(0)
                body(0, None, 1)
                body(1, 0, 2)
                with dve.Fori(2, B - 1) as a:
                    body(a, a - 1, a + 1)
                body(B - 1, B - 2, None)
                body(None, B - 1, None)

            @block.tensor
            def _(pe):
                T = nc.tensor

                def transpose4(banks, use, batch, src):
                    ps, full, free, turn = banks.at(use, batch)
                    pe.wait_ge(free, turn)
                    for c in range(ND):
                        for t in range(NT):
                            last = T.transpose(ps[:, c * S + t * P:c * S + (t + 1) * P], src[:, t, c * P:(c + 1) * P], ident[:])
                    last.then_inc(full, 1)

                def features(banks, use, batch, w, x, chunk):
                    ps, full, free, turn = banks.at(use, batch)
                    pe.wait_ge(free, turn)
                    for u in range(2):
                        m = slice((chunk + u) * P, (chunk + u + 1) * P)
                        last = product3(nc, ps[:, u * S:(u + 1) * S],
                                        [(w[0][:, c, m], w[1][:, c, m], x[0][:, c, :], x[1][:, c, :]) for c in range(ND)])
                    last.then_inc(full, 1)

                def values(a, t):
                    ps, full, free, turn = attn.at(f"v{t}", a)
                    pe.wait_ge(free, turn)
                    m = slice(t * P, (t + 1) * P)
                    product3(nc, ps[:, 0:D], [(cT[0][:, c, m], cT[1][:, c, m], wv[0][:, c, :], wv[1][:, c, :])
                                              for c in range(ND)]).then_inc(full, 1)

                def head_scores(a, j):
                    c, r = j // HPC1, slice((j % HPC1) * SLOT, (j % HPC1 + 1) * SLOT)
                    ps, full, free, turn = score.at(f"s{j}", a)
                    pe.wait_ge(free, turn)
                    for t in range(NT):
                        for part in range(2):
                            last = T.matmul(ps[:, t * S:(t + 1) * S], q[r, c, t * P:(t + 1) * P], k[part][r, c, :], start=part == 0, stop=part == 1)
                    last.then_inc(full, 1)

                def head_transpose(a, j):
                    ps, full, free, turn = attn.at(f"T{j}", a)
                    pe.wait_ge(free, turn)
                    pe.wait_ge(norm_done, H * a + j + 1)
                    for kt in range(NT):
                        for t in range(NT):
                            last = T.transpose(ps[:, kt * S + t * P:kt * S + (t + 1) * P], probs[:, j % 4, t * S + kt * P:t * S + (kt + 1) * P], ident[:])
                    last.then_inc(full, 1)

                def head_values(a, j):
                    g, u, r = j // 8, (j // HPC1) % 2, slice((j % HPC1) * SLOT, (j % HPC1 + 1) * SLOT)
                    ps, _, free, turn = heads.at(f"o{g}", a)
                    if j % 8 == 0:
                        pe.wait_ge(free, turn)
                    attn.emptied(pe, f"T{j}", a)
                    for kt in range(NT):
                        last = T.matmul(ps[r, u * S:(u + 1) * S], v[:, kt, j, :], probsT[:, j % 2, kt * S:(kt + 1) * S], start=kt == 0, stop=kt == NT - 1)
                    last.then_inc(pv_done, 1)

                def attn_out(a):
                    ps, full, free, turn = attn.at("out", a)
                    heads.emptied(pe, "o0", a)
                    heads.emptied(pe, "o1", a)
                    pe.wait_ge(free, turn)
                    for t in range(NT):
                        for c in range(NC1):
                            last = T.matmul(ps[:, t * D:(t + 1) * D], oT[:, c, t * P:(t + 1) * P], wo[:, c, :], start=c == 0, stop=c == NC1 - 1)
                    last.then_inc(full, 1)

                def ffn_down(b, t, piece):
                    ps, full, free, turn = ffn.at(f"y{t}", b)
                    if piece == 0:
                        pe.wait_ge(free, turn)
                        ffn.emptied(pe, "h10", b)
                        ffn.emptied(pe, "h11", b)
                    n = 3 * NHC // 4
                    for c in range(piece * n, (piece + 1) * n):
                        last = T.matmul(ps[:, 0:D], hid[:, c, t * P:(t + 1) * P], w2[:, c, :], start=c == 0, stop=c == 3 * NHC - 1)
                    if piece == 3:
                        last.then_inc(full, 1)

                def body(a, b, nxt):
                    if b is not None:
                        pe.wait_ge(xf_ready, b + 1)
                        transpose4(ffn, "xfT", b, xf)
                        transpose4(ffn, "x0T", b, x0)
                    if a is not None:
                        pe.wait_ge(xn_ready, a + 1)
                        transpose4(attn, "xT", a, xn)
                        pe.wait_ge(ctx_ready, a + 1)
                        features(attn, "k0", a, wk, cT, 0)
                        features(attn, "k1", a, wk, cT, 2)
                        values(a, 0)
                        values(a, 1)
                        attn.emptied(pe, "xT", a)
                        features(attn, "q0", a, wq, xT, 0)
                        features(attn, "q1", a, wq, xT, 2)
                        attn.emptied(pe, "q0", a)
                        attn.emptied(pe, "q1", a)
                    for s in range(H + 3):
                        if a is not None:
                            if s < H:
                                head_scores(a, s)
                            if 2 <= s < H + 2:
                                head_transpose(a, s - 2)
                            if s >= 3:
                                head_values(a, s - 3)
                        if b is not None:
                            if s == 0:
                                ffn.emptied(pe, "xfT", b)
                                ffn.emptied(pe, "x0T", b)
                            if s == 8:
                                pe.wait_ge(x1T_ready, b + 1)
                            if s < 12:
                                features(ffn, f"h{s}", b, w1, (xfT, x0T, x1T)[s // 4], 2 * s)
                            if 14 <= s < 18:
                                ffn_down(b, 0, s - 14)
                    if a is not None:
                        attn_out(a)
                    if b is not None:
                        for piece in range(4):
                            ffn_down(b, 1, piece)

                pe.wait_ge(consts, 1)
                pe.wait_ge(params_in, 16 * len(params))
                pe.wait_ge(split_lo, NS)
                body(0, None, 1)
                body(1, 0, 2)
                with pe.Fori(2, B - 1) as a:
                    body(a, a - 1, a + 1)
                body(B - 1, B - 2, None)
                body(None, B - 1, None)



def chunked(w):
    c = w.shape[0] // P
    return w.reshape(c, P, w.shape[1]).transpose(1, 0, 2).reshape(P, c * w.shape[1])


def layouts(i):
    import numpy as np
    gates = np.stack([i["g_xattn"][0], i["g_ffn"][0], i["g_xattn"][1], i["g_ffn"][1]])[None]
    tiles = lambda x: x.reshape(B, NT, P, D).transpose(0, 2, 1, 3)
    w1 = np.concatenate([i["L1_ffn_sw1"][None], i["L1_ffn_w1"]])
    w2 = np.concatenate([i["L1_ffn_sw2"][None], i["L1_ffn_w2"]])
    b1 = np.concatenate([i["L1_ffn_sb1"][None], i["L1_ffn_b1"]])
    b2 = np.concatenate([i["L1_ffn_sb2"][None], i["L1_ffn_b2"]])
    again = np.zeros((P, 1), np.float32)
    again.reshape(HPC1, 2, HD)[:, 1] = -1.0

    def twice(w):
        w = w.reshape(*w.shape[:-1], H, 1, HD)
        return np.concatenate([w, w], axis=-2).reshape(*w.shape[:-3], NC1 * P)
    spread = np.zeros((H, SLOT, D), np.float32)
    spread[:, 0:HD] = i["L1_xattn_Wo"].T.reshape(H, HD, D)
    return {
        "wq1": chunked(twice(i["L1_xattn_Wq"].T)), "wk1": chunked(twice(i["L1_xattn_Wk"].T)), "wv1": chunked(i["L1_xattn_Wv"].T),
        "bq1": twice(i["L1_xattn_bq"]).reshape(NC1, P).T, "bk1": twice(i["L1_xattn_bk"]).reshape(NC1, P).T,
        "wo1": chunked(spread.reshape(H * SLOT, D)), "bv1": i["L1_xattn_bv"][None], "bo1": i["L1_xattn_bo"][None],
        "w1": w1.transpose(1, 0, 2).reshape(ND, P, 3 * HID).transpose(1, 0, 2), "b1": b1.reshape(3 * NHC, P).T,
        "w2": chunked(w2.reshape(3 * HID, D)), "b2": b2.reshape(1, 3 * D), "gw": i["L1_ffn_gate_w"].reshape(1, 2 * D),
        "again": again,
        "x": tiles(i["x"]),
        "ctx": i["ctx_1024"].transpose(0, 2, 1).reshape(B, ND, P, S).transpose(0, 2, 1, 3),
        "mask": i["mask_BxS2_bf1"],
        "gates": gates,
        "wq": chunked(i["L0_xattn_Wq"].T), "wk": chunked(i["L0_xattn_Wk"].T), "wv": chunked(i["L0_xattn_Wv"].T),
        "wo": chunked(i["L0_xattn_Wo"].T), "bo": i["L0_xattn_bo"][None],
        "fq": chunked(i["L0_ffn_Wq"]), "fdown": chunked(i["L0_ffn_Wdown"]), "fup": i["L0_ffn_Wup"], "fo": chunked(i["L0_ffn_Wo"]),
        "wg": chunked(i["L0_ffn_Wg"]),
        "we": i["L0_ffn_We"].transpose(1, 0, 2).reshape(ND, P, E * D).transpose(1, 0, 2),
        "bq": i["L0_ffn_bq"][None], "bup": i["L0_ffn_bup"][None], "bfo": i["L0_ffn_bo"][None], "bg": i["L0_ffn_bg"][None],
        "bdown": i["L0_ffn_bdown"][:, None],
        "gamma1": i["L0_ffn_gamma1"].reshape(ND, P).T, "gamma2": i["L0_ffn_gamma2"].reshape(ND, P).T,
    }


def kernel(**inputs):
    import numpy as np
    import concourse.bacc as bacc
    from concourse.bass_utils import run_bass_kernel_spmd

    nc = bacc.Bacc("TRN2", target_bir_lowering=False, num_devices=1)
    arrays = {f"in_{k}": np.ascontiguousarray(v) for k, v in layouts({k: np.asarray(v) for k, v in inputs.items()}).items()}
    ins = {k[3:]: nc.dram_tensor(k, v.shape, mybir.dt.from_np(v.dtype), kind="ExternalInput").ap() for k, v in arrays.items()}
    out = nc.dram_tensor("out", (B, P, NT, D), F32, kind="ExternalOutput").ap()
    x2 = nc.dram_tensor("x2", (B, P, NT, D), F32, kind="Internal").ap()
    layer0(nc, ins, x2)
    layer1(nc, ins, x2, out)
    got = run_bass_kernel_spmd(nc, [arrays], core_ids=[0]).results[0]["out"]
    return got.reshape(B, P, NT, D).transpose(0, 2, 1, 3).reshape(B, S, D)
```

```python
from contextlib import ExitStack

import concourse.bass as bass
from concourse import mybir
from concourse.alu_op_type import AluOpType as ALU

F32 = mybir.dt.float32
F32R = mybir.dt.float32r
U8 = mybir.dt.uint8
ACT = mybir.ActivationFunctionType
AX = mybir.AxisListType

B, S, D = 16, 256, 256
P = 128
NT = S // P
ND = D // P
H = 16
HD0 = 64
INNER = H * HD0
NC0 = INNER // P
HPC = P // HD0
HD = D // H
LAT = 64
E = 8
HID = 1024
NHC = HID // P
SLOT = 32
NC1 = H * SLOT // P
HPC1 = P // SLOT
LN_EPS = 1e-5
RMS_EPS = 1e-6
NEG = 1e30
CAUSAL = S + P
LAG_T, LAG_V = 3, 4
STEPS = H + LAG_V


class Banks:

    def __init__(self, nc, ctx, name, uses, count=2, ahead=()):
        assert len(uses) % count == 0
        self.uses, self.count, self.ahead = uses, count, list(ahead)
        self.bank = [ctx.enter_context(nc.psum_tensor(f"{name}{n}", [P, 512], F32)) for n in range(count)]
        self.full = [ctx.enter_context(nc.semaphore(f"{name}{n}_full")) for n in range(count)]
        self.free = [ctx.enter_context(nc.semaphore(f"{name}{n}_free")) for n in range(count)]

    def at(self, use, batch):
        uses = self.uses
        if use in self.ahead and first(batch):
            k = self.ahead.index(use)
        elif use in self.ahead:
            batch, k = batch - 1, len(self.ahead) + uses.index(use)
        else:
            if isinstance(batch, int) and batch == B - 1:
                uses = [u for u in uses if u not in self.ahead]
            k = len(self.ahead) + uses.index(use)
        turn = batch * (len(self.uses) // self.count) + k // self.count + 1
        n = k % self.count
        return self.bank[n], self.full[n], self.free[n], turn

    def emptied(self, engine, use, batch):
        _, _, free, turn = self.at(use, batch)
        engine.wait_ge(free, turn + 1)

    def open(self, engine):
        for f in self.free:
            engine.sem_inc(f, 1)


def first(batch):
    return isinstance(batch, int) and batch == 0


def wait_apart(engine, passed, sem, value):
    engine.wait_ge(sem, value)
    engine.sem_inc(passed, 1)


def product3(nc, out, terms):
    last = None
    for n, (wh, wl, xh, xl) in enumerate(terms):
        last = nc.tensor.matmul(out, wh, xh, start=n == 0, stop=False)
        last = nc.tensor.matmul(out, wh, xl, start=False, stop=False)
        last = nc.tensor.matmul(out, wl, xh, start=False, stop=n == len(terms) - 1)
    return last


def layer0(nc, ins, x2):
    with ExitStack() as ctx:
        def sb(name, shape, dtype=F32):
            return ctx.enter_context(nc.sbuf_tensor("l0_" + name, shape, dtype))

        def sem(name):
            return ctx.enter_context(nc.semaphore("l0_" + name))

        def pair(name, shape):
            return sb(name + "_hi", shape, F32R), sb(name + "_lo", shape, F32R)

        wq, wk, wv = pair("wq", [P, ND, INNER]), pair("wk", [P, ND, INNER]), pair("wv", [P, ND, INNER])
        fq, fdown, fup, fo = pair("fq", [P, ND, D]), pair("fdown", [P, ND, LAT]), pair("fup", [LAT, 2 * D]), pair("fo", [P, ND, D])
        wg, we = pair("wg", [P, ND, E]), pair("we", [P, ND, E * D])
        wo = sb("wo", [P, NC0, D])
        prod = sb("prod", [P, 2, H * D // 2])
        stage = prod
        bo, bq, bup, bfo, bg = sb("bo", [P, D]), sb("bq", [P, D]), sb("bup", [P, 2 * D]), sb("bfo", [P, D]), sb("bg", [P, E])
        bdown, gamma1, gamma2 = sb("bdown", [LAT, 1]), sb("gamma1", [P, ND]), sb("gamma2", [P, ND])
        gates, tg = sb("gates", [P, 4]), sb("tg", [P, 4])
        maskbits = sb("maskbits", [P, S], U8)
        ident, cmask, neghalf = sb("ident", [P, P]), sb("cmask", [P, CAUSAL]), sb("neghalf", [P, NT])

        xin, ctxin = sb("xin", [P, NT, D]), sb("ctxin", [P, ND, S])
        xn = sb("xn", [P, NT, D])
        statA, mvA, varA, rstdA = sb("statA", [P, NT, 6]), sb("mvA", [P, NT, 2]), sb("varA", [P, NT]), sb("rstdA", [P, NT])
        xT, cT = pair("xT", [P, ND, S]), pair("cT", [P, ND, S])
        qT, kT, v = sb("qT", [P, NC0, S]), sb("kT", [P, NC0, S]), sb("v", [P, NT, INNER])
        pos, mbias = sb("pos", [P, S]), sb("mbias", [P, CAUSAL])
        probs, probsT = sb("probs", [P, 4, CAUSAL]), sb("probsT", [P, 2, CAUSAL])
        negmax, rsum, rinv = sb("negmax", [P, H, NT]), sb("rsum", [P, H, NT]), sb("rinv", [P, H, NT])
        x1, ytmp = sb("x1", [P, NT, D]), sb("ytmp", [P, NT, D])
        oT = qT

        x1res, n, h = sb("x1res", [P, NT, D]), sb("n", [P, NT, D]), sb("h", [P, NT, D])
        statB, mvB, varB, rstdB = sb("statB", [P, NT, 6]), sb("mvB", [P, NT, 2]), sb("varB", [P, NT]), sb("rstdB", [P, NT])
        ms1, r1, ms2, r2 = sb("ms1", [P, NT]), sb("r1", [P, NT]), sb("ms2", [P, NT]), sb("r2", [P, NT])
        hT, dT = pair("hT", [P, ND, S]), pair("dT", [LAT, S])
        q, kv = sb("q", [P, NT, D]), sb("kv", [P, NT, 2 * D])
        att, amax, asum = sb("att", [P, NT, D]), sb("amax", [P, NT * H]), sb("asum", [P, NT * H])
        glog, gmax, gsum, gate = sb("glog", [P, NT, E]), sb("gmax", [P, NT]), sb("gsum", [P, NT]), sb("gate", [P, NT, E])
        y, acc, h2T = sb("y", [P, NT, D]), sb("acc", [P, NT, D]), pair("h2T", [P, ND, S])
        o, foT = h, hT

        own_at = {0: "k3", 1: "v1", 2: "v3", 3: "q2", 5: "q3"}
        ahead_at = {9: "k0", 10: "xT", 11: "k1", 13: "v0", 16: "k2", 19: "v2"}
        attn_uses = ["q0", "q1"]
        for s in range(STEPS):
            attn_uses += [f"T{s - LAG_T}"] * (LAG_T <= s < H + LAG_T)
            attn_uses += [use for at, use in (own_at | ahead_at).items() if at == s]
        attn = Banks(nc, ctx, "l0_attn", attn_uses + ["out"], ahead=["xT", "k0", "k1", "k2", "v0", "v2"])
        mix_at = {2: "hT", 3: "q", 4: "down", 5: "up0", 6: "up1"}
        expert_at = {6: 0, 7: 1, 8: 2, 10: 3, 12: 4, 14: 5, 15: 6, 17: 7}
        score_at = {7: 0, 9: 1, 11: 2, 12: 3}
        weighing_at = {13: ("divide",), 14: ("weigh0",), 16: ("other0",), 17: ("own0",), 18: ("weigh1",), 19: ("own1", "other1")}
        score = Banks(nc, ctx, "l0_score", [f"s{j}" for j in range(H)])
        heads = Banks(nc, ctx, "l0_heads", [f"o{j}" for j in range(4)], 1)
        mix = Banks(nc, ctx, "l0_mix", ["hT", "q", "down", "up0", "up1"], 1)
        moe = Banks(nc, ctx, "l0_moe", ["oT", "out", "h2T", "gate"] + [f"we{j}" for j in range(E)])

        raw_in, split_hi, split_lo = [sem("raw_in0"), sem("raw_in1")], sem("split_hi"), sem("split_lo")
        mask_in, scored = sem("mask_in"), sem("scored")
        pool_passed, dve_passed, sp_passed = sem("pool_passed"), sem("dve_passed"), sem("sp_passed")
        params_in, wo_in, consts, tanh_done = sem("params_in"), sem("wo_in"), sem("consts"), sem("tanh_done")
        x_in, ctx_in, xres_in, x2_stored = sem("x_in"), sem("ctx_in"), sem("xres_in"), sem("x2_stored")
        varA_ready, rstdA_ready, xn_ready, ctx_ready = sem("varA_ready"), sem("rstdA_ready"), sem("xn_ready"), sem("ctx_ready")
        mask_ready, exp_done, rinv_ready, norm_done = sem("mask_ready"), sem("exp_done"), sem("rinv_ready"), sem("norm_done")
        xT_hi, pv_done, x1_ready, x1_copied = sem("xT_hi"), sem("pv_done"), sem("x1_ready"), sem("x1_copied")
        varB_ready, rstdB_ready, ms1_ready, r1_ready = sem("varB_ready"), sem("rstdB_ready"), sem("ms1_ready"), sem("r1_ready")
        h_ready, hT_hi, dT_hi = sem("h_ready"), sem("hT_hi"), sem("dT_hi")
        prod_ready, sub_ready, aexp_done = sem("prod_ready"), sem("sub_ready"), sem("aexp_done")
        foT_hi, ms2_ready, r2_ready, h2_ready = sem("foT_hi"), sem("ms2_ready"), sem("r2_ready"), sem("h2_ready")
        att_ready, gathered = sem("att_ready"), sem("gathered")
        h2T_hi, glog_ready, gexp_done, x2_ready = sem("h2T_hi"), sem("glog_ready"), sem("gexp_done"), sem("x2_ready")

        def piece(src, dst, rows=P):
            return src, dst[0], dst[1], rows
        splits = [piece(ins["wk"], (wk[0][:].rearrange("p c n -> p (c n)"), wk[1][:].rearrange("p c n -> p (c n)"))),
                  piece(ins["wv"], (wv[0][:].rearrange("p c n -> p (c n)"), wv[1][:].rearrange("p c n -> p (c n)"))),
                  piece(ins["wq"], (wq[0][:].rearrange("p c n -> p (c n)"), wq[1][:].rearrange("p c n -> p (c n)"))),
                  piece(ins["fq"], (fq[0][:].rearrange("p c n -> p (c n)"), fq[1][:].rearrange("p c n -> p (c n)"))),
                  piece(ins["fdown"], (fdown[0][:].rearrange("p c n -> p (c n)"), fdown[1][:].rearrange("p c n -> p (c n)"))),
                  piece(ins["fup"], (fup[0][:], fup[1][:]), LAT),
                  piece(ins["fo"], (fo[0][:].rearrange("p c n -> p (c n)"), fo[1][:].rearrange("p c n -> p (c n)"))),
                  piece(ins["wg"], (wg[0][:].rearrange("p c n -> p (c n)"), wg[1][:].rearrange("p c n -> p (c n)"))),
                  piece(ins["we"][:, 0, :], (we[0][:, 0, :], we[1][:, 0, :])),
                  piece(ins["we"][:, 1, :], (we[0][:, 1, :], we[1][:, 1, :]))]
        NS, NS_FIRST = len(splits), 3
        params = [(bo[:], ins["bo"].to_broadcast([P, D])),
                  (bq[:], ins["bq"].to_broadcast([P, D])), (bup[:], ins["bup"].to_broadcast([P, 2 * D])),
                  (bfo[:], ins["bfo"].to_broadcast([P, D])), (bg[:], ins["bg"].to_broadcast([P, E])),
                  (bdown[:], ins["bdown"]), (gamma1[:], ins["gamma1"]), (gamma2[:], ins["gamma2"]),
                  (gates[:], ins["gates"].to_broadcast([P, 4]))]

        with nc.Block() as block:

            @block.sync
            def _(sp):
                def load(b):
                    if not first(b):
                        sp.wait_ge(xn_ready, b)
                    sp.dma_start(xin[:], ins["x"][bass.ds(b, 1)][0]).then_inc(x_in, 16)
                    if not first(b):
                        sp.wait_ge(ctx_ready, b)
                    sp.dma_start(ctxin[:], ins["ctx"][bass.ds(b, 1)][0]).then_inc(ctx_in, 16)

                    if not first(b):
                        wait_apart(sp, sp_passed, mask_ready, b)
                    sp.dma_start(maskbits[:], ins["mask"][bass.ds(b, 1)].to_broadcast([P, S])).then_inc(mask_in, 16)

                def load_residual(b):
                    if not first(b):
                        sp.wait_ge(x1_copied, b)
                        sp.wait_ge(h_ready, b)
                    sp.dma_start(x1[:], ins["x"][bass.ds(b, 1)][0]).then_inc(xres_in, 16)

                def store(b):
                    sp.wait_ge(x2_ready, b + 1)
                    sp.dma_start(x2[bass.ds(b, 1)][0], acc[:]).then_inc(x2_stored, 16)

                load(0)
                for k, (src, _hi, _lo, rows) in enumerate(splits):
                    if k >= 2:
                        sp.wait_ge(split_lo, k - 1)
                    sp.dma_start(stage[0:rows, k % 2, 0:src.shape[1]], src).then_inc(raw_in[k % 2], 16)
                    if k == 1:
                        for dst, src in params:
                            sp.dma_start(dst, src).then_inc(params_in, 16)
                    if k == 2:
                        load_residual(0)
                        sp.dma_start(wo[:].rearrange("p c n -> p (c n)"), ins["wo"]).then_inc(wo_in, 16)
                    if k == 3:
                        load(1)
                load(2)
                load_residual(1)
                with sp.Fori(3, B) as b:
                    load(b)
                    load_residual(b - 1)
                    store(b - 3)
                load_residual(B - 1)
                for b in (B - 3, B - 2, B - 1):
                    store(b)
                sp.wait_ge(x2_stored, 16 * B)

            @block.gpsimd
            def _(pool):
                nc.gpsimd.memset(ident[:], 0.0)
                nc.gpsimd.memset(cmask[:], 0.0)
                nc.gpsimd.memset(neghalf[:], -0.5)
                pool.drain()
                nc.gpsimd.affine_select(out=ident[:], in_=ident[:], compare_op=ALU.not_equal, fill=1.0, base=0,
                                        pattern=[[-1, P]], channel_multiplier=1)
                for c in (P, S):
                    last = nc.gpsimd.affine_select(out=cmask[:, c:c + P], in_=cmask[:, c:c + P], compare_op=ALU.is_ge,
                                                   fill=-NEG, base=0, pattern=[[-1, P]], channel_multiplier=1)
                last.then_inc(consts, 1)

                def power(ready, done, src, dst, b):
                    pool.wait_ge(ready, b + 1)
                    nc.gpsimd.tensor_tensor(dst[:], src[:], neghalf[:], ALU.pow).then_inc(done, 1)

                def split_context(a):
                    if not first(a):
                        _, full, _, turn = attn.at("v3", a - 1)
                        pool.wait_ge(full, turn)
                    wait_apart(pool, pool_passed, ctx_in, 16 * (a + 1))
                    nc.gpsimd.tensor_copy(cT[0][:], ctxin[:])
                    pool.drain()
                    nc.gpsimd.tensor_sub(cT[1][:], ctxin[:], cT[0][:].bitcast(F32)).then_inc(ctx_ready, 1)

                def mask(a):
                    if not first(a):
                        score.emptied(pool, f"s{H - 2}", a - 1)
                        score.emptied(pool, f"s{H - 1}", a - 1)
                    wait_apart(pool, pool_passed, mask_in, 16 * (a + 1))
                    nc.gpsimd.tensor_scalar(pos[:], maskbits[:], -1.0, NEG, ALU.add, ALU.mult)
                    pool.drain()
                    nc.gpsimd.tensor_tensor(mbias[:, 0:S], cmask[:, 0:S], pos[:], ALU.add)
                    nc.gpsimd.tensor_tensor(mbias[:, S:CAUSAL], cmask[:, S:CAUSAL], pos[:, 0:P], ALU.add).then_inc(mask_ready, 1)

                def query_key(b, t, u):
                    half, piece = H // 2, NT * t + u
                    if piece < 2:
                        mix.emptied(pool, "q", b)
                        mix.emptied(pool, f"up{t}", b)
                    else:
                        mix.emptied(pool, f"up{t}", b)
                        pool.wait_ge(scored, 4 * b + piece - 1)
                    k4 = kv[:, t].rearrange("p (g two d) -> p g two d", two=2, d=HD)[:, :, 0, :]
                    q4 = q[:, t].rearrange("p (h d) -> p h d", d=HD)
                    nc.gpsimd.tensor_tensor(
                        prod[:, u].rearrange("p (h g d) -> p h g d", h=half, g=H),
                        q4[:, u * half:(u + 1) * half].unsqueeze(2).to_broadcast([P, half, H, HD]),
                        k4.unsqueeze(1).to_broadcast([P, half, H, HD]), ALU.mult).then_inc(prod_ready, 1)

                def weigh(b, u):
                    half = H // 2
                    if u == 0:
                        pool.wait_ge(att_ready, b + 1)
                    else:
                        pool.wait_ge(gathered, 2 * b + 1)
                    v4 = kv[:, 0].rearrange("p (g two d) -> p two d g", two=2, d=HD)[:, 1]
                    a4 = att[:, 0].rearrange("p (h g) -> p h g", g=H)[:, u * half:(u + 1) * half]
                    nc.gpsimd.tensor_tensor(prod[:, 1].rearrange("p (h d g) -> p h d g", h=half, d=HD),
                                            a4.unsqueeze(2).to_broadcast([P, half, HD, H]), v4.unsqueeze(1).to_broadcast([P, half, HD, H]),
                                            ALU.mult).then_inc(prod_ready, 1)

                def body(a, b, c, nxt):
                    if a is not None:
                        mask(a)
                    if b is not None:
                        power(varB_ready, rstdB_ready, varB, rstdB, b)
                    if b is not None:
                        power(ms1_ready, r1_ready, ms1, r1, b)
                    if c is not None:
                        power(ms2_ready, r2_ready, ms2, r2, c)
                    if nxt is not None:
                        split_context(nxt)
                        power(varA_ready, rstdA_ready, varA, rstdA, nxt)
                    if b is not None:
                        query_key(b, 0, 0)
                        query_key(b, 0, 1)
                        query_key(b, 1, 0)
                        query_key(b, 1, 1)
                        weigh(b, 0)
                        weigh(b, 1)

                split_context(0)
                power(varA_ready, rstdA_ready, varA, rstdA, 0)
                body(0, None, None, 1)
                pool.wait_ge(split_lo, NS)
                body(1, 0, None, 2)
                body(2, 1, 0, 3)
                with pool.Fori(3, B - 1) as a:
                    body(a, a - 1, a - 2, a + 1)
                body(B - 1, B - 2, B - 3, None)
                body(None, B - 1, B - 2, None)
                body(None, None, B - 1, None)

            @block.scalar
            def _(act):
                nc.scalar.preload_act_table(ACT.Exp)

                def split(k):
                    src, hi, _lo, rows = splits[k]
                    act.wait_ge(raw_in[k % 2], 16 * (k // 2 + 1))
                    nc.scalar.copy(hi, stage[0:rows, k % 2, 0:src.shape[1]]).then_inc(split_hi, 1)

                for k in range(NS_FIRST):
                    split(k)
                act.wait_ge(params_in, 16 * len(params))
                nc.scalar.activation(tg[:], gates[:], ACT.Tanh).then_inc(tanh_done, 1)

                def high(banks, use, batch, dst, ready, scales=None):
                    ps, full, free, turn = banks.at(use, batch)
                    act.wait_ge(full, turn)
                    if scales is None:
                        nc.scalar.copy(dst[:].rearrange("p c n -> p (c n)"), ps[:]).then_inc(ready, 1)
                    else:
                        for c in range(ND):
                            last = nc.scalar.activation(dst[:, c, :], ps[:, c * S:(c + 1) * S], ACT.Copy, scale=scales[:, c:c + 1])
                        last.then_inc(ready, 1)

                def copy_out(use, a, dst):
                    ps, full, free, turn = attn.at(use, a)
                    act.wait_ge(full, turn)
                    nc.scalar.copy(dst, ps[:]).then_inc(free, 1)

                def pair_of(t, j):
                    return t[:, 2 * j:2 * j + 2, :].rearrange("p c n -> p (c n)")

                def attn_exp(a, s):
                    score.emptied(act, f"s{s}", a)
                    nc.scalar.activation(probs[:, s % 4, 0:S], probs[:, s % 4, 0:S], ACT.Exp, bias=negmax[:, s, 1:2],
                                         scale=-1.0, accum_out=rsum[:, s, 1:2])
                    nc.scalar.activation(probs[:, s % 4, S:CAUSAL], probs[:, s % 4, S:CAUSAL], ACT.Exp, bias=negmax[:, s, 0:1],
                                         scale=-1.0, accum_out=rsum[:, s, 0:1]).then_inc(exp_done, 1)

                def attn_normalise(a, j):
                    act.wait_ge(rinv_ready, H * a + j + 1)
                    nc.scalar.activation(probs[:, j % 4, 0:S], probs[:, j % 4, 0:S], ACT.Copy, scale=rinv[:, j, 1:2])
                    nc.scalar.activation(probs[:, j % 4, S:CAUSAL], probs[:, j % 4, S:CAUSAL], ACT.Copy,
                                         scale=rinv[:, j, 0:1]).then_inc(norm_done, 1)

                def attn_copy(a, j):
                    ps, full, free, turn = attn.at(f"T{j}", a)
                    act.wait_ge(full, turn)
                    if j >= 2:
                        act.wait_ge(pv_done, H * a + j - 1)
                    nc.scalar.copy(probsT[:, j % 2, :], ps[:, 0:CAUSAL]).then_inc(free, 1)

                def project(use, a):
                    j = int(use[1:]) if use != "xT" else None
                    if use == "xT":
                        high(attn, "xT", a, xT[0], xT_hi)
                    elif use[0] == "q":
                        copy_out(use, a, pair_of(qT, j))
                    elif use[0] == "k":
                        copy_out(use, a, pair_of(kT, j))
                    else:
                        copy_out(use, a, v[:, j // 2, (j % 2) * 512:(j % 2 + 1) * 512])

                def before_exp(b, c, s):
                    if b is not None and mix_at.get(s) == "hT":
                        high(mix, "hT", b, hT[0], hT_hi, gamma1)
                    if b is not None and mix_at.get(s) == "down":
                        ps, full, _, turn = mix.at("down", b)
                        act.wait_ge(full, turn)
                        nc.scalar.activation(dT[0][:], ps[0:LAT, 0:S], ACT.Identity, bias=bdown[:]).then_inc(dT_hi, 1)
                    if c is not None and s == 4:
                        high(moe, "h2T", c, h2T[0], h2T_hi, gamma2)

                def beside_head(a, b, c, nxt, s):
                    if c is not None and s == 5:
                        act.wait_ge(glog_ready, c + 1)
                        for t in range(NT):
                            last = nc.scalar.activation(gate[:, t], glog[:, t], ACT.Exp, bias=gmax[:, t:t + 1], accum_out=gsum[:, t:t + 1])
                        last.then_inc(gexp_done, 1)
                    if b is not None and s == 12:
                        act.wait_ge(sub_ready, b + 1)
                        nc.scalar.activation(att[:], att[:], ACT.Exp, scale=HD ** -0.5).then_inc(aexp_done, 1)
                    if a is not None and s in own_at:
                        project(own_at[s], a)
                    if nxt is not None and s in ahead_at:
                        project(ahead_at[s], nxt)

                def head_group(a, j):
                    ps, _, free, _ = heads.at(f"o{j}", a)
                    act.wait_ge(pv_done, H * a + 4 * j + 4)
                    nc.scalar.copy(pair_of(oT, j), ps[:]).then_inc(free, 1)

                def body(a, b, c, nxt):
                    if c is not None:
                        high(moe, "oT", c, foT[0], foT_hi)
                    if a is not None:
                        project("q0", a)
                        project("q1", a)
                    for s in range(STEPS):
                        if s >= 1:
                            beside_head(a, b, c, nxt, s - 1)
                        if first(a) and 1 <= s <= NS - NS_FIRST:
                            split(NS_FIRST + s - 1)
                        before_exp(b, c, s)
                        if a is not None:
                            if LAG_T <= s < H + LAG_T:
                                attn_copy(a, s - LAG_T)
                            if s - LAG_V in (3, 7, 11):
                                head_group(a, (s - LAG_V) // 4)
                            if s < H:
                                attn_exp(a, s)
                            if 1 <= s < H + 1:
                                attn_normalise(a, s - 1)
                    if a is not None:
                        head_group(a, 3)
                    beside_head(a, b, c, nxt, STEPS - 1)

                for use in attn.ahead:
                    project(use, 0)
                body(0, None, None, 1)
                body(1, 0, None, 2)
                body(2, 1, 0, 3)
                with act.Fori(3, B - 1) as a:
                    body(a, a - 1, a - 2, a + 1)
                body(B - 1, B - 2, B - 3, None)
                body(None, B - 1, B - 2, None)
                body(None, None, B - 1, None)

            @block.vector
            def _(dve):
                for banks in (attn, score, heads, mix, moe):
                    banks.open(dve)
                V = nc.vector

                def variance(src, stat, mv, var, ready):
                    for t in range(NT):
                        V.bn_stats(stat[:, t], src[:, t])
                    dve.drain()
                    for t in range(NT):
                        V.bn_aggr(mv[:, t], stat[:, t])
                    dve.drain()
                    V.tensor_scalar(var[:], mv[:, :, 1], LN_EPS, None, ALU.add).then_inc(ready, 1)

                def pre_variance(a):
                    dve.wait_ge(x_in, 16 * (a + 1))
                    variance(xin, statA, mvA, varA, varA_ready)

                def pre_normalise(a):
                    dve.wait_ge(rstdA_ready, a + 1)
                    for t in range(NT):
                        last = V.tensor_scalar(xn[:, t], xin[:, t], mvA[:, t, 0:1], rstdA[:, t:t + 1], ALU.subtract, ALU.mult)
                    last.then_inc(xn_ready, 1)

                def low(banks, use, batch, dst, hi_ready, scales=None):
                    ps, _, free, _ = banks.at(use, batch)
                    dve.wait_ge(hi_ready, batch + 1)
                    if scales is None:
                        last = V.tensor_sub(dst[1][:].rearrange("p c n -> p (c n)"), ps[:],
                                            dst[0][:].rearrange("p c n -> p (c n)").bitcast(F32))
                    else:
                        for c in range(ND):
                            last = V.scalar_tensor_tensor(out=dst[1][:, c, :], in0=ps[:, c * S:(c + 1) * S], scalar=scales[:, c:c + 1],
                                                          in1=dst[0][:, c, :].bitcast(F32), op0=ALU.mult, op1=ALU.subtract)
                    last.then_inc(free, 1)

                def mix_normalise(b):
                    dve.wait_ge(rstdB_ready, b + 1)
                    V.tensor_tensor(ms1[:], mvB[:, :, 1], rstdB[:], ALU.mult)
                    for t in range(NT):
                        V.tensor_scalar(n[:, t], x1[:, t], mvB[:, t, 0:1], rstdB[:, t:t + 1], ALU.subtract, ALU.mult)
                    dve.drain()
                    V.tensor_tensor(ms1[:], ms1[:], rstdB[:], ALU.mult)
                    dve.drain()
                    V.tensor_scalar(ms1[:], ms1[:], RMS_EPS, None, ALU.add).then_inc(ms1_ready, 1)

                def mix_rms(b):
                    dve.wait_ge(r1_ready, b + 1)
                    for t in range(NT):
                        last = V.tensor_scalar(h[:, t], n[:, t], r1[:, t:t + 1], None, ALU.mult)
                    last.then_inc(h_ready, 1)

                def mix_queries(b):
                    ps, full, free, turn = mix.at("q", b)
                    dve.wait_ge(full, turn)
                    V.tensor_tensor(q[:], ps[:].rearrange("p (t n) -> p t n", t=NT), bq[:].unsqueeze(1).to_broadcast([P, NT, D]),
                                    ALU.add).then_inc(free, 1)

                def mix_down(b):
                    ps, _, free, _ = mix.at("down", b)
                    dve.wait_ge(dT_hi, b + 1)
                    V.scalar_tensor_tensor(out=dT[1][:], in0=ps[0:LAT, 0:S], scalar=bdown[:], in1=dT[0][:].bitcast(F32),
                                           op0=ALU.add, op1=ALU.subtract).then_inc(free, 1)

                def mix_kv(b, t):
                    ps, full, free, turn = mix.at(f"up{t}", b)
                    dve.wait_ge(full, turn)
                    V.tensor_tensor(kv[:, t], ps[:], bup[:], ALU.add).then_inc(free, 1)

                def mix_scores(b, t, u):
                    dve.wait_ge(prod_ready, 6 * b + 2 * t + u + 1)
                    V.tensor_reduce(att[:, t, u * P:(u + 1) * P], prod[:, u].rearrange("p (x d) -> p x d", d=HD),
                                    axis=AX.X, op=ALU.add).then_inc(scored, 1)

                att3 = att[:].rearrange("p t (h g) -> p (t h) g", g=H)

                def mix_softmax_max(b):
                    dve.drain()
                    V.tensor_reduce(amax[:], att3, axis=AX.X, op=ALU.max)
                    dve.drain()
                    V.tensor_tensor(att3, att3, amax[:].unsqueeze(2).to_broadcast([P, NT * H, H]), ALU.subtract).then_inc(sub_ready, 1)

                def mix_softmax_divide(b):
                    dve.wait_ge(aexp_done, b + 1)
                    V.tensor_reduce(asum[:], att3, axis=AX.X, op=ALU.add)
                    dve.drain()
                    V.reciprocal(asum[:], asum[:])
                    dve.drain()
                    V.tensor_tensor(att3, att3, asum[:].unsqueeze(2).to_broadcast([P, NT * H, H]), ALU.mult).then_inc(att_ready, 1)
                    dve.drain()

                half = H // 2

                def mix_weigh(u):
                    v4 = kv[:, 1].rearrange("p (g two d) -> p two d g", two=2, d=HD)[:, 1]
                    a4 = att[:, 1].rearrange("p (h g) -> p h g", g=H)[:, u * half:(u + 1) * half]
                    V.tensor_tensor(prod[:, 0].rearrange("p (h d g) -> p h d g", h=half, d=HD),
                                    a4.unsqueeze(2).to_broadcast([P, half, HD, H]), v4.unsqueeze(1).to_broadcast([P, half, HD, H]), ALU.mult)

                def mix_gather(t, u, buffer):
                    return V.tensor_reduce(o[:, t, u * P:(u + 1) * P], prod[:, buffer].rearrange("p (x g) -> p x g", g=H),
                                           axis=AX.X, op=ALU.add)

                def moe_residual(c):
                    ps, full, free, turn = moe.at("out", c)
                    dve.wait_ge(full, turn)
                    V.tensor_tensor(y[:], ps[:].rearrange("p (t n) -> p t n", t=NT), bfo[:].unsqueeze(1).to_broadcast([P, NT, D]),
                                    ALU.add).then_inc(free, 1)
                    dve.drain()
                    V.tensor_tensor(y[:], y[:], n[:], ALU.add)
                    dve.drain()

                def moe_squares(c):
                    if not first(c):
                        dve.wait_ge(x2_stored, 16 * c)
                    V.scalar_tensor_tensor(out=acc[:], in0=y[:], scalar=tg[:, 1:2], in1=x1res[:], op0=ALU.mult, op1=ALU.add)
                    for t in range(NT):
                        V.tensor_tensor_reduce(out=ytmp[:, t], in0=y[:, t], in1=y[:, t], scale=1.0 / D, scalar=0.0,
                                               op0=ALU.mult, op1=ALU.add, accum_out=ms2[:, t:t + 1])
                    dve.drain()
                    V.tensor_scalar(ms2[:], ms2[:], RMS_EPS, None, ALU.add).then_inc(ms2_ready, 1)

                def moe_normalise(c):
                    dve.wait_ge(r2_ready, c + 1)
                    for t in range(NT):
                        last = V.tensor_scalar(y[:, t], y[:, t], r2[:, t:t + 1], None, ALU.mult)
                    last.then_inc(h2_ready, 1)

                def moe_gate_logits(c):
                    ps, full, free, turn = moe.at("gate", c)
                    dve.wait_ge(full, turn)
                    V.tensor_tensor(glog[:], ps[:, 0:NT * E].rearrange("p (t e) -> p t e", t=NT), bg[:].unsqueeze(1).to_broadcast([P, NT, E]),
                                    ALU.add).then_inc(free, 1)
                    dve.drain()
                    V.tensor_reduce(gmax[:], glog[:], axis=AX.X, op=ALU.max, negate=True).then_inc(glog_ready, 1)

                def moe_gate(c):
                    dve.wait_ge(gexp_done, c + 1)
                    V.reciprocal(gsum[:], gsum[:])
                    dve.drain()
                    V.tensor_scalar(gsum[:], gsum[:], tg[:, 1:2], None, ALU.mult)
                    dve.drain()
                    V.tensor_tensor(gate[:], gate[:], gsum[:].unsqueeze(2).to_broadcast([P, NT, E]), ALU.mult)
                    dve.drain()

                def moe_experts(c, j):
                    ps, full, free, turn = moe.at(f"we{j}", c)
                    dve.wait_ge(full, turn)
                    for t in range(NT):
                        last = V.scalar_tensor_tensor(out=acc[:, t], in0=ps[:, t * D:(t + 1) * D], scalar=gate[:, t, j:j + 1], in1=acc[:, t],
                                                      op0=ALU.mult, op1=ALU.add)
                    last.then_inc(free, 1)
                    if j == E - 1:
                        dve.drain().then_inc(x2_ready, 1)
                    else:
                        dve.drain()

                def attn_max(a, j):
                    ps, full, free, turn = score.at(f"s{j}", a)
                    wait_apart(dve, dve_passed, full, turn)
                    for t, lo, hi in ((1, 0, S), (0, S, CAUSAL)):
                        last = V.tensor_tensor_reduce(out=probs[:, j % 4, lo:hi], in0=ps[:, lo:hi], in1=mbias[:, lo:hi], scale=-HD0 ** -0.5,
                                                      scalar=3e38, op0=ALU.add, op1=ALU.min, accum_out=negmax[:, j, t:t + 1])
                    last.then_inc(free, 1)

                def attn_sum(a, j):
                    dve.wait_ge(exp_done, H * a + j + 1)
                    V.reciprocal(rinv[:, j], rsum[:, j]).then_inc(rinv_ready, 1)

                def attn_final(a):
                    ps, full, free, turn = attn.at("out", a)
                    dve.wait_ge(full, turn)
                    V.tensor_tensor(ytmp[:], ps[:].rearrange("p (t n) -> p t n", t=NT), bo[:].unsqueeze(1).to_broadcast([P, NT, D]),
                                    ALU.add).then_inc(free, 1)
                    dve.drain()
                    dve.wait_ge(xres_in, 16 * (a + 1))
                    V.scalar_tensor_tensor(out=x1[:], in0=ytmp[:], scalar=tg[:, 0:1], in1=x1[:], op0=ALU.mult,
                                           op1=ALU.add).then_inc(x1_ready, 1)

                def beside_head(b, c, nxt, s):
                    if s == 0 and b is not None:
                        mix_rms(b)
                    if s == 1:
                        if c is not None:
                            moe_squares(c)
                        if b is not None:
                            V.tensor_copy(x1res[:], x1[:]).then_inc(x1_copied, 1)
                    if b is not None and s in mix_at:
                        use = mix_at[s]
                        if use == "hT":
                            low(mix, "hT", b, hT, hT_hi, gamma1)
                        elif use == "q":
                            mix_queries(b)
                        elif use == "down":
                            mix_down(b)
                        else:
                            mix_kv(b, int(use[2:]))
                    if c is not None:
                        if s == 2:
                            moe_normalise(c)
                        elif s == 4:
                            low(moe, "h2T", c, h2T, h2T_hi, gamma2)
                        elif s == 5:
                            moe_gate_logits(c)
                        elif s in expert_at:
                            if expert_at[s] == 0:
                                moe_gate(c)
                            moe_experts(c, expert_at[s])
                    if nxt is not None:
                        if s == 3:
                            pre_variance(nxt)
                        elif s == 7:
                            pre_normalise(nxt)
                        elif ahead_at.get(s) == "xT":
                            low(attn, "xT", nxt, xT, xT_hi)
                    if b is not None:
                        if s in score_at:
                            mix_scores(b, score_at[s] // 2, score_at[s] % 2)
                            if score_at[s] == 3:
                                mix_softmax_max(b)
                        for what in weighing_at.get(s, ()):
                            dve.drain()
                            if what == "divide":
                                mix_softmax_divide(b)
                            elif what in ("weigh0", "weigh1"):
                                mix_weigh(int(what[-1]))
                            elif what in ("own0", "own1"):
                                mix_gather(1, int(what[-1]), 0)
                            else:
                                u = int(what[-1])
                                mix_gather_ready(b, u)
                                mix_gather(0, u, 1).then_inc(gathered, 1)

                def split(k):
                    src, hi, lo, rows = splits[k]
                    dve.wait_ge(split_hi, k + 1)
                    V.tensor_sub(lo, stage[0:rows, k % 2, 0:src.shape[1]], hi.bitcast(F32)).then_inc(split_lo, 1)

                def mix_gather_ready(b, u):
                    dve.wait_ge(prod_ready, 6 * b + 4 + u + 1)

                def body(a, b, c, nxt):
                    if c is not None:
                        low(moe, "oT", c, foT, foT_hi)
                    if b is not None:
                        dve.drain()
                        variance(x1, statB, mvB, varB, varB_ready)
                    if c is not None:
                        moe_residual(c)
                    if b is not None:
                        mix_normalise(b)
                    if a is not None:
                        dve.wait_ge(mask_ready, a + 1)
                    for s in range(STEPS):
                        if a is not None:
                            if s < H:
                                attn_max(a, s)
                            if 1 <= s < H + 1:
                                attn_sum(a, s - 1)
                        beside_head(b, c, nxt, s)
                        if first(a) and 1 <= s <= NS - NS_FIRST:
                            split(NS_FIRST + s - 1)
                    if a is not None:
                        attn_final(a)

                pre_variance(0)
                split(0)
                pre_normalise(0)
                for k in range(1, NS_FIRST):
                    split(k)
                dve.wait_ge(params_in, 16 * len(params))
                dve.wait_ge(tanh_done, 1)
                low(attn, "xT", 0, xT, xT_hi)
                body(0, None, None, 1)
                body(1, 0, None, 2)
                body(2, 1, 0, 3)
                with dve.Fori(3, B - 1) as a:
                    body(a, a - 1, a - 2, a + 1)
                body(B - 1, B - 2, B - 3, None)
                body(None, B - 1, B - 2, None)
                body(None, None, B - 1, None)

            @block.tensor
            def _(pe):
                T = nc.tensor

                def transpose4(banks, use, batch, src):
                    ps, full, free, turn = banks.at(use, batch)
                    pe.wait_ge(free, turn)
                    for c in range(ND):
                        for t in range(NT):
                            last = T.transpose(ps[:, c * S + t * P:c * S + (t + 1) * P], src[:, t, c * P:(c + 1) * P], ident[:])
                    last.then_inc(full, 1)

                def features(use, a, w, x):
                    j = int(use[1:])
                    ps, full, free, turn = attn.at(use, a)
                    pe.wait_ge(free, turn)
                    for u in range(2):
                        m = slice((2 * j + u) * P, (2 * j + u + 1) * P)
                        last = product3(nc, ps[:, u * S:(u + 1) * S],
                                        [(w[0][:, c, m], w[1][:, c, m], x[0][:, c, :], x[1][:, c, :]) for c in range(ND)])
                    last.then_inc(full, 1)

                def values(j, a):
                    t, m = j // 2, slice((j % 2) * 512, (j % 2 + 1) * 512)
                    ps, full, free, turn = attn.at(f"v{j}", a)
                    pe.wait_ge(free, turn)
                    product3(nc, ps[:], [(cT[0][:, c, t * P:(t + 1) * P], cT[1][:, c, t * P:(t + 1) * P], wv[0][:, c, m], wv[1][:, c, m])
                                         for c in range(ND)]).then_inc(full, 1)

                def tokens(banks, use, b, x, w, cols):
                    ps, full, free, turn = banks.at(use, b)
                    pe.wait_ge(free, turn)
                    for t in range(NT):
                        last = product3(nc, ps[:, t * cols:(t + 1) * cols],
                                        [(x[0][:, c, t * P:(t + 1) * P], x[1][:, c, t * P:(t + 1) * P], w[0][:, c, :], w[1][:, c, :])
                                         for c in range(ND)])
                    last.then_inc(full, 1)

                def mix_down(b):
                    ps, full, free, turn = mix.at("down", b)
                    pe.wait_ge(free, turn)
                    product3(nc, ps[0:LAT, 0:S], [(fdown[0][:, c, :], fdown[1][:, c, :], hT[0][:, c, :], hT[1][:, c, :])
                                                  for c in range(ND)]).then_inc(full, 1)

                def mix_up(b, t):
                    if t == 0:
                        mix.emptied(pe, "down", b)
                    ps, full, free, turn = mix.at(f"up{t}", b)
                    pe.wait_ge(free, turn)
                    product3(nc, ps[:], [(dT[0][:, t * P:(t + 1) * P], dT[1][:, t * P:(t + 1) * P], fup[0][:], fup[1][:])]).then_inc(full, 1)

                def moe_experts(c, j):
                    moe_product(f"we{j}", c, [w[:, :, j * D:(j + 1) * D] for w in we], D)

                def moe_product(use, c, w, cols):
                    ps, full, free, turn = moe.at(use, c)
                    pe.wait_ge(free, turn)
                    for t in range(NT):
                        last = product3(nc, ps[:, t * cols:(t + 1) * cols],
                                        [(h2T[0][:, k, t * P:(t + 1) * P], h2T[1][:, k, t * P:(t + 1) * P], w[0][:, k, :], w[1][:, k, :])
                                         for k in range(ND)])
                    last.then_inc(full, 1)

                def head_scores(a, j):
                    c, r = j // HPC, slice((j % HPC) * HD0, (j % HPC + 1) * HD0)
                    ps, full, free, turn = score.at(f"s{j}", a)
                    pe.wait_ge(free, turn)
                    T.matmul(ps[:, 0:S], qT[r, c, P:S], kT[r, c, :], start=True, stop=True)
                    T.matmul(ps[:, S:CAUSAL], qT[r, c, 0:P], kT[r, c, 0:P], start=True, stop=True).then_inc(full, 1)

                def head_transpose(a, j):
                    ps, full, free, turn = attn.at(f"T{j}", a)
                    pe.wait_ge(free, turn)
                    pe.wait_ge(norm_done, H * a + j + 1)
                    T.transpose(ps[:, 0:P], probs[:, j % 4, S:CAUSAL], ident[:])
                    T.transpose(ps[:, P:S], probs[:, j % 4, 0:P], ident[:])
                    T.transpose(ps[:, S:CAUSAL], probs[:, j % 4, P:S], ident[:]).then_inc(full, 1)

                def head_values(a, j):
                    g, u, r = j // 4, (j // HPC) % 2, slice((j % HPC) * HD0, (j % HPC + 1) * HD0)
                    ps, full, free, turn = heads.at(f"o{g}", a)
                    if j % 4 == 0:
                        pe.wait_ge(free, turn)
                    attn.emptied(pe, f"T{j}", a)
                    m = slice(j * HD0, (j + 1) * HD0)
                    T.matmul(ps[r, u * S:(u + 1) * S], v[:, 0, m], probsT[:, j % 2, 0:S], start=True, stop=False)
                    last = T.matmul(ps[r, u * S + P:(u + 1) * S], v[:, 1, m], probsT[:, j % 2, S:CAUSAL], start=False, stop=True)
                    last.then_inc(pv_done, 1)

                def attn_out(a):
                    ps, full, free, turn = attn.at("out", a)
                    if first(a):
                        pe.wait_ge(wo_in, 16)
                    pe.wait_ge(free, turn)
                    for t in range(NT):
                        for c in range(NC0):
                            last = T.matmul(ps[:, t * D:(t + 1) * D], oT[:, c, t * P:(t + 1) * P], wo[:, c, :], start=c == 0, stop=c == NC0 - 1)
                    last.then_inc(full, 1)

                def project(use, a):
                    if use == "xT":
                        pe.wait_ge(xn_ready, a + 1)
                        transpose4(attn, "xT", a, xn)
                    elif use[0] == "q":
                        features(use, a, wq, xT)
                    elif use[0] == "k":
                        if use == "k0":
                            pe.wait_ge(ctx_ready, a + 1)
                        features(use, a, wk, cT)
                    else:
                        values(int(use[1:]), a)

                def beside_head(b, c, s):
                    if b is not None and s in mix_at:
                        use = mix_at[s]
                        if use == "hT":
                            pe.wait_ge(h_ready, b + 1)
                            transpose4(mix, "hT", b, h)
                        elif use == "q":
                            mix.emptied(pe, "hT", b)
                            tokens(mix, "q", b, hT, fq, D)
                        elif use == "down":
                            mix_down(b)
                        else:
                            mix_up(b, int(use[2:]))
                    if c is not None:
                        if s == 4:
                            pe.wait_ge(h2_ready, c + 1)
                            transpose4(moe, "h2T", c, y)
                        elif s == 5:
                            moe.emptied(pe, "h2T", c)
                            moe_product("gate", c, wg, E)
                        elif s in expert_at:
                            moe_experts(c, expert_at[s])

                def body(a, b, c, nxt):
                    if c is not None:
                        pe.wait_ge(gathered, 2 * (c + 1))
                        transpose4(moe, "oT", c, o)
                    if a is not None:
                        attn.emptied(pe, "xT", a)
                        project("q0", a)
                        project("q1", a)
                    if c is not None:
                        moe.emptied(pe, "oT", c)
                        tokens(moe, "out", c, foT, fo, D)
                    if a is not None:
                        attn.emptied(pe, "v2", a)
                        attn.emptied(pe, "q0", a)
                    for s in range(STEPS):
                        if a is not None and s < H:
                            if s % 4 == 0 and s > 0:
                                attn.emptied(pe, f"q{s // 4}", a)
                            if s == 12:
                                attn.emptied(pe, "k3", a)
                            head_scores(a, s)
                        if a is not None and s == LAG_T:
                            head_transpose(a, 0)
                        beside_head(b, c, s)
                        if a is not None:
                            if LAG_T < s < H + LAG_T:
                                head_transpose(a, s - LAG_T)
                            if s >= LAG_V:
                                if s - LAG_V == 8:
                                    attn.emptied(pe, "v1", a)
                                    attn.emptied(pe, "v3", a)
                                head_values(a, s - LAG_V)
                            if s in own_at:
                                project(own_at[s], a)
                        if nxt is not None and s in ahead_at:
                            project(ahead_at[s], nxt)
                    if a is not None:
                        heads.emptied(pe, "o2", a)
                        heads.emptied(pe, "o3", a)
                        attn_out(a)

                pe.wait_ge(consts, 1)
                for use in attn.ahead:
                    if use in ("k0", "v0"):
                        pe.wait_ge(split_lo, 1 + ("k0", "v0").index(use))
                    project(use, 0)
                pe.wait_ge(split_lo, NS_FIRST)
                body(0, None, None, 1)
                pe.wait_ge(split_lo, NS)
                body(1, 0, None, 2)
                body(2, 1, 0, 3)
                with pe.Fori(3, B - 1) as a:
                    body(a, a - 1, a - 2, a + 1)
                body(B - 1, B - 2, B - 3, None)
                body(None, B - 1, B - 2, None)
                body(None, None, B - 1, None)


def layer1(nc, ins, x2, out):
    with ExitStack() as ctx:
        def sb(name, shape, dtype=F32):
            return ctx.enter_context(nc.sbuf_tensor("l1_" + name, shape, dtype))

        def sem(name):
            return ctx.enter_context(nc.semaphore("l1_" + name))

        def pair(name, shape):
            return sb(name + "_hi", shape, F32R), sb(name + "_lo", shape, F32R)

        wq, wk, wv = pair("wq", [P, ND, NC1 * P]), pair("wk", [P, ND, NC1 * P]), pair("wv", [P, ND, D])
        w1 = pair("w1", [P, ND, 3 * HID])
        wo, w2 = sb("wo", [P, NC1, D]), sb("w2", [P, 3 * NHC, D])
        bq, bk, b1 = sb("bq", [P, NC1]), sb("bk", [P, NC1]), sb("b1", [P, 3 * NHC])
        bv, bo, b2, b2sum = sb("bv", [P, D]), sb("bo", [P, D]), sb("b2", [P, 3, D]), sb("b2sum", [P, D])
        gw, gates, tg = sb("gw", [P, 2, D]), sb("gates", [P, 4]), sb("tg", [P, 4])
        ident, neghalf = sb("ident", [P, P]), sb("neghalf", [P, NT])
        again = sb("again", [P, 1])

        xin, ctxin, xn = sb("xin", [P, NT, D]), sb("ctxin", [P, ND, S]), sb("xn", [P, NT, D])
        statC, mvC, varC, rstdC = sb("statC", [P, NT, 6]), sb("mvC", [P, NT, 2]), sb("varC", [P, NT]), sb("rstdC", [P, NT])
        xT, cT, k = pair("xT", [P, ND, S]), pair("cT", [P, ND, S]), pair("k", [P, NC1, S])
        qfull, qhi, q = sb("qfull", [P, NC1, S]), sb("qhi", [P, NC1, S], F32R), sb("q", [P, NC1, S], F32R)
        v = sb("v", [P, NT, H, SLOT])
        probs, probsT = sb("probs", [P, 4, NT * S]), sb("probsT", [P, 2, NT * S])
        negmax, rsum, rinv = sb("negmax", [P, H, NT]), sb("rsum", [P, H, NT]), sb("rinv", [P, H, NT])
        oT, x3, ytmp = sb("oT", [P, NC1, S]), sb("x3", [P, NT, D]), sb("ytmp", [P, NT, D])

        x3res, xf, x0 = sb("x3res", [P, NT, D]), sb("xf", [P, NT, D]), sb("x0", [P, NT, D])
        statF, mvF, varF, rstdF = sb("statF", [P, NT, 6]), sb("mvF", [P, NT, 2]), sb("varF", [P, NT]), sb("rstdF", [P, NT])
        gscore, first_wins = sb("gscore", [P, NT, 2]), sb("first_wins", [P, NT])
        xfT, x0T, x1T = pair("xfT", [P, ND, S]), pair("x0T", [P, ND, S]), pair("x1T", [P, ND, S])
        hid = sb("hid", [P, 3 * NHC, S])
        stage = hid[:].rearrange("p (a c) n -> p a (c n)", a=2)
        x4 = sb("x4", [P, NT, D])

        own_at = {0: "v0", 1: "v1", 2: "k1", 3: "q1"}
        ahead_at = {9: "k0", 14: "xT", 16: "q0"}
        attn_uses = []
        for s in range(STEPS):
            attn_uses += [f"T{s - LAG_T}"] * (LAG_T <= s < H + LAG_T)
            attn_uses += [use for at, use in (own_at | ahead_at).items() if at == s]
        attn = Banks(nc, ctx, "l1_attn", attn_uses + ["out"], ahead=["xT", "k0", "q0"])
        score = Banks(nc, ctx, "l1_score", [f"s{j}" for j in range(H)])
        heads = Banks(nc, ctx, "l1_heads", ["o0", "o1"])
        ffn = Banks(nc, ctx, "l1_ffn", ["xfT", "x0T"] + [f"h{j}" for j in range(12)] + ["y0", "y1"])

        raw_in, split_hi, split_lo = [sem("raw_in0"), sem("raw_in1")], sem("split_hi"), sem("split_lo")
        pool_passed = sem("pool_passed")
        params_in, wo_in, w2_in, consts, tanh_done, bias_ready = sem("params_in"), sem("wo_in"), sem("w2_in"), sem("consts"), sem("tanh_done"), sem("bias_ready")
        x_in, ctx_in, xres_in, x4_stored = sem("x_in"), sem("ctx_in"), sem("xres_in"), sem("x4_stored")
        varC_ready, rstdC_ready, xn_ready, ctx_ready = sem("varC_ready"), sem("rstdC_ready"), sem("xn_ready"), sem("ctx_ready")
        xT_hi, k_hi, q_hi, max_ready = sem("xT_hi"), sem("k_hi"), sem("q_hi"), sem("max_ready")
        rinv_ready, norm_done, pv_done = sem("rinv_ready"), sem("norm_done"), sem("pv_done")
        x3_ready, x3_copied, varF_ready, rstdF_ready = sem("x3_ready"), sem("x3_copied"), sem("varF_ready"), sem("rstdF_ready")
        xf_ready, xfT_hi, x0T_hi, x1T_ready, x4_ready = sem("xf_ready"), sem("xfT_hi"), sem("x0T_hi"), sem("x1T_ready"), sem("x4_ready")

        def flat(t):
            return t[:].rearrange("p c n -> p (c n)")
        splits = [(ins["wk1"], flat(wk[0]), flat(wk[1])), (ins["wq1"], flat(wq[0]), flat(wq[1])), (ins["wv1"], flat(wv[0]), flat(wv[1])),
                  (ins["w1"][:, 0, :], w1[0][:, 0, :], w1[1][:, 0, :]), (ins["w1"][:, 1, :], w1[0][:, 1, :], w1[1][:, 1, :])]
        NS, NS_FIRST = len(splits), 3
        params = [(bq[:], ins["bq1"]), (bk[:], ins["bk1"]), (b1[:], ins["b1"]),
                  (bv[:], ins["bv1"].to_broadcast([P, D])), (bo[:], ins["bo1"].to_broadcast([P, D])),
                  (flat(b2), ins["b2"].to_broadcast([P, 3 * D])), (flat(gw), ins["gw"].to_broadcast([P, 2 * D])),
                  (gates[:], ins["gates"].to_broadcast([P, 4])), (again[:], ins["again"])]

        with nc.Block() as block:

            @block.sync
            def _(sp):
                def load(b):
                    if not first(b):
                        sp.wait_ge(xn_ready, b)
                    sp.dma_start(xin[:], x2[bass.ds(b, 1)][0]).then_inc(x_in, 16)
                    if not first(b):
                        sp.wait_ge(ctx_ready, b)
                    sp.dma_start(ctxin[:], ins["ctx"][bass.ds(b, 1)][0]).then_inc(ctx_in, 16)

                def load_residual(b):
                    if not first(b):
                        sp.wait_ge(x3_copied, b)
                        sp.wait_ge(xf_ready, b)
                    sp.dma_start(x3[:], x2[bass.ds(b, 1)][0]).then_inc(xres_in, 16)

                def store(b):
                    sp.wait_ge(x4_ready, b + 1)
                    sp.dma_start(out[bass.ds(b, 1)][0], x4[:]).then_inc(x4_stored, 16)

                load(0)
                for n, (src, _hi, _lo) in enumerate(splits):
                    if n >= 2:
                        sp.wait_ge(split_lo, n - 1)
                    sp.dma_start(stage[:, n % 2, 0:src.shape[1]], src).then_inc(raw_in[n % 2], 16)
                    if n == 1:
                        for dst, src in params:
                            sp.dma_start(dst, src).then_inc(params_in, 16)
                    if n == 2:
                        load_residual(0)
                        sp.dma_start(flat(wo), ins["wo1"]).then_inc(wo_in, 16)
                    if n == 3:
                        load(1)
                sp.dma_start(flat(w2), ins["w2"]).then_inc(w2_in, 16)
                load_residual(1)
                with sp.Fori(2, B) as b:
                    load(b)
                    store(b - 2)
                    load_residual(b)
                store(B - 2)
                store(B - 1)
                sp.wait_ge(x4_stored, 16 * B)

            @block.gpsimd
            def _(pool):
                nc.gpsimd.memset(ident[:], 0.0)
                nc.gpsimd.memset(neghalf[:], -0.5)
                nc.gpsimd.memset(v[:], 0.0)
                pool.drain()
                nc.gpsimd.affine_select(out=ident[:], in_=ident[:], compare_op=ALU.not_equal, fill=1.0, base=0,
                                        pattern=[[-1, P]], channel_multiplier=1).then_inc(consts, 1)

                def power(ready, done, src, dst, b):
                    pool.wait_ge(ready, b + 1)
                    nc.gpsimd.tensor_tensor(dst[:], src[:], neghalf[:], ALU.pow).then_inc(done, 1)

                def split_context(a):
                    if not first(a):
                        _, full, _, turn = attn.at("v1", a - 1)
                        pool.wait_ge(full, turn)
                    wait_apart(pool, pool_passed, ctx_in, 16 * (a + 1))
                    nc.gpsimd.tensor_copy(cT[0][:], ctxin[:])
                    pool.drain()
                    nc.gpsimd.tensor_sub(cT[1][:], ctxin[:], cT[0][:].bitcast(F32)).then_inc(ctx_ready, 1)

                def normalise(a, j):
                    wait_apart(pool, pool_passed, rinv_ready, H * a + j + 1)
                    for t in range(NT):
                        last = nc.gpsimd.tensor_scalar(probs[:, j % 4, t * S:(t + 1) * S], probs[:, j % 4, t * S:(t + 1) * S],
                                                       rinv[:, j, t:t + 1], 1.0, ALU.mult, ALU.mult)
                    last.then_inc(norm_done, 1)

                def copy_residual(b):
                    if not first(b):
                        pool.wait_ge(x4_ready, b)
                    wait_apart(pool, pool_passed, x3_ready, b + 1)
                    nc.gpsimd.tensor_copy(x3res[:], x3[:]).then_inc(x3_copied, 1)

                def other_tokens(b):
                    ffn.emptied(pool, "xfT", b)
                    ffn.emptied(pool, "x0T", b)
                    for part in range(2):
                        last = nc.gpsimd.tensor_sub(x1T[part][:], xfT[part][:].bitcast(F32), x0T[part][:].bitcast(F32))
                    last.then_inc(x1T_ready, 1)

                def body(a, b, nxt):
                    if b is not None:
                        power(varF_ready, rstdF_ready, varF, rstdF, b)
                    for j in range(H):
                        if a is not None:
                            normalise(a, j)
                        if b is not None and j == 1:
                            copy_residual(b)
                        if b is not None and j == 3:
                            other_tokens(b)
                        if nxt is not None and j == 5:
                            split_context(nxt)
                        if nxt is not None and j == 9:
                            power(varC_ready, rstdC_ready, varC, rstdC, nxt)

                split_context(0)
                power(varC_ready, rstdC_ready, varC, rstdC, 0)
                body(0, None, 1)
                body(1, 0, 2)
                with pool.Fori(2, B - 1) as a:
                    body(a, a - 1, a + 1)
                body(B - 1, B - 2, None)
                body(None, B - 1, None)

            @block.scalar
            def _(act):
                nc.scalar.preload_act_table(ACT.Exp)

                def split(n):
                    src, hi, _lo = splits[n]
                    act.wait_ge(raw_in[n % 2], 16 * (n // 2 + 1))
                    nc.scalar.copy(hi, stage[:, n % 2, 0:src.shape[1]]).then_inc(split_hi, 1)

                for n in range(NS_FIRST):
                    split(n)
                act.wait_ge(params_in, 16 * len(params))
                nc.scalar.activation(tg[:], gates[:], ACT.Tanh).then_inc(tanh_done, 1)
                act.wait_ge(bias_ready, 1)

                def high(banks, use, batch, dst, ready):
                    ps, full, _, turn = banks.at(use, batch)
                    act.wait_ge(full, turn)
                    nc.scalar.copy(flat(dst), ps[:]).then_inc(ready, 1)

                def project(use, a):
                    if use == "xT":
                        high(attn, "xT", a, xT[0], xT_hi)
                    elif use[0] in "kq":
                        ps, full, _, turn = attn.at(use, a)
                        act.wait_ge(full, turn)
                        for u in range(2):
                            c, src = 2 * int(use[1]) + u, ps[:, u * S:(u + 1) * S]
                            if use[0] == "k":
                                last = nc.scalar.activation(k[0][:, c, :], src, ACT.Identity, bias=bk[:, c:c + 1])
                            else:
                                nc.scalar.activation(qfull[:, c, :], src, ACT.Identity, bias=bq[:, c:c + 1], scale=HD ** -0.5)
                                last = nc.scalar.activation(qhi[:, c, :], src, ACT.Identity, bias=bq[:, c:c + 1], scale=HD ** -0.5)
                        last.then_inc(k_hi if use[0] == "k" else q_hi, 1)

                def hidden(b, j):
                    ps, full, free, turn = ffn.at(f"h{j}", b)
                    act.wait_ge(full, turn)
                    for u in range(2):
                        c = 2 * j + u
                        last = nc.scalar.activation(hid[:, c, :], ps[:, u * S:(u + 1) * S], ACT.Relu, bias=b1[:, c:c + 1])
                    last.then_inc(free, 1)

                def head_group(a, g):
                    ps, _, free, _ = heads.at(f"o{g}", a)
                    act.wait_ge(pv_done, H * a + 8 * g + 8)
                    nc.scalar.copy(oT[:, 2 * g:2 * g + 2, :].rearrange("p c n -> p (c n)"), ps[:]).then_inc(free, 1)

                def body(a, b, nxt):
                    if b is not None:
                        high(ffn, "xfT", b, xfT[0], xfT_hi)
                        high(ffn, "x0T", b, x0T[0], x0T_hi)
                    for s in range(STEPS):
                        if a is not None and s - 1 in own_at:
                            project(own_at[s - 1], a)
                        if nxt is not None and s - 1 in ahead_at:
                            project(ahead_at[s - 1], nxt)
                        if a is not None and s < H:
                            ps, _, free, _ = score.at(f"s{s}", a)
                            act.wait_ge(max_ready, H * a + s + 1)
                            for t in range(NT):
                                last = nc.scalar.activation(probs[:, s % 4, t * S:(t + 1) * S], ps[:, t * S:(t + 1) * S], ACT.Exp,
                                                            bias=negmax[:, s, t:t + 1], accum_out=rsum[:, s, t:t + 1])
                            last.then_inc(free, 1)
                        if b is not None and s < 12:
                            hidden(b, s)
                        if a is not None and s == 8 + LAG_V:
                            head_group(a, 0)
                        if first(a) and s in (4, 8):
                            split(NS_FIRST + (s - 4) // 4)
                    if a is not None:
                        head_group(a, 1)

                for use in attn.ahead:
                    project(use, 0)
                body(0, None, 1)
                act.wait_ge(split_lo, NS)
                body(1, 0, 2)
                with act.Fori(2, B - 1) as a:
                    body(a, a - 1, a + 1)
                body(B - 1, B - 2, None)
                body(None, B - 1, None)

            @block.vector
            def _(dve):
                for banks in (attn, score, heads, ffn):
                    banks.open(dve)
                V = nc.vector

                def variance(src, stat, mv, var, ready):
                    for t in range(NT):
                        V.bn_stats(stat[:, t], src[:, t])
                    dve.drain()
                    for t in range(NT):
                        V.bn_aggr(mv[:, t], stat[:, t])
                    dve.drain()
                    V.tensor_scalar(var[:], mv[:, :, 1], LN_EPS, None, ALU.add).then_inc(ready, 1)

                def pre_variance(a):
                    dve.wait_ge(x_in, 16 * (a + 1))
                    variance(xin, statC, mvC, varC, varC_ready)

                def pre_normalise(a):
                    dve.wait_ge(rstdC_ready, a + 1)
                    for t in range(NT):
                        last = V.tensor_scalar(xn[:, t], xin[:, t], mvC[:, t, 0:1], rstdC[:, t:t + 1], ALU.subtract, ALU.mult)
                    last.then_inc(xn_ready, 1)

                def low(banks, use, batch, dst, hi_ready):
                    ps, _, free, _ = banks.at(use, batch)
                    dve.wait_ge(hi_ready, batch + 1)
                    V.tensor_sub(flat(dst[1]), ps[:], flat(dst[0]).bitcast(F32)).then_inc(free, 1)

                def ffn_norm(b):
                    dve.drain()
                    variance(x3, statF, mvF, varF, varF_ready)
                    dve.wait_ge(rstdF_ready, b + 1)
                    for t in range(NT):
                        V.tensor_scalar(xf[:, t], x3[:, t], mvF[:, t, 0:1], rstdF[:, t:t + 1], ALU.subtract, ALU.mult)
                    dve.drain()
                    for t in range(NT):
                        for e in range(2):
                            V.tensor_tensor_reduce(out=(ytmp, x0)[t][:, e], in0=xf[:, t], in1=gw[:, e], scale=1.0, scalar=0.0,
                                                   op0=ALU.mult, op1=ALU.add, accum_out=gscore[:, t, e:e + 1])
                    dve.drain()
                    V.tensor_tensor(first_wins[:], gscore[:, :, 0], gscore[:, :, 1], ALU.is_ge)
                    dve.drain()
                    for t in range(NT):
                        last = V.tensor_scalar(x0[:, t], xf[:, t], first_wins[:, t:t + 1], None, ALU.mult)
                    last.then_inc(xf_ready, 1)

                def keys(a, j):
                    ps, _, free, _ = attn.at(f"k{j}", a)
                    dve.wait_ge(k_hi, 2 * a + j + 1)
                    for u in range(2):
                        c = 2 * j + u
                        last = V.scalar_tensor_tensor(out=k[1][:, c, :], in0=ps[:, u * S:(u + 1) * S], scalar=bk[:, c:c + 1],
                                                      in1=k[0][:, c, :].bitcast(F32), op0=ALU.add, op1=ALU.subtract)
                    last.then_inc(free, 1)

                def values(a, t):
                    ps, full, free, turn = attn.at(f"v{t}", a)
                    dve.wait_ge(full, turn)
                    V.tensor_tensor(v[:, t, :, 0:HD], ps[:, 0:D].rearrange("p (h d) -> p h d", d=HD),
                                    bv[:].rearrange("p (h d) -> p h d", d=HD), ALU.add).then_inc(free, 1)

                def queries(a, j):
                    _, _, free, _ = attn.at(f"q{j}", a)
                    dve.wait_ge(q_hi, 2 * a + j + 1)
                    V.scalar_tensor_tensor(out=q[:, 2 * j:2 * j + 2, :], in0=qhi[:, 2 * j:2 * j + 2, :].bitcast(F32), scalar=again[:],
                                           in1=qfull[:, 2 * j:2 * j + 2, :], op0=ALU.mult, op1=ALU.add).then_inc(free, 1)

                def attn_max(a, j):
                    ps, full, _, turn = score.at(f"s{j}", a)
                    dve.wait_ge(full, turn)
                    V.tensor_reduce(negmax[:, j], ps[:].rearrange("p (t k) -> p t k", t=NT), axis=AX.X, op=ALU.max,
                                    negate=True).then_inc(max_ready, 1)

                def attn_sum(a, j):
                    score.emptied(dve, f"s{j}", a)
                    V.reciprocal(rinv[:, j], rsum[:, j]).then_inc(rinv_ready, 1)

                def attn_copy(a, j):
                    ps, full, free, turn = attn.at(f"T{j}", a)
                    dve.wait_ge(full, turn)
                    if j >= 2:
                        dve.wait_ge(pv_done, H * a + j - 1)
                    V.tensor_copy(probsT[:, j % 2, :], ps[:]).then_inc(free, 1)

                def attn_final(a):
                    ps, full, free, turn = attn.at("out", a)
                    dve.wait_ge(full, turn)
                    V.tensor_tensor(ytmp[:], ps[:].rearrange("p (t n) -> p t n", t=NT), bo[:].unsqueeze(1).to_broadcast([P, NT, D]),
                                    ALU.add).then_inc(free, 1)
                    dve.drain()
                    dve.wait_ge(xres_in, 16 * (a + 1))
                    V.scalar_tensor_tensor(out=x3[:], in0=ytmp[:], scalar=tg[:, 2:3], in1=x3[:], op0=ALU.mult,
                                           op1=ALU.add).then_inc(x3_ready, 1)

                def ffn_sum(b, t):
                    ps, full, free, turn = ffn.at(f"y{t}", b)
                    dve.wait_ge(full, turn)
                    V.tensor_tensor(x4[:, t], ps[:, 0:D], b2sum[:], ALU.add).then_inc(free, 1)

                def ffn_final(b):
                    ffn_sum(b, 1)
                    dve.drain()
                    dve.wait_ge(x3_copied, b + 1)
                    V.scalar_tensor_tensor(out=x4[:], in0=x4[:], scalar=tg[:, 3:4], in1=x3res[:], op0=ALU.mult,
                                           op1=ALU.add).then_inc(x4_ready, 1)

                def project(use, a):
                    if use == "xT":
                        low(attn, "xT", a, xT, xT_hi)
                    elif use[0] == "k":
                        keys(a, int(use[1]))
                    elif use[0] == "v":
                        values(a, int(use[1]))
                    else:
                        queries(a, int(use[1]))

                def body(a, b, c, nxt):
                    if b is not None:
                        ffn_norm(b)
                    if c is not None:
                        ffn_final(c)
                    if b is not None:
                        low(ffn, "xfT", b, xfT, xfT_hi)
                        low(ffn, "x0T", b, x0T, x0T_hi)
                    for s in range(STEPS):
                        if a is not None:
                            if s < H:
                                attn_max(a, s)
                            if 1 <= s < H + 1:
                                attn_sum(a, s - 1)
                            if LAG_T <= s < H + LAG_T:
                                attn_copy(a, s - LAG_T)
                            if s in own_at:
                                project(own_at[s], a)
                        if nxt is not None:
                            if s == 7:
                                pre_variance(nxt)
                            if s == 11:
                                pre_normalise(nxt)
                            if s in ahead_at:
                                project(ahead_at[s], nxt)
                        if first(a) and s in (4, 8):
                            split(NS_FIRST + (s - 4) // 4)
                    if b is not None:
                        if not first(b):
                            dve.wait_ge(x4_stored, 16 * b)
                        ffn_sum(b, 0)
                    if a is not None:
                        attn_final(a)

                def split(n):
                    src, hi, lo = splits[n]
                    dve.wait_ge(split_hi, n + 1)
                    V.tensor_sub(lo, stage[:, n % 2, 0:src.shape[1]], hi.bitcast(F32)).then_inc(split_lo, 1)

                pre_variance(0)
                split(0)
                pre_normalise(0)
                for n in range(1, NS_FIRST):
                    split(n)
                dve.wait_ge(params_in, 16 * len(params))
                V.tensor_scalar(bq[:], bq[:], HD ** -0.5, None, ALU.mult).then_inc(bias_ready, 1)
                V.tensor_tensor(b2sum[:], b2[:, 1], b2[:, 2], ALU.add)
                dve.drain()
                V.tensor_tensor(b2sum[:], b2sum[:], b2[:, 0], ALU.add)
                dve.wait_ge(tanh_done, 1)
                dve.wait_ge(consts, 1)
                for use in attn.ahead:
                    project(use, 0)
                body(0, None, None, 1)
                body(1, 0, None, 2)
                body(2, 1, 0, 3)
                with dve.Fori(3, B - 1) as a:
                    body(a, a - 1, a - 2, a + 1)
                body(B - 1, B - 2, B - 3, None)
                body(None, B - 1, B - 2, None)
                ffn_final(B - 1)

            @block.tensor
            def _(pe):
                T = nc.tensor

                def transpose4(banks, use, batch, src):
                    ps, full, free, turn = banks.at(use, batch)
                    pe.wait_ge(free, turn)
                    for c in range(ND):
                        for t in range(NT):
                            last = T.transpose(ps[:, c * S + t * P:c * S + (t + 1) * P], src[:, t, c * P:(c + 1) * P], ident[:])
                    last.then_inc(full, 1)

                def features(banks, use, batch, w, x, chunk):
                    ps, full, free, turn = banks.at(use, batch)
                    pe.wait_ge(free, turn)
                    for u in range(2):
                        m = slice((chunk + u) * P, (chunk + u + 1) * P)
                        last = product3(nc, ps[:, u * S:(u + 1) * S],
                                        [(w[0][:, c, m], w[1][:, c, m], x[0][:, c, :], x[1][:, c, :]) for c in range(ND)])
                    last.then_inc(full, 1)

                def values(a, t):
                    ps, full, free, turn = attn.at(f"v{t}", a)
                    pe.wait_ge(free, turn)
                    m = slice(t * P, (t + 1) * P)
                    product3(nc, ps[:, 0:D], [(cT[0][:, c, m], cT[1][:, c, m], wv[0][:, c, :], wv[1][:, c, :])
                                              for c in range(ND)]).then_inc(full, 1)

                def head_scores(a, j):
                    c, r = j // HPC1, slice((j % HPC1) * SLOT, (j % HPC1 + 1) * SLOT)
                    ps, full, free, turn = score.at(f"s{j}", a)
                    pe.wait_ge(free, turn)
                    for t in range(NT):
                        for part in range(2):
                            last = T.matmul(ps[:, t * S:(t + 1) * S], q[r, c, t * P:(t + 1) * P], k[part][r, c, :], start=part == 0, stop=part == 1)
                    last.then_inc(full, 1)

                def head_transpose(a, j):
                    ps, full, free, turn = attn.at(f"T{j}", a)
                    pe.wait_ge(free, turn)
                    pe.wait_ge(norm_done, H * a + j + 1)
                    for kt in range(NT):
                        for t in range(NT):
                            last = T.transpose(ps[:, kt * S + t * P:kt * S + (t + 1) * P], probs[:, j % 4, t * S + kt * P:t * S + (kt + 1) * P], ident[:])
                    last.then_inc(full, 1)

                def head_values(a, j):
                    g, u, r = j // 8, (j // HPC1) % 2, slice((j % HPC1) * SLOT, (j % HPC1 + 1) * SLOT)
                    ps, _, free, turn = heads.at(f"o{g}", a)
                    if j % 8 == 0:
                        pe.wait_ge(free, turn)
                    attn.emptied(pe, f"T{j}", a)
                    for kt in range(NT):
                        last = T.matmul(ps[r, u * S:(u + 1) * S], v[:, kt, j, :], probsT[:, j % 2, kt * S:(kt + 1) * S], start=kt == 0, stop=kt == NT - 1)
                    last.then_inc(pv_done, 1)

                def attn_out(a):
                    ps, full, free, turn = attn.at("out", a)
                    heads.emptied(pe, "o0", a)
                    heads.emptied(pe, "o1", a)
                    if first(a):
                        pe.wait_ge(wo_in, 16)
                    pe.wait_ge(free, turn)
                    for t in range(NT):
                        for c in range(NC1):
                            last = T.matmul(ps[:, t * D:(t + 1) * D], oT[:, c, t * P:(t + 1) * P], wo[:, c, :], start=c == 0, stop=c == NC1 - 1)
                    last.then_inc(full, 1)

                def ffn_down(b, t, piece):
                    ps, full, free, turn = ffn.at(f"y{t}", b)
                    if piece == 0:
                        pe.wait_ge(free, turn)
                        ffn.emptied(pe, "h10", b)
                        ffn.emptied(pe, "h11", b)
                    n = 3 * NHC // 4
                    for c in range(piece * n, (piece + 1) * n):
                        last = T.matmul(ps[:, 0:D], hid[:, c, t * P:(t + 1) * P], w2[:, c, :], start=c == 0, stop=c == 3 * NHC - 1)
                    if piece == 3:
                        last.then_inc(full, 1)

                def project(use, a):
                    j = int(use[1]) if use != "xT" else None
                    if use == "xT":
                        pe.wait_ge(xn_ready, a + 1)
                        transpose4(attn, "xT", a, xn)
                    elif use[0] == "k":
                        if j == 0:
                            pe.wait_ge(ctx_ready, a + 1)
                        features(attn, use, a, wk, cT, 2 * j)
                    elif use[0] == "v":
                        values(a, j)
                    else:
                        if j == 0:
                            attn.emptied(pe, "xT", a)
                        features(attn, use, a, wq, xT, 2 * j)

                def body(a, b, nxt):
                    if b is not None:
                        pe.wait_ge(xf_ready, b + 1)
                        transpose4(ffn, "xfT", b, xf)
                        transpose4(ffn, "x0T", b, x0)
                    for s in range(STEPS):
                        if a is not None and s < H:
                            if s % 8 == 0:
                                attn.emptied(pe, f"k{s // 8}", a)
                                attn.emptied(pe, f"q{s // 8}", a)
                            head_scores(a, s)
                        if b is not None:
                            if s == 0:
                                ffn.emptied(pe, "xfT", b)
                                ffn.emptied(pe, "x0T", b)
                            if s == 8:
                                pe.wait_ge(x1T_ready, b + 1)
                            if s < 12:
                                features(ffn, f"h{s}", b, w1, (xfT, x0T, x1T)[s // 4], 2 * s)
                            if STEPS - 4 <= s:
                                ffn_down(b, 0, s - STEPS + 4)
                        if a is not None:
                            if LAG_T <= s < H + LAG_T:
                                head_transpose(a, s - LAG_T)
                            if s >= LAG_V:
                                if s == LAG_V:
                                    attn.emptied(pe, "v0", a)
                                    attn.emptied(pe, "v1", a)
                                head_values(a, s - LAG_V)
                            if s in own_at:
                                project(own_at[s], a)
                        if nxt is not None and s in ahead_at:
                            project(ahead_at[s], nxt)
                    if a is not None:
                        attn_out(a)
                    if b is not None:
                        for piece in range(4):
                            ffn_down(b, 1, piece)

                pe.wait_ge(consts, 1)
                for use in attn.ahead:
                    if use in ("k0", "q0"):
                        pe.wait_ge(split_lo, 1 + ("k0", "q0").index(use))
                    project(use, 0)
                pe.wait_ge(split_lo, NS_FIRST)
                body(0, None, 1)
                pe.wait_ge(split_lo, NS)
                pe.wait_ge(w2_in, 16)
                body(1, 0, 2)
                with pe.Fori(2, B - 1) as a:
                    body(a, a - 1, a + 1)
                body(B - 1, B - 2, None)
                body(None, B - 1, None)



def chunked(w):
    c = w.shape[0] // P
    return w.reshape(c, P, w.shape[1]).transpose(1, 0, 2).reshape(P, c * w.shape[1])


def layouts(i):
    import numpy as np
    gates = np.stack([i["g_xattn"][0], i["g_ffn"][0], i["g_xattn"][1], i["g_ffn"][1]])[None]
    tiles = lambda x: x.reshape(B, NT, P, D).transpose(0, 2, 1, 3)
    w1 = np.concatenate([i["L1_ffn_sw1"][None], i["L1_ffn_w1"]])
    w2 = np.concatenate([i["L1_ffn_sw2"][None], i["L1_ffn_w2"]])
    b1 = np.concatenate([i["L1_ffn_sb1"][None], i["L1_ffn_b1"]])
    b2 = np.concatenate([i["L1_ffn_sb2"][None], i["L1_ffn_b2"]])
    again = np.zeros((P, 1), np.float32)
    again.reshape(HPC1, 2, HD)[:, 1] = -1.0

    def twice(w):
        w = w.reshape(*w.shape[:-1], H, 1, HD)
        return np.concatenate([w, w], axis=-2).reshape(*w.shape[:-3], NC1 * P)
    spread = np.zeros((H, SLOT, D), np.float32)
    spread[:, 0:HD] = i["L1_xattn_Wo"].T.reshape(H, HD, D)
    return {
        "wq1": chunked(twice(i["L1_xattn_Wq"].T)), "wk1": chunked(twice(i["L1_xattn_Wk"].T)), "wv1": chunked(i["L1_xattn_Wv"].T),
        "bq1": twice(i["L1_xattn_bq"]).reshape(NC1, P).T, "bk1": twice(i["L1_xattn_bk"]).reshape(NC1, P).T,
        "wo1": chunked(spread.reshape(H * SLOT, D)), "bv1": i["L1_xattn_bv"][None], "bo1": i["L1_xattn_bo"][None],
        "w1": w1.transpose(1, 0, 2).reshape(ND, P, 3 * HID).transpose(1, 0, 2), "b1": b1.reshape(3 * NHC, P).T,
        "w2": chunked(w2.reshape(3 * HID, D)), "b2": b2.reshape(1, 3 * D), "gw": i["L1_ffn_gate_w"].reshape(1, 2 * D),
        "again": again,
        "x": tiles(i["x"]),
        "ctx": i["ctx_1024"].transpose(0, 2, 1).reshape(B, ND, P, S).transpose(0, 2, 1, 3),
        "mask": i["mask_BxS2_bf1"],
        "gates": gates,
        "wq": chunked(i["L0_xattn_Wq"].T), "wk": chunked(i["L0_xattn_Wk"].T), "wv": chunked(i["L0_xattn_Wv"].T),
        "wo": chunked(i["L0_xattn_Wo"].T), "bo": i["L0_xattn_bo"][None],
        "fq": chunked(i["L0_ffn_Wq"]), "fdown": chunked(i["L0_ffn_Wdown"]), "fup": i["L0_ffn_Wup"], "fo": chunked(i["L0_ffn_Wo"]),
        "wg": chunked(i["L0_ffn_Wg"]),
        "we": i["L0_ffn_We"].transpose(1, 0, 2).reshape(ND, P, E * D).transpose(1, 0, 2),
        "bq": i["L0_ffn_bq"][None], "bup": i["L0_ffn_bup"][None], "bfo": i["L0_ffn_bo"][None], "bg": i["L0_ffn_bg"][None],
        "bdown": i["L0_ffn_bdown"][:, None],
        "gamma1": i["L0_ffn_gamma1"].reshape(ND, P).T, "gamma2": i["L0_ffn_gamma2"].reshape(ND, P).T,
    }


def kernel(**inputs):
    import numpy as np
    import concourse.bacc as bacc
    from concourse.bass_utils import run_bass_kernel_spmd

    nc = bacc.Bacc("TRN2", target_bir_lowering=False, num_devices=1)
    arrays = {f"in_{k}": np.ascontiguousarray(v) for k, v in layouts({k: np.asarray(v) for k, v in inputs.items()}).items()}
    ins = {k[3:]: nc.dram_tensor(k, v.shape, mybir.dt.from_np(v.dtype), kind="ExternalInput").ap() for k, v in arrays.items()}
    out = nc.dram_tensor("out", (B, P, NT, D), F32, kind="ExternalOutput").ap()
    x2 = nc.dram_tensor("x2", (B, P, NT, D), F32, kind="Internal").ap()
    layer0(nc, ins, x2)
    layer1(nc, ins, x2, out)
    got = run_bass_kernel_spmd(nc, [arrays], core_ids=[0]).results[0]["out"]
    return got.reshape(B, P, NT, D).transpose(0, 2, 1, 3).reshape(B, S, D)
```
